# Optimizing a Trainium2 kernel written in Bass

```python
import numpy as np
import jax
import jax.numpy as jnp

def _softmax(x, axis=-1):
    return jax.nn.softmax(x, axis=axis)

def _gelu(x):
    return jax.nn.gelu(x, approximate=True)

def _silu(x):
    return jax.nn.silu(x)

def _sigmoid(x):
    return jax.nn.sigmoid(x)

def _layernorm(x, axis=-1, eps=1e-05):
    m = jnp.mean(x, axis=axis, keepdims=True)
    v = jnp.var(x, axis=axis, keepdims=True)
    return (x - m) / jnp.sqrt(v + eps)

def _scatter_add(tgt, idx, src, axis=0):
    return tgt.at[idx].add(src)

def _segment_sum(src, seg, n):
    return jax.ops.segment_sum(src, seg, n)
kernel_name = 'mk_gps_d1_gnn_r8_f39080'

def setup_inputs(seed: int=0):
    np.random.seed(seed)
    _w = jnp.asarray

    def _rec_inputs():
        import jax
        import jax.numpy as jnp
        _gk = jax.random.key(seed)
        x = -0.0003713 + 1 * jax.random.normal(jax.random.fold_in(_gk, 1), (6250, 256), jnp.float32)
        src = jax.random.randint(jax.random.fold_in(_gk, 2), (200000,), 0, 6250, jnp.int32)
        dst = jnp.minimum((6250 * jax.random.uniform(jax.random.fold_in(_gk, 3), (200000,)) ** 2.0).astype(jnp.int32), 49999)
        _o = jnp.argsort(dst, stable=True)
        src = src[_o]
        dst = dst[_o]
        edge_weight = jax.random.uniform(jax.random.fold_in(_gk, 12), (200000,), jnp.float32, 0.0, 0.999999)
        return (x, src, dst, edge_weight)
    x, src, dst, edge_weight = _rec_inputs()

    def _L0_gnn_setup():
        import jax, jax.numpy as jnp
        import numpy as np
        N_NODES = 6250
        N_EDGES = 100000
        D = 256
        key = jax.random.key(seed)
        k1, k2, k3, k4, k5, k6 = jax.random.split(key, 6)
        x = jax.random.normal(k1, (N_NODES, D), dtype=jnp.float32)
        edge_row = jax.random.randint(k2, (N_EDGES,), 0, N_NODES, dtype=jnp.int32)
        edge_col = jax.random.randint(k3, (N_EDGES,), 0, N_NODES, dtype=jnp.int32)
        edge_val = jax.random.uniform(k4, (N_EDGES,), dtype=jnp.float32)
        stdv = 1.0 / np.sqrt(D)
        weight = jax.random.uniform(k5, (D, D), minval=-stdv, maxval=stdv, dtype=jnp.float32)
        bias = jax.random.uniform(k6, (D,), minval=-stdv, maxval=stdv, dtype=jnp.float32)
        return {'x': x, 'edge_row': edge_row, 'edge_col': edge_col, 'edge_val': edge_val, 'weight': weight, 'bias': bias}
    _L0_gnn_all = _L0_gnn_setup()
    _L0_gnn_in = {k: v for k, v in _L0_gnn_all.items() if k in ('weight', 'bias')}
    del _L0_gnn_all

    def _L0_mix_setup():
        import jax, jax.numpy as jnp
        import numpy as np
        D_MODEL = 256
        NHEAD = 8
        D_HEAD = D_MODEL // NHEAD
        DIM_FF = 1024
        B, L = (4, 2048)
        LN_EPS = 1e-05

        def _layernorm(x, g, b):
            mu = jnp.mean(x, axis=-1, keepdims=True)
            var = jnp.mean((x - mu) ** 2, axis=-1, keepdims=True)
            return (x - mu) * jax.lax.rsqrt(var + LN_EPS) * g + b

        def _phi(x):
            return jnp.where(x > 0, x + 1.0, jnp.exp(x))
        key = jax.random.key(seed)
        ks = jax.random.split(key, 16)
        s_in = 1.0 / np.sqrt(D_MODEL)
        s_ff = 1.0 / np.sqrt(DIM_FF)
        inp = {'x': jax.random.normal(ks[0], (B, L, D_MODEL), dtype=jnp.float32), 'Wq': jax.random.normal(ks[1], (D_MODEL, D_MODEL), dtype=jnp.float32) * s_in, 'bq': jnp.zeros((D_MODEL,), jnp.float32), 'Wk': jax.random.normal(ks[2], (D_MODEL, D_MODEL), dtype=jnp.float32) * s_in, 'bk': jnp.zeros((D_MODEL,), jnp.float32), 'Wv': jax.random.normal(ks[3], (D_MODEL, D_MODEL), dtype=jnp.float32) * s_in, 'bv': jnp.zeros((D_MODEL,), jnp.float32), 'Wo': jax.random.normal(ks[4], (D_MODEL, D_MODEL), dtype=jnp.float32) * s_in, 'bo': jnp.zeros((D_MODEL,), jnp.float32), 'W1': jax.random.normal(ks[5], (D_MODEL, DIM_FF), dtype=jnp.float32) * s_in, 'b1': jnp.zeros((DIM_FF,), jnp.float32), 'W2': jax.random.normal(ks[6], (DIM_FF, D_MODEL), dtype=jnp.float32) * s_ff, 'b2': jnp.zeros((D_MODEL,), jnp.float32), 'ln1_g': jnp.ones((D_MODEL,), jnp.float32), 'ln1_b': jnp.zeros((D_MODEL,), jnp.float32), 'ln2_g': jnp.ones((D_MODEL,), jnp.float32), 'ln2_b': jnp.zeros((D_MODEL,), jnp.float32)}
        return inp
    _L0_mix_all = _L0_mix_setup()
    _L0_mix_in = {k: v for k, v in _L0_mix_all.items() if k in ('Wq', 'bq', 'Wk', 'bk', 'Wv', 'bv', 'Wo', 'bo', 'W1', 'b1', 'W2', 'b2', 'ln1_g', 'ln1_b', 'ln2_g', 'ln2_b')}
    del _L0_mix_all

    def _L0_ffn_setup():
        import jax, jax.numpy as jnp
        import numpy as np
        E = 8
        K = 2
        D = 256
        H = 512
        DOUT = 256
        EPS = 1e-05
        key = jax.random.key(seed)
        ks = jax.random.split(key, 9)
        s = 0.02
        return {'x': jax.random.normal(ks[0], (4, 1024, D), jnp.float32), 'gamma': 1.0 + 0.05 * jax.random.normal(ks[1], (D,), jnp.float32), 'beta': 0.05 * jax.random.normal(ks[2], (D,), jnp.float32), 'Wr': 0.01 * jax.random.normal(ks[3], (D, E), jnp.float32), 'br': jnp.zeros((E,), jnp.float32), 'W1': s * jax.random.normal(ks[4], (E, D, H), jnp.float32), 'b1': s * jax.random.normal(ks[5], (E, H), jnp.float32), 'W2': s * jax.random.normal(ks[6], (E, H, DOUT), jnp.float32), 'b2': s * jax.random.normal(ks[7], (E, DOUT), jnp.float32)}
    _L0_ffn_all = _L0_ffn_setup()
    _L0_ffn_in = {k: v for k, v in _L0_ffn_all.items() if k in ('gamma', 'beta', 'Wr', 'br', 'W1', 'b1', 'W2', 'b2')}
    del _L0_ffn_all
    return {'x': x, 'src': src, 'dst': dst, 'edge_weight': edge_weight, 'L0_gnn_weight': _L0_gnn_in['weight'], 'L0_gnn_bias': _L0_gnn_in['bias'], 'L0_mix_Wq': _L0_mix_in['Wq'], 'L0_mix_bq': _L0_mix_in['bq'], 'L0_mix_Wk': _L0_mix_in['Wk'], 'L0_mix_bk': _L0_mix_in['bk'], 'L0_mix_Wv': _L0_mix_in['Wv'], 'L0_mix_bv': _L0_mix_in['bv'], 'L0_mix_Wo': _L0_mix_in['Wo'], 'L0_mix_bo': _L0_mix_in['bo'], 'L0_mix_W1': _L0_mix_in['W1'], 'L0_mix_b1': _L0_mix_in['b1'], 'L0_mix_W2': _L0_mix_in['W2'], 'L0_mix_b2': _L0_mix_in['b2'], 'L0_mix_ln1_g': _L0_mix_in['ln1_g'], 'L0_mix_ln1_b': _L0_mix_in['ln1_b'], 'L0_mix_ln2_g': _L0_mix_in['ln2_g'], 'L0_mix_ln2_b': _L0_mix_in['ln2_b'], 'L0_ffn_gamma': _L0_ffn_in['gamma'], 'L0_ffn_beta': _L0_ffn_in['beta'], 'L0_ffn_Wr': _L0_ffn_in['Wr'], 'L0_ffn_br': _L0_ffn_in['br'], 'L0_ffn_W1': _L0_ffn_in['W1'], 'L0_ffn_b1': _L0_ffn_in['b1'], 'L0_ffn_W2': _L0_ffn_in['W2'], 'L0_ffn_b2': _L0_ffn_in['b2']}

def reference(x, src, dst, edge_weight, L0_gnn_weight, L0_gnn_bias, L0_mix_Wq, L0_mix_bq, L0_mix_Wk, L0_mix_bk, L0_mix_Wv, L0_mix_bv, L0_mix_Wo, L0_mix_bo, L0_mix_W1, L0_mix_b1, L0_mix_W2, L0_mix_b2, L0_mix_ln1_g, L0_mix_ln1_b, L0_mix_ln2_g, L0_mix_ln2_b, L0_ffn_gamma, L0_ffn_beta, L0_ffn_Wr, L0_ffn_br, L0_ffn_W1, L0_ffn_b1, L0_ffn_W2, L0_ffn_b2):
    import jax
    import jax.numpy as jnp

    def _L0_gnn_ref(x, edge_row, edge_col, edge_val, weight, bias):
        import jax, jax.numpy as jnp
        import numpy as np
        N_NODES = 6250
        N_EDGES = 100000
        D = 256
        support = x @ weight
        msgs = edge_val[:, None] * support[edge_col]
        agg = jax.ops.segment_sum(msgs, edge_row, num_segments=N_NODES)
        return jax.nn.relu(agg + bias + x)

    def _L0_mix_ref(x, Wq, bq, Wk, bk, Wv, bv, Wo, bo, W1, b1, W2, b2, ln1_g, ln1_b, ln2_g, ln2_b):
        import jax, jax.numpy as jnp
        import numpy as np
        D_MODEL = 256
        NHEAD = 8
        D_HEAD = D_MODEL // NHEAD
        DIM_FF = 1024
        B, L = (4, 2048)
        LN_EPS = 1e-05

        def _layernorm(x, g, b):
            mu = jnp.mean(x, axis=-1, keepdims=True)
            var = jnp.mean((x - mu) ** 2, axis=-1, keepdims=True)
            return (x - mu) * jax.lax.rsqrt(var + LN_EPS) * g + b

        def _phi(x):
            return jnp.where(x > 0, x + 1.0, jnp.exp(x))
        Bq, Lq, _ = x.shape
        q = (x @ Wq + bq).reshape(Bq, Lq, NHEAD, D_HEAD)
        k = (x @ Wk + bk).reshape(Bq, Lq, NHEAD, D_HEAD)
        v = (x @ Wv + bv).reshape(Bq, Lq, NHEAD, D_HEAD)
        q_phi = _phi(q)
        k_phi = _phi(k)
        kv = jnp.einsum('blhd,blhe->bhde', k_phi, v)
        k_sum = k_phi.sum(axis=1)
        z = 1.0 / (jnp.einsum('blhd,bhd->blh', q_phi, k_sum) + 1e-06)
        out = jnp.einsum('blhd,bhde,blh->blhe', q_phi, kv, z)
        out = out.reshape(Bq, Lq, D_MODEL) @ Wo + bo
        x = _layernorm(x + out, ln1_g, ln1_b)
        ff = jax.nn.relu(x @ W1 + b1) @ W2 + b2
        x = _layernorm(x + ff, ln2_g, ln2_b)
        return x

    def _L0_ffn_ref(x, gamma, beta, Wr, br, W1, b1, W2, b2):
        import jax, jax.numpy as jnp
        import numpy as np
        E = 8
        K = 2
        D = 256
        H = 512
        DOUT = 256
        EPS = 1e-05
        mu = jnp.mean(x, axis=-1, keepdims=True)
        var = jnp.mean(jnp.square(x - mu), axis=-1, keepdims=True)
        xn = (x - mu) * jax.lax.rsqrt(var + EPS) * gamma + beta
        logits = jnp.einsum('bsd,de->bse', xn, Wr) + br
        top_vals, top_idx = jax.lax.top_k(logits, K)
        w = jax.nn.softmax(top_vals, axis=-1)
        w_full = jnp.einsum('bsk,bske->bse', w, jax.nn.one_hot(top_idx, E, dtype=w.dtype))
        y = jnp.zeros(x.shape[:-1] + (DOUT,), x.dtype)
        for e in range(E):
            h = jax.nn.gelu(jnp.einsum('bsd,dh->bsh', xn, W1[e]) + b1[e], approximate=False)
            y_e = jnp.einsum('bsh,hd->bsd', h, W2[e]) + b2[e]
            y = y + y_e * w_full[..., e, None]
        return y
    xn = _layernorm(x, axis=-1)
    x = x + _L0_gnn_ref(xn, src, dst, edge_weight, L0_gnn_weight, L0_gnn_bias) + _L0_mix_ref(xn[None], L0_mix_Wq, L0_mix_bq, L0_mix_Wk, L0_mix_bk, L0_mix_Wv, L0_mix_bv, L0_mix_Wo, L0_mix_bo, L0_mix_W1, L0_mix_b1, L0_mix_W2, L0_mix_b2, L0_mix_ln1_g, L0_mix_ln1_b, L0_mix_ln2_g, L0_mix_ln2_b)[0]
    x = x + _L0_ffn_ref(_layernorm(x, axis=-1)[None], L0_ffn_gamma, L0_ffn_beta, L0_ffn_Wr, L0_ffn_br, L0_ffn_W1, L0_ffn_b1, L0_ffn_W2, L0_ffn_b2)[0]
    return x

_drawn_inputs = setup_inputs


def setup_inputs(seed=0):
    import zlib

    import numpy as np

    out = dict(_drawn_inputs(seed))
    spreads = {'L0_mix_bq': (0.0, 2.0),
     'L0_mix_bk': (0.0, 2.0),
     'L0_mix_bv': (0.0, 0.1),
     'L0_mix_bo': (0.0, 0.1),
     'L0_mix_b1': (0.0, 0.376),
     'L0_mix_b2': (0.0, 0.274),
     'L0_mix_ln1_g': (1.0, 0.2),
     'L0_mix_ln1_b': (0.0, 0.1),
     'L0_mix_ln2_g': (1.0, 0.2),
     'L0_mix_ln2_b': (0.0, 0.1),
     'L0_ffn_br': (0.0, 0.409)}
    factors = {'L0_gnn_bias': 6.044,
     'L0_mix_Wq': 8.0,
     'L0_mix_Wk': 8.0,
     'L0_mix_Wv': 8.0,
     'L0_ffn_gamma': 8.0,
     'L0_ffn_beta': 8.0,
     'L0_ffn_Wr': 4.198,
     'L0_ffn_W1': 2.955,
     'L0_ffn_b1': 22.764,
     'L0_ffn_W2': 2.87,
     'L0_ffn_b2': 21.729}
    for name, (base, spread) in spreads.items():
        noise = np.random.default_rng([zlib.crc32(name.encode()), seed]).standard_normal(out[name].shape)
        drawn = base * np.exp(spread * noise) if base else spread * noise
        out[name] = jnp.asarray(drawn.astype(out[name].dtype))
    for name, factor in factors.items():
        out[name] = (out[name] * factor).astype(out[name].dtype)
    return out
```

```python
import concourse.bass as bass
from concourse import mybir
from contextlib import ExitStack

F32 = mybir.dt.float32
I32 = mybir.dt.int32
U32 = mybir.dt.uint32
ALU = mybir.AluOpType
ACT = mybir.ActivationFunctionType
ds = bass.ds

P = 128
N = 6250
NE = 200000
D = 256
KC = D // P
NH = 8
DH = D // NH
FF = 1024
FC = FF // P
E = 8
H = 512
HC = H // P
EPS = 1e-5

NB = -(-N // P)
LASTN = N - (NB - 1) * P
GB = 4
FULL = NB // GB
assert NB == FULL * GB + 1

EC = -(-NE // P)
TAILE = NE - (P - 1) * EC
SH = 8
SCAT_STEPS = -(-EC // (2 * SH))
ECP = SCAT_STEPS * 2 * SH

GT = 4
GS = GT * P
NG = (P * EC + GS * NB) // GS
HALF_G = 2
GATHER_STEPS = -(-NG // (2 * HALF_G))
NG = GATHER_STEPS * 2 * HALF_G
NT = NG * GT
HT = HALF_G * GT
CARRY = 2 * HALF_G
ZERO_DMAS = 16
STATB = 7
assert NB % STATB == 0


def wait(eng, sem, value, passed=None):
    eng.wait_ge(sem, value)


def wait_apart(eng, sem, value, passed):
    eng.wait_ge(sem, value)
    eng.sem_inc(passed, 1)


class Chain:

    def __init__(self, eng, sem, passed=None):
        self.eng, self.sem, self.base, self.off, self.k, self.passed = eng, sem, 0, 0, 0, passed

    def __call__(self, ins, apart=False):
        self.k += 1
        ins.then_inc(self.sem, 1)
        (wait_apart if apart else wait)(self.eng, self.sem, self.off + (self.base + self.k), self.passed)

    def turn(self, i, per):
        self.base, self.off, self.k = self.base + self.k, i * per, 0

    def end_turn(self, per):
        assert self.k == per, (self.k, per)

    def after(self, turns, per):
        self.base, self.off, self.k = self.base + turns * per, 0, 0


def over_groups(eng, chain, per, body):
    if chain is not None:
        chain.turn(0, 0)
    with eng.Fori(0, FULL) as g:
        if chain is not None:
            chain.off, chain.k = g * per, 0
        body(g, GB)
        if chain is not None:
            chain.end_turn(per)
    if chain is not None:
        chain.after(FULL, per)
    body(FULL, 1)


def program(nc, x, src, dst, edge_weight, gnn_w, gnn_b, Wq, bq, Wk, bk, Wv, bv, Wo, bo,
            W1, b1, W2, b2, ln1_g, ln1_b, ln2_g, ln2_b, gamma, beta, Wr, br, eW1, eb1, eW2, eb2, out):
    support = nc.dram_tensor("support", (NB * P, D), F32).ap()
    slots = nc.dram_tensor("slots", (P * NT + (ECP - EC) * P, 4), F32).ap()
    agg = nc.dram_tensor("agg", ((NB + NG) * P, D), F32).ap()

    ctx = ExitStack()
    with ctx:
        def sem(name):
            return ctx.enter_context(nc.semaphore(name))

        def alloc(stack, name, shape, dt=F32):
            return stack.enter_context(nc.sbuf_tensor(name, shape, dt))

        R = alloc(ctx, "R", [P, NB, D])
        ident = alloc(ctx, "ident", [P, P])
        iota_row = alloc(ctx, "iota_row", [P, P])
        ones = alloc(ctx, "ones", [P, P])
        eps_col = alloc(ctx, "eps_col", [P, 1])
        mv = alloc(ctx, "mv", [P, NB, 2])
        rstd = alloc(ctx, "rstd", [P, NB])
        ps = [ctx.enter_context(nc.psum_tensor(f"ps{i}", [P, 512], F32)) for i in range(8)]

        early = ExitStack()
        rec = alloc(early, "rec", [P, ECP, 4])
        pos_i = alloc(early, "pos_i", [P, ECP], I32)
        cnt = alloc(early, "cnt", [P, NB])
        base = alloc(early, "base", [P, NB])
        prefix = alloc(early, "prefix", [P, NB])
        gcount = alloc(early, "gcount", [P, NB])
        gint = alloc(early, "gint", [P, NB], I32)
        gcol = alloc(early, "gcol", [P, 4])
        gcol_i = alloc(early, "gcol_i", [P, 1], I32)
        iota_g = alloc(early, "iota_g", [P, NG])
        keep = alloc(early, "keep", [P, NG])
        dest_f = alloc(early, "dest_f", [P, NG])
        dest_i = alloc(early, "dest_i", [P, NG], I32)
        tri = alloc(early, "tri", [P, P])
        blockones = alloc(early, "blockones", [P, P])
        zeros = alloc(early, "zeros", [P, NT * 4 // ZERO_DMAS])
        st_rec = [alloc(early, f"st_rec{h}", [P, SH, 4]) for h in range(2)]
        st_pos = [alloc(early, f"st_pos{h}", [P, SH], I32) for h in range(2)]
        st_tab = [alloc(early, f"st_tab{h}", [P, HT, 4]) for h in range(2)]
        big = alloc(early, "big", [P, 2, HT, D])
        rows = [big[:, h, :, :] for h in range(2)]
        uT = big[:, :, :, :].rearrange("p h t d -> p (h t d)").rearrange("p (f t) -> p f t", f=FC)
        mid = alloc(early, "mid", [P, 2, HT * P])
        hot = [mid[:, h, :].rearrange("p (t n) -> p t n", t=HT) for h in range(2)]
        xn = mid[:, 0, :].rearrange("p (t d) -> p t d", t=GB)
        xnT = mid[:, 1, :].rearrange("p (c t) -> p c t", c=KC)
        carry = alloc(early, "carry", [P, CARRY, D])

        wg_sb = alloc(early, "wg_sb", [P, KC, D])
        wkv_sb = alloc(early, "wkv_sb", [P, KC, 2 * D])
        wq_sb = alloc(early, "wq_sb", [P, KC, D])
        wo_sb = alloc(early, "wo_sb", [P, KC, D])
        w1_sb = alloc(early, "w1_sb", [P, KC, FF])
        w2_sb = alloc(early, "w2_sb", [P, FC, D])
        bkv_b = alloc(early, "bkv_b", [P, 2 * D])
        row_b = alloc(early, "row_b", [P, 6, D])
        bq_col = alloc(early, "bq_col", [P, KC])
        b1_col = alloc(early, "b1_col", [P, FC])
        kraw = alloc(early, "kraw", [P, 2, D])
        kneg = alloc(early, "kneg", [P, 2, D])
        kphi = alloc(early, "kphi", [P, 2, D])
        vaug = alloc(early, "vaug", [P, 2, KC, P + 4])
        sup_sb = alloc(early, "sup_sb", [P, GB, D])
        kvbd = alloc(early, "kvbd", [P, KC, P])
        ksum = alloc(early, "ksum", [P, KC])
        ksel = alloc(early, "ksel", [P, KC, P])
        stats = alloc(early, "stats", [P, STATB, 6])
        smv = alloc(early, "smv", [P, STATB, 2])
        gmv = alloc(early, "gmv", [P, GB, 2])
        grs = alloc(early, "grs", [P, GB])
        edge = ExitStack()
        hi = alloc(edge, "hi", [P, EC])
        ea = alloc(edge, "ea", [P, EC])
        eb = alloc(edge, "eb", [P, EC])
        ec = alloc(edge, "ec", [P, EC])
        gflags = ea[:, 0:3 * NG].rearrange("p (k g) -> p k g", k=3)
        edge.close()
        qneg = alloc(early, "qneg", [P, KC, GB * P])
        qphi = alloc(early, "qphi", [P, KC, GB * P])
        attnT = alloc(early, "attnT", [P, KC, GB * P])
        h1 = alloc(early, "h1", [P, GB, D])
        tmp = alloc(early, "tmp", [P, GB, D])
        hT = alloc(early, "hT", [P, KC, GB * P])
        early.close()

        late = ExitStack()
        zT = alloc(late, "zT", [P, NB, KC, P])
        ew1_sb = alloc(late, "ew1_sb", [P, E, KC, H])
        ew2_sb = alloc(late, "ew2_sb", [P, E, HC, D])
        eb1_col = alloc(late, "eb1_col", [P, E * HC])
        eb2_sb = alloc(late, "eb2_sb", [E, D])
        wr_sb = alloc(late, "wr_sb", [P, KC, E])
        br_b = alloc(late, "br_b", [P, E])
        lrow_b = alloc(late, "lrow_b", [P, 3, D])
        wfg = alloc(late, "wfg", [P, GB, E])
        hid = alloc(late, "hid", [P, 2, HC, GB * P])
        xg = hid[:, 0, 0:2, :].rearrange("p a (t d) -> p (a t) d", d=D)
        ag = hid[:, 0, 2:4, :].rearrange("p a (t d) -> p (a t) d", d=D)
        zg = hid[:, 1, 0:2, :].rearrange("p a (t d) -> p (a t) d", d=D)
        zTg = hid[:, 1, 2:4, :].rearrange("p a (t d) -> p (a t) d", d=KC * P).rearrange("p t (c q) -> p t c q", c=KC)
        lstats = alloc(late, "lstats", [P, GB, 6])
        lmv = alloc(late, "lmv", [P, GB, 2])
        lrs = alloc(late, "lrs", [P, GB])
        logit = alloc(late, "logit", [P, GB, E])
        top = alloc(late, "top", [P, GB, 8])
        topi = alloc(late, "topi", [P, GB, 8], U32)
        topf = alloc(late, "topf", [P, NB, 2])
        gw = alloc(late, "gw", [P, NB, 4])
        wfull = alloc(late, "wfull", [P, NB, E])
        wtmp = alloc(late, "wtmp", [P, NB, E])
        wfT = alloc(late, "wfT", [E, GB * P])
        late.close()

        edges_in = sem("edges_in")
        x_in = sem("x_in")
        mixw_in = sem("mixw_in")
        slots_zero = sem("slots_zero")
        consts = sem("consts")
        pool_seq = sem("pool_seq")
        dve_seq = sem("dve_seq")
        pool_passed = sem("pool_passed")
        dve_passed = sem("dve_passed")
        act_seq = sem("act_seq")
        r_ready = sem("r_ready")
        e_ready = sem("e_ready")
        z_ready = sem("z_ready")
        counts_done = sem("counts_done")
        sums_ready = sem("sums_ready")
        gb_done = sem("gb_done")
        sg_ready = sem("sg_ready")
        flags_done = sem("flags_done")
        flags_summed = sem("flags_summed")
        pos_done = sem("pos_done")
        dest_done = sem("dest_done")
        staged = [sem(f"staged{h}") for h in range(2)]
        scattered = [sem(f"scattered{h}") for h in range(2)]
        var_done = sem("var_done")
        std_done = sem("std_done")
        xn_done = sem("xn_done")
        tr_done = sem("tr_done")
        trc_done = sem("trc_done")
        kv_done = sem("kv_done")
        kv_read = sem("kv_read")
        kneg_done = sem("kneg_done")
        kexp_done = sem("kexp_done")
        kphi_done = sem("kphi_done")
        acc_done = sem("acc_done")
        sup_done = sem("sup_done")
        sup_read = sem("sup_read")
        sup_stored = sem("sup_stored")
        kvacc_done = sem("kvacc_done")
        kvbd_done = sem("kvbd_done")
        xn2_done = sem("xn2_done")
        tr2_done = sem("tr2_done")
        trc2_done = sem("trc2_done")
        q_done = sem("q_done")
        qneg_done = sem("qneg_done")
        qexp_done = sem("qexp_done")
        qphi_done = sem("qphi_done")
        att_done = sem("att_done")
        attn_done = sem("attn_done")
        wo_done = sem("wo_done")
        var1_done = sem("var1_done")
        std1_done = sem("std1_done")
        h1_done = sem("h1_done")
        trh_done = sem("trh_done")
        trhc_done = sem("trhc_done")
        ff1_done = sem("ff1_done")
        relu_done = sem("relu_done")
        ff2_done = sem("ff2_done")
        var2_done = sem("var2_done")
        std2_done = sem("std2_done")
        mix_done = sem("mix_done")
        tab_in = [sem(f"tab_in{h}") for h in range(2)]
        gathered = [sem(f"gathered{h}") for h in range(2)]
        hot_done = [sem(f"hot_done{h}") for h in range(2)]
        summed = [sem(f"summed{h}") for h in range(2)]
        carried = sem("carried")
        agg_stored = [sem(f"agg_stored{c}") for c in range(CARRY)]
        late_in = sem("late_in")
        ew_in = sem("ew_in")
        rg_in = sem("rg_in")
        rx_done = sem("rx_done")
        varA_done = sem("varA_done")
        stdA_done = sem("stdA_done")
        varB_done = sem("varB_done")
        stdB_done = sem("stdB_done")
        z_done = sem("z_done")
        trz_done = sem("trz_done")
        trzc_done = sem("trzc_done")
        logit_done = sem("logit_done")
        logit_read = sem("logit_read")
        gap_done = sem("gap_done")
        gexp_done = sem("gexp_done")
        wfull_done = sem("wfull_done")
        wfg_done = sem("wfg_done")
        wft_done = sem("wft_done")
        wftc_done = sem("wftc_done")
        bias_done = sem("bias_done")
        bias_read = sem("bias_read")
        up_done = sem("up_done")
        gelu_done = sem("gelu_done")
        down_done = sem("down_done")
        down_read = sem("down_read")
        y_done = sem("y_done")
        out_stored = sem("out_stored")

        MIXW_DMAS = 17
        LATE_DMAS = 7

        block = ctx.enter_context(nc.Block())

        @block.sync
        def _(sp):
            split = (P - 1) * EC
            sp.wait_ge(e_ready, 1)
            for buf, a in ((eb[:, :].bitcast(I32), src), (ea[:, :].bitcast(I32), dst), (ec[:, :], edge_weight)):
                sp.dma_start(buf[0:P - 1, :], a[0:split].rearrange("(p j) -> p j", p=P - 1)).then_inc(edges_in, 16)
                sp.dma_start(buf[P - 1:P, 0:TAILE], a[split:NE].rearrange("(p j) -> p j", p=1)).then_inc(edges_in, 16)
            sp.wait_ge(r_ready, 1)
            sp.dma_start(R[:, 0:NB - 1, :], x[0:(NB - 1) * P, :].rearrange("(t p) d -> p t d", p=P)).then_inc(x_in, 16)
            sp.dma_start(R[0:LASTN, NB - 1, :], x[(NB - 1) * P:N, :]).then_inc(x_in, 16)
            for w, a in ((wg_sb[:, :, :], gnn_w), (wkv_sb[:, :, 0:D], Wk), (wkv_sb[:, :, D:2 * D], Wv),
                         (wq_sb[:, :, :], Wq), (wo_sb[:, :, :], Wo), (w1_sb[:, :, :], W1), (w2_sb[:, :, :], W2)):
                sp.dma_start(w, a.rearrange("(c p) n -> p c n", p=P)).then_inc(mixw_in, 16)
            for n, a in enumerate((bo, b2, ln1_g, ln1_b, ln2_g, ln2_b)):
                sp.dma_start(row_b[:, n, :], a.partition_broadcast(P)).then_inc(mixw_in, 16)
            sp.dma_start(bkv_b[:, 0:D], bk.partition_broadcast(P)).then_inc(mixw_in, 16)
            sp.dma_start(bkv_b[:, D:2 * D], bv.partition_broadcast(P)).then_inc(mixw_in, 16)
            with nc.allow_non_contiguous_dma(reason="bias columns, a few kilobytes"):
                sp.dma_start(bq_col[:, :], bq.rearrange("(c p) -> p c", p=P)).then_inc(mixw_in, 16)
                sp.dma_start(b1_col[:, :], b1.rearrange("(c p) -> p c", p=P)).then_inc(mixw_in, 16)

            sp.wait_ge(pos_done, 1)

            def stage(it, h):
                col = it * (2 * SH) + h * SH
                sp.dma_start(st_rec[h][:, :, :], rec[:, ds(col, SH), :]).then_inc(staged[h], 16)
                sp.dma_start(st_pos[h][:, :], pos_i[:, ds(col, SH)]).then_inc(staged[h], 16)

            for h in range(2):
                stage(0, h)
            with sp.Fori(1, SCAT_STEPS) as it:
                for h in range(2):
                    sp.wait_ge(scattered[h], it * (16 * SH))
                    stage(it, h)
            for h in range(2):
                sp.wait_ge(scattered[h], SCAT_STEPS * 16 * SH)

            table = slots[0:P * NT, :].rearrange("(p t) c -> p t c", p=P)

            def load_slots(it, h):
                sp.dma_start(st_tab[h][:, :, :], table[:, ds(it * (2 * HT) + h * HT, HT), :]).then_inc(tab_in[h], 16)

            for h in range(2):
                load_slots(0, h)
            with sp.Fori(1, GATHER_STEPS) as it:
                for h in range(2):
                    sp.wait_ge(gathered[h], it * (16 * HT))
                    sp.wait_ge(hot_done[h], it)
                    load_slots(it, h)

            sp.wait_ge(carried, NG)
            for h in range(2):
                sp.wait_ge(gathered[h], GATHER_STEPS * 16 * HT)
            for c in range(CARRY):
                sp.wait_ge(agg_stored[c], NG // CARRY * 16)
            for n, a in enumerate((gnn_b, gamma, beta)):
                sp.dma_start(lrow_b[:, n, :], a.partition_broadcast(P)).then_inc(late_in, 16)
            sp.dma_start(br_b[:, :], br.partition_broadcast(P)).then_inc(late_in, 16)
            sp.dma_start(eb2_sb[:, :], eb2).then_inc(late_in, 16)
            sp.dma_start(wr_sb[:, :, :], Wr.rearrange("(c p) n -> p c n", p=P)).then_inc(late_in, 16)
            with nc.allow_non_contiguous_dma(reason="bias columns, a few kilobytes"):
                sp.dma_start(eb1_col[:, :], eb1.rearrange("e (c p) -> p (e c)", p=P)).then_inc(late_in, 16)

            def load_group(g, nb):
                row = g * (GB * P)
                if nb == GB:
                    sp.dma_start(xg[:, :, :], x[ds(row, GB * P), :].rearrange("(t p) d -> p t d", p=P)).then_inc(rg_in, 16)
                else:
                    sp.dma_start(xg[0:LASTN, 0, :], x[row:N, :]).then_inc(rg_in, 16)
                sp.dma_start(ag[:, 0:nb, :], agg[ds(row, nb * P), :].rearrange("(t p) d -> p t d", p=P)).then_inc(rg_in, 16)

            load_group(0, GB)
            sp.dma_start(ew1_sb[:, :, :, :], eW1.rearrange("e (c p) n -> p e c n", p=P)).then_inc(ew_in, 16)
            sp.dma_start(ew2_sb[:, :, :, :], eW2.rearrange("e (c p) n -> p e c n", p=P)).then_inc(ew_in, 16)
            with sp.Fori(1, FULL) as g:
                sp.wait_ge(rx_done, g)
                load_group(g, GB)
            sp.wait_ge(rx_done, FULL)
            load_group(FULL, 1)

            with sp.Fori(0, FULL) as g:
                sp.wait_ge(y_done, g + 1)
                sp.dma_start(out[ds(g * (GB * P), GB * P), :].rearrange("(t p) d -> p t d", p=P),
                             R[:, ds(g * GB, GB), :]).then_inc(out_stored, 16)
            sp.wait_ge(y_done, FULL + 1)
            sp.dma_start(out[FULL * GB * P:N, :], R[0:LASTN, NB - 1, :]).then_inc(out_stored, 16)
            sp.wait_ge(out_stored, 16 * (FULL + 1))

        @block.gpsimd
        def _(pool):
            seq = Chain(pool, pool_seq)
            seq(pool.memset(ones[:, :], 1.0))
            seq(pool.iota(iota_row[:, :], [[1, P]], base=0, channel_multiplier=0, allow_small_or_imprecise_dtypes=True))
            seq(pool.iota(iota_g[:, :], [[1, NG]], base=0, channel_multiplier=0, allow_small_or_imprecise_dtypes=True))
            seq(pool.affine_select(out=ident[:, :], in_=ones[:, :], compare_op=ALU.is_equal, fill=0.0, base=0,
                                   pattern=[[-1, P]], channel_multiplier=1))
            seq(pool.affine_select(out=tri[:, :], in_=ones[:, :], compare_op=ALU.is_gt, fill=0.0, base=0,
                                   pattern=[[1, P]], channel_multiplier=-1))
            bv3 = blockones[:, :].rearrange("p (h d) -> p h d", d=DH)
            seq(pool.affine_select(out=bv3, in_=ones[:, :].rearrange("p (h d) -> p h d", d=DH), compare_op=ALU.is_ge,
                                   fill=0.0, base=0, pattern=[[-DH, P // DH], [0, DH]], channel_multiplier=1))
            pool.affine_select(out=bv3, in_=bv3, compare_op=ALU.is_ge, fill=0.0, base=DH - 1,
                               pattern=[[DH, P // DH], [0, DH]], channel_multiplier=-1).then_inc(consts, 1)
            if ECP > EC:
                pool.iota(pos_i[:, EC:ECP], [[P, ECP - EC]], base=P * NT, channel_multiplier=1).then_inc(consts, 1)

            pool.wait_ge(slots_zero, 16 * ZERO_DMAS)
            with pool.Fori(0, SCAT_STEPS) as it:
                for h in range(2):
                    wait_apart(pool, staged[h], it * 32 + 32, pool_passed)
                    for j in range(SH):
                        pool.indirect_dma_start(
                            out=slots, out_offset=bass.IndirectOffsetOnAxis(ap=st_pos[h][:, j:j + 1], axis=0),
                            in_=st_rec[h][:, j, :], in_offset=None).then_inc(scattered[h], 16)

            pool.wait_ge(sup_stored, 16 * (FULL + 1))

            def gather(it, h):
                wait_apart(pool, tab_in[h], it * 16 + 16, pool_passed)
                for j in range(HT):
                    pool.indirect_dma_start(
                        out=rows[h][:, j, :], out_offset=None, in_=support,
                        in_offset=bass.IndirectOffsetOnAxis(ap=st_tab[h][:, j, 0:1].bitcast(I32), axis=0)
                    ).then_inc(gathered[h], 16)

            pool.wait_ge(mix_done, FULL + 1)
            for h in range(2):
                gather(0, h)
            with pool.Fori(1, GATHER_STEPS) as it:
                for h in range(2):
                    pool.wait_ge(summed[h], it * HALF_G)
                    gather(it, h)

        @block.tensor
        def _(pe):
            pe.wait_ge(consts, 1)
            pe.wait_ge(counts_done, 1)
            pe.matmul(ps[6][:, 0:NB], lhsT=tri[:, :], rhs=cnt[:, :], start=True, stop=True)
            pe.matmul(ps[6][:, 64:64 + NB], lhsT=ones[:, :], rhs=cnt[:, :], start=True, stop=True)
            pe.matmul(ps[6][0:NB, 128:129], lhsT=cnt[:, :], rhs=ones[:, 0:1], start=True, stop=True).then_inc(sums_ready, 1)
            pe.wait_ge(gb_done, 1)
            pe.matmul(ps[5][0:NB, 0:1], lhsT=tri[0:NB, 0:NB], rhs=gcol[0:NB, 0:1], start=True, stop=True).then_inc(sg_ready, 1)
            pe.wait_ge(flags_done, 1)
            for k, bank in enumerate((6, 7, 5)):
                last = pe.matmul(ps[bank][:, 0:NG], lhsT=ones[0:NB, :], rhs=gflags[0:NB, k, :], start=True, stop=True)
            last.then_inc(flags_summed, 1)
            pe.wait_ge(dest_done, 1)

            def transposes(nb, source, banks, done):
                for c in range(KC):
                    for j in range(nb):
                        last = pe.transpose(ps[banks[c]][:, j * P:(j + 1) * P], source[:, j, c * P:(c + 1) * P], ident[:, :])
                last.then_inc(done, 1)

            pe.wait_ge(mixw_in, 16 * MIXW_DMAS)
            pe.matmul(ps[5][:, 0:2 * (P + 4)], lhsT=zeros[:, 0:P], rhs=zeros[:, 0:2 * (P + 4)], start=True, stop=False)

            def pass1(g, nb):
                rowsn = P if nb == GB else LASTN
                pe.wait_ge(xn_done, g + 1)
                transposes(nb, xn, (0, 1), tr_done)
                pe.wait_ge(trc_done, g + 1)

                def products(j):
                    if j >= 2:
                        pe.wait_ge(kv_read, g * GB + (j - 1))
                        pe.wait_ge(sup_read, g * GB + (j - 1))
                    for c in range(KC):
                        last = pe.matmul(ps[2 + j % 2][:, :], lhsT=xnT[:, c, j * P:(j + 1) * P], rhs=wkv_sb[:, c, :],
                                         start=(c == 0), stop=(c == KC - 1))
                    last.then_inc(kv_done, 1)
                    for c in range(KC):
                        last = pe.matmul(ps[4 + j % 2 * 2][:, 0:D], lhsT=xnT[:, c, j * P:(j + 1) * P],
                                         rhs=wg_sb[:, c, :], start=(c == 0), stop=(c == KC - 1))
                    last.then_inc(sup_done, 1)

                def accumulate(j):
                    pe.wait_ge(kphi_done, g * GB + (j + 1))
                    for c in range(KC):
                        last = pe.matmul(ps[5][:, c * (P + 4):c * (P + 4) + P + 1], lhsT=kphi[0:rowsn, j % 2, c * P:(c + 1) * P],
                                         rhs=vaug[0:rowsn, j % 2, c, 0:P + 1], start=False, stop=False, skip_group_check=True)
                    last.then_inc(acc_done, 1)

                for j in range(nb):
                    products(j)
                    if j:
                        accumulate(j - 1)
                accumulate(nb - 1)

            over_groups(pe, None, 0, pass1)
            pe.matmul(ps[5][:, 0:2 * (P + 4)], lhsT=zeros[:, 0:P], rhs=zeros[:, 0:2 * (P + 4)], start=False, stop=True).then_inc(kvacc_done, 1)

            pe.wait_ge(kvbd_done, 1)

            def pass2(g, nb):
                T = nb * P
                pe.wait_ge(xn2_done, g + 1)
                transposes(nb, xn, (0, 1), tr2_done)
                pe.wait_ge(trc2_done, g + 1)
                for hh in range(KC):
                    for c in range(KC):
                        last = pe.matmul(ps[2 + hh][:, 0:T], lhsT=wq_sb[:, c, hh * P:(hh + 1) * P], rhs=xnT[:, c, 0:T],
                                         start=(c == 0), stop=(c == KC - 1))
                last.then_inc(q_done, 1)
                pe.wait_ge(qphi_done, g + 1)
                for hh in range(KC):
                    pe.matmul(ps[4 + hh][:, 0:T], lhsT=kvbd[:, hh, :], rhs=qphi[:, hh, 0:T], start=True, stop=True)
                    last = pe.matmul(ps[6 + hh][:, 0:T], lhsT=ksel[:, hh, :], rhs=qphi[:, hh, 0:T], start=True, stop=True)
                last.then_inc(att_done, 1)
                pe.wait_ge(attn_done, g + 1)
                for j in range(nb):
                    for c in range(KC):
                        last = pe.matmul(ps[2 + j // 2][:, (j % 2) * D:(j % 2 + 1) * D], lhsT=attnT[:, c, j * P:(j + 1) * P],
                                         rhs=wo_sb[:, c, :], start=(c == 0), stop=(c == KC - 1))
                last.then_inc(wo_done, 1)
                pe.wait_ge(h1_done, g + 1)
                transposes(nb, h1, (0, 1), trh_done)
                pe.wait_ge(trhc_done, g + 1)
                for f in range(FC):
                    if f >= 2:
                        pe.wait_ge(relu_done, g * FC + (f - 1))
                    for c in range(KC):
                        last = pe.matmul(ps[4 + f % 2][:, 0:T], lhsT=w1_sb[:, c, f * P:(f + 1) * P], rhs=hT[:, c, 0:T],
                                         start=(c == 0), stop=(c == KC - 1))
                    last.then_inc(ff1_done, 1)
                pe.wait_ge(relu_done, g * FC + FC)
                for j in range(nb):
                    for f in range(FC):
                        last = pe.matmul(ps[6 + j // 2][:, (j % 2) * D:(j % 2 + 1) * D], lhsT=uT[:, f, j * P:(j + 1) * P],
                                         rhs=w2_sb[:, f, :], start=(f == 0), stop=(f == FC - 1))
                last.then_inc(ff2_done, 1)

            over_groups(pe, None, 0, pass2)

            def sum_half(it, h, wait_free):
                pe.wait_ge(hot_done[h], it + 1)
                pe.wait_ge(gathered[h], it * (16 * HT) + 16 * HT)
                for q in range(HALF_G):
                    c = h * HALF_G + q
                    if wait_free:
                        pe.wait_ge(carried, it * CARRY + (c + 1 - CARRY))
                    for t in range(GT):
                        k = q * GT + t
                        last = pe.matmul(ps[c][:, 0:D], lhsT=hot[h][:, k, :], rhs=rows[h][:, k, :],
                                         start=(t == 0), stop=(t == GT - 1))
                    last.then_inc(summed[h], 1)

            for h in range(2):
                sum_half(0, h, False)
            with pe.Fori(1, GATHER_STEPS) as it:
                for h in range(2):
                    sum_half(it, h, True)

            pe.wait_ge(late_in, 16 * LATE_DMAS)

            def route(g, nb):
                pe.wait_ge(z_done, g + 1)
                transposes(nb, zg, (2, 3), trz_done)
                pe.wait_ge(trzc_done, g + 1)
                for j in range(nb):
                    for c in range(KC):
                        last = pe.matmul(ps[4][:, j * E:(j + 1) * E], lhsT=zTg[:, j, c, :], rhs=wr_sb[:, c, :],
                                         start=(c == 0), stop=(c == KC - 1))
                last.then_inc(logit_done, 1)

            over_groups(pe, None, 0, route)

            pe.wait_ge(wfull_done, 1)
            pe.wait_ge(ew_in, 32)

            def experts(g, nb):
                T = nb * P
                pe.wait_ge(wfg_done, g + 1)
                for j in range(nb):
                    last = pe.transpose(ps[0][0:E, j * P:(j + 1) * P], wfg[:, j, :], ident[:, :])
                last.then_inc(wft_done, 1)
                pe.wait_ge(wftc_done, g + 1)
                for j in range(nb):
                    last = pe.matmul(ps[4 + j][:, 0:D], lhsT=wfT[:, j * P:(j + 1) * P], rhs=eb2_sb[:, :], start=True, stop=True)
                last.then_inc(bias_done, 1)

                def up(e):
                    for f in range(HC):
                        if e:
                            pe.wait_ge(gelu_done, g * (E * HC) + ((e - 1) * HC + f + 1))
                        for c in range(KC):
                            last = pe.matmul(ps[f][:, 0:T], lhsT=ew1_sb[:, e, c, f * P:(f + 1) * P],
                                             rhs=zT[:, ds(g * GB, nb), c, :], start=(c == 0), stop=(c == KC - 1))
                        last.then_inc(up_done, 1)

                def down(e):
                    pe.wait_ge(gelu_done, g * (E * HC) + (e + 1) * HC)
                    for j in range(nb):
                        if e == 0:
                            pe.wait_ge(bias_read, g * GB + (j + 1))
                        else:
                            pe.wait_ge(down_read, g * (E * GB) + ((e - 1) * nb + j + 1))
                        for f in range(HC):
                            last = pe.matmul(ps[4 + j][:, 0:D], lhsT=hid[:, e % 2, f, j * P:(j + 1) * P],
                                             rhs=ew2_sb[:, e, f, :], start=(f == 0), stop=(f == HC - 1))
                        last.then_inc(down_done, 1)

                up(0)
                for e in range(E):
                    if e + 1 < E:
                        up(e + 1)
                    down(e)

            over_groups(pe, None, 0, experts)

        @block.scalar
        def _(act):
            seq = Chain(act, act_seq)
            act.wait_ge(z_ready, 1)
            for k in range(ZERO_DMAS):
                act.dma_start(slots[0:P * NT, :].rearrange("(p a t) c -> a p (t c)", p=P, a=ZERO_DMAS)[k, :, :],
                              zeros[:, :]).then_inc(slots_zero, 16)
            act.wait_ge(var_done, 1)
            act.activation(rstd[:, :], mv[:, :, 1], ACT.Sqrt, bias=eps_col[:, 0:1]).then_inc(std_done, 1)

            def copy_transposed(g, nb, wait, to, done):
                T = nb * P
                act.wait_ge(wait, g + 1)
                act.activation(to[:, 0, 0:T], ps[0][:, 0:T], ACT.Copy)
                act.activation(to[:, 1, 0:T], ps[1][:, 0:T], ACT.Copy).then_inc(done, 1)

            def pass1(g, nb):
                copy_transposed(g, nb, tr_done, xnT, trc_done)
                for j in range(nb):
                    n = g * GB + (j + 1)
                    act.wait_ge(kneg_done, n)
                    act.activation(kneg[:, j % 2, :], kneg[:, j % 2, :], ACT.Exp).then_inc(kexp_done, 1)
                    act.wait_ge(sup_done, n)
                    act.activation(sup_sb[:, j, :], ps[4 + j % 2 * 2][:, 0:D], ACT.Copy).then_inc(sup_read, 1)
                act.wait_ge(sup_read, g * GB + nb)
                act.dma_start(support[ds(g * (GB * P), nb * P), :].rearrange("(t p) d -> p t d", p=P),
                              sup_sb[:, 0:nb, :]).then_inc(sup_stored, 16)
                act.wait_ge(sup_stored, g * 16 + 16)

            over_groups(act, None, 0, pass1)

            def pass2(g, nb):
                T = nb * P
                copy_transposed(g, nb, tr2_done, xnT, trc2_done)
                for hh in range(KC):
                    act.wait_ge(qneg_done, g * KC + (hh + 1))
                    act.activation(qneg[:, hh, 0:T], qneg[:, hh, 0:T], ACT.Exp).then_inc(qexp_done, 1)
                act.wait_ge(var1_done, g + 1)
                act.activation(grs[:, 0:nb], gmv[:, 0:nb, 1], ACT.Sqrt, bias=eps_col[:, 0:1]).then_inc(std1_done, 1)
                copy_transposed(g, nb, trh_done, hT, trhc_done)
                for f in range(FC):
                    act.wait_ge(ff1_done, g * FC + (f + 1))
                    act.activation(uT[:, f, 0:T], ps[4 + f % 2][:, 0:T], ACT.Relu, bias=b1_col[:, f:f + 1]).then_inc(relu_done, 1)
                act.wait_ge(var2_done, g + 1)
                act.activation(grs[:, 0:nb], gmv[:, 0:nb, 1], ACT.Sqrt, bias=eps_col[:, 0:1]).then_inc(std2_done, 1)

            over_groups(act, None, 0, pass2)

            act.wait_ge(dest_done, 1)
            with act.Fori(0, GATHER_STEPS) as it:
                for c in range(CARRY):
                    where = act.value_load(dest_i[0:1, ds(it * CARRY + c, 1)], min_val=0, max_val=NB + NG - 1)
                    act.wait_ge(carried, it * CARRY + (c + 1))
                    act.dma_start(agg[ds(where * P, P), :], carry[:, c, :]).then_inc(agg_stored[c], 16)

            def route(g, nb):
                act.wait_ge(varA_done, g + 1)
                act.activation(lrs[:, 0:nb], lmv[:, 0:nb, 1], ACT.Sqrt, bias=eps_col[:, 0:1]).then_inc(stdA_done, 1)
                act.wait_ge(varB_done, g + 1)
                act.activation(lrs[:, 0:nb], lmv[:, 0:nb, 1], ACT.Sqrt, bias=eps_col[:, 0:1]).then_inc(stdB_done, 1)
                act.wait_ge(trz_done, g + 1)
                for c in range(KC):
                    ins = act.activation(zT[:, ds(g * GB, nb), c, :], ps[2 + c][:, 0:nb * P].rearrange("p (t q) -> p t q", q=P), ACT.Copy)
                    last = act.activation(zTg[:, 0:nb, c, :], ps[2 + c][:, 0:nb * P].rearrange("p (t q) -> p t q", q=P), ACT.Copy)
                last.then_inc(trzc_done, 1)

            over_groups(act, None, 0, route)
            act.wait_ge(gap_done, 1)
            act.activation(gw[:, :, 1], gw[:, :, 0], ACT.Exp).then_inc(gexp_done, 1)

            def experts(g, nb):
                T = nb * P
                act.wait_ge(wft_done, g + 1)
                act.activation(wfT[:, 0:T], ps[0][0:E, 0:T], ACT.Copy).then_inc(wftc_done, 1)
                for e in range(E):
                    for f in range(HC):
                        act.wait_ge(up_done, g * (E * HC) + (e * HC + f + 1))
                        if f == 0 and e >= 2:
                            act.wait_ge(down_done, g * (E * GB) + (e - 1) * nb)
                        act.activation(hid[:, e % 2, f, 0:T], ps[f][:, 0:T], ACT.Gelu,
                                       bias=eb1_col[:, e * HC + f:e * HC + f + 1]).then_inc(gelu_done, 1)

            over_groups(act, None, 0, experts)

        @block.vector
        def _(dve):
            seq = Chain(dve, dve_seq, dve_passed)
            ebi, eai, eci = eb[:, :].bitcast(I32), ea[:, :].bitcast(I32), ec[:, :].bitcast(I32)
            seq(dve.memset(ebi[:, TAILE:EC], N))
            seq(dve.memset(eai[:, TAILE:EC], 0))
            dve.memset(ec[:, TAILE:EC], 0.0).then_inc(e_ready, 1)
            dve.memset(R[:, NB - 1, :], 0.0).then_inc(r_ready, 1)
            dve.memset(zeros[:, :], 0.0).then_inc(z_ready, 1)
            dve.memset(eps_col[:, :], EPS)
            dve.memset(vaug[:, :, :, P:P + 1], 1.0)
            dve.memset(carry[:, CARRY - 1, :], 0.0)
            seq(dve.memset(rec[:, :, :], 0.0))

            dve.wait_ge(edges_in, 16 * 6)
            dve.tensor_copy(out=rec[:, 0:EC, 0].bitcast(I32), in_=eai)
            seq(dve.tensor_copy(out=rec[:, 0:EC, 2], in_=ec[:, :]))
            dve.tensor_scalar(out=eai, in0=ebi, scalar1=7, scalar2=None, op0=ALU.logical_shift_right)
            seq(dve.tensor_scalar(out=eci, in0=ebi, scalar1=127, scalar2=None, op0=ALU.bitwise_and))
            dve.tensor_copy(out=hi[:, :], in_=eai)
            seq(dve.tensor_copy(out=rec[:, 0:EC, 1], in_=eci))

            dve.wait_ge(consts, 1)
            seq.turn(0, 0)
            with dve.Fori(0, NB) as b:
                seq.off, seq.k = b * 1, 0
                seq(dve.tensor_scalar(out=ea[:, :], in0=hi[:, :], scalar1=iota_row[:, ds(b, 1)], scalar2=None,
                                      op0=ALU.is_equal, op1=ALU.add, accum_out=cnt[:, ds(b, 1)]))
            seq.after(NB, 1)
            dve.sem_inc(counts_done, 1)

            dve.wait_ge(sums_ready, 1)
            def groups_of(count, out_f, out_i):
                seq(dve.tensor_scalar(out=out_i, in0=count, scalar1=float(GS - 1), scalar2=None, op0=ALU.add))
                seq(dve.tensor_scalar(out=out_i, in0=out_i, scalar1=GS.bit_length() - 1, scalar2=None, op0=ALU.logical_shift_right))
                seq(dve.tensor_scalar(out=out_f, in0=out_i, scalar1=1.0, scalar2=None, op0=ALU.max))
            groups_of(ps[6][0:NB, 128:129], gcol[0:NB, 0:1], gcol_i[0:NB, :])
            dve.sem_inc(gb_done, 1)
            groups_of(ps[6][:, 64:64 + NB], gcount[:, :], gint[:, :])
            seq(dve.tensor_tensor_scan(out=prefix[:, :], data0=ones[:, 0:NB], data1=gcount[:, :], initial=0.0,
                                       op0=ALU.mult, op1=ALU.add))
            seq(dve.tensor_tensor(out=prefix[:, :], in0=prefix[:, :], in1=gcount[:, :], op=ALU.subtract))
            seq(dve.tensor_scalar(out=base[:, :], in0=prefix[:, :], scalar1=float(GS), scalar2=-1.0, op0=ALU.mult, op1=ALU.add))
            seq(dve.tensor_tensor(out=base[:, :], in0=base[:, :], in1=ps[6][:, 0:NB], op=ALU.add))

            dve.wait_ge(sg_ready, 1)
            seq(dve.tensor_copy(out=gcol[0:NB, 1:2], in_=ps[5][0:NB, 0:1]))
            seq(dve.tensor_tensor(out=gcol[0:NB, 2:3], in0=gcol[0:NB, 1:2], in1=gcol[0:NB, 0:1], op=ALU.add))
            seq(dve.tensor_scalar(out=gcol[0:NB, 3:4], in0=gcol[0:NB, 2:3], scalar1=-1.0, scalar2=None, op0=ALU.add))
            for k, (col, op) in enumerate(((2, ALU.is_ge), (1, ALU.is_equal), (3, ALU.is_equal))):
                seq(dve.tensor_scalar(out=gflags[0:NB, k, :], in0=iota_g[0:NB, :], scalar1=gcol[0:NB, col:col + 1],
                                      scalar2=None, op0=op))
            dve.sem_inc(flags_done, 1)

            dve.wait_ge(flags_summed, 1)
            seq.turn(0, 0)
            with dve.Fori(0, NB) as b:
                seq.off, seq.k = b * 3, 0
                seq(dve.tensor_scalar(out=ea[:, :], in0=hi[:, :], scalar1=iota_row[:, ds(b, 1)], scalar2=None, op0=ALU.is_equal))
                seq(dve.tensor_tensor_scan(out=ec[:, :], data0=ones[:, 0:1].to_broadcast([P, EC]), data1=ea[:, :],
                                           initial=base[:, ds(b, 1)], op0=ALU.mult, op1=ALU.add), apart=True)
                seq(dve.copy_predicated(eb[:, :], eai, ec[:, :]))
            seq.after(NB, 3)
            seq(dve.tensor_copy(out=eai, in_=eb[:, :]))
            seq(dve.tensor_scalar(out=eci, in0=eai, scalar1=2, scalar2=127, op0=ALU.logical_shift_right, op1=ALU.bitwise_and))
            seq(dve.tensor_scalar(out=eb[:, :], in0=eci, scalar1=float(NT), scalar2=None, op0=ALU.mult))
            seq(dve.tensor_scalar(out=eci, in0=eai, scalar1=9, scalar2=None, op0=ALU.logical_shift_right))
            seq(dve.scalar_tensor_tensor(out=eb[:, :], in0=eci, scalar=float(GT), in1=eb[:, :], op0=ALU.mult, op1=ALU.add))
            seq(dve.tensor_scalar(out=eci, in0=eai, scalar1=3, scalar2=None, op0=ALU.bitwise_and))
            dve.wait_ge(consts, 1 + (ECP > EC))
            dve.tensor_tensor(out=pos_i[:, 0:EC], in0=eci, in1=eb[:, :], op=ALU.add).then_inc(pos_done, 1)

            dve.wait_ge(flags_summed, 1)
            dve.tensor_scalar(out=keep[:, :], in0=ps[7][:, 0:NG], scalar1=-1.0, scalar2=1.0, op0=ALU.mult, op1=ALU.add)
            seq(dve.tensor_scalar(out=iota_g[:, :], in0=iota_g[:, :], scalar1=float(NB), scalar2=None, op0=ALU.add))
            seq(dve.tensor_tensor(out=dest_f[:, :], in0=ps[6][:, 0:NG], in1=iota_g[:, :], op=ALU.subtract))
            seq(dve.tensor_tensor(out=dest_f[:, :], in0=dest_f[:, :], in1=ps[5][:, 0:NG], op=ALU.mult))
            dve.tensor_tensor(out=dest_i[:, :], in0=dest_f[:, :], in1=iota_g[:, :], op=ALU.add).then_inc(dest_done, 1)

            dve.wait_ge(x_in, 32)
            seq.turn(0, 0)
            with dve.Fori(0, NB // STATB) as t:
                seq.off, seq.k = t * 3, 0
                for j in range(STATB):
                    last = dve.bn_stats(out=stats[:, j, :], in_=R[:, ds(t * STATB + j, 1), :].rearrange("p a d -> p (a d)"))
                seq(last, apart=True)
                for j in range(STATB):
                    last = dve.bn_aggr(out=smv[:, j, :], in_=stats[:, j, :])
                seq(last)
                seq(dve.tensor_copy(out=mv[:, ds(t * STATB, STATB), :], in_=smv[:, :, :]))
            seq.after(NB // STATB, 3)
            dve.sem_inc(var_done, 1)
            dve.wait_ge(std_done, 1)
            seq(dve.reciprocal(out=rstd[:, :], in_=rstd[:, :]))

            def normalise(g, nb, to, source, dynamic):
                for j in range(nb):
                    n = g * GB + j
                    s = source[:, ds(n, 1), :].rearrange("p a d -> p (a d)") if dynamic else source[:, j, :]
                    last = dve.tensor_scalar(out=to[:, j, :], in0=s, scalar1=mv[:, ds(n, 1), 0:1].rearrange("p a d -> p (a d)"),
                                             scalar2=rstd[:, ds(n, 1)], op0=ALU.subtract, op1=ALU.mult)
                return last

            dve.wait_ge(mixw_in, 16 * MIXW_DMAS)

            def pass1(g, nb):
                normalise(g, nb, xn, R, True).then_inc(xn_done, 1)
                for j in range(nb):
                    n = g * GB + (j + 1)
                    dve.wait_ge(kv_done, n)
                    if j >= 2:
                        dve.wait_ge(acc_done, g * GB + (j - 1))
                    bank = ps[2 + j % 2]
                    seq(dve.tensor_tensor(out=kraw[:, j % 2, :], in0=bank[:, 0:D], in1=bkv_b[:, 0:D], op=ALU.add))
                    dve.tensor_scalar(out=kneg[:, j % 2, :], in0=kraw[:, j % 2, :], scalar1=0.0, scalar2=None,
                                      op0=ALU.min).then_inc(kneg_done, 1)
                    dve.tensor_tensor(out=vaug[:, j % 2, :, 0:P], in0=bank[:, D:2 * D].rearrange("p (c e) -> p c e", c=KC),
                                      in1=bkv_b[:, D:2 * D].rearrange("p (c e) -> p c e", c=KC), op=ALU.add).then_inc(kv_read, 1)
                    dve.wait_ge(kexp_done, n)
                    dve.scalar_tensor_tensor(out=kphi[:, j % 2, :], in0=kraw[:, j % 2, :], scalar=0.0, in1=kneg[:, j % 2, :],
                                             op0=ALU.max, op1=ALU.add).then_inc(kphi_done, 1)

            over_groups(dve, seq, GB, pass1)

            dve.wait_ge(kvacc_done, 1)
            for c in range(KC):
                o = c * (P + 4)
                dve.tensor_tensor(out=kvbd[:, c, :], in0=ps[5][:, o:o + P], in1=blockones[:, :], op=ALU.mult)
                seq(dve.tensor_copy(out=ksum[:, c:c + 1], in_=ps[5][:, o + P:o + P + 1]))
            for c in range(KC):
                last = dve.tensor_scalar(out=ksel[:, c, :], in0=blockones[:, :], scalar1=ksum[:, c:c + 1], scalar2=None, op0=ALU.mult)
            last.then_inc(kvbd_done, 1)

            def wide(row, nb):
                return row_b[:, row:row + 1, :].to_broadcast([P, nb, D])

            def layer_norm(nb, t, affine, to, var_ready, std_ready, g, s=stats, m=gmv, r=grs):
                for j in range(nb):
                    last = dve.bn_stats(out=s[:, j, :], in_=t[:, j, :])
                seq(last, apart=True)
                for j in range(nb):
                    last = dve.bn_aggr(out=m[:, j, :], in_=s[:, j, :])
                last.then_inc(var_ready, 1)
                dve.wait_ge(std_ready, g + 1)
                seq(dve.reciprocal(out=r[:, 0:nb], in_=r[:, 0:nb]))
                for j in range(nb):
                    if affine is None:
                        last = dve.tensor_scalar(out=to(j), in0=t[:, j, :], scalar1=m[:, j, 0:1], scalar2=r[:, j:j + 1],
                                                 op0=ALU.subtract, op1=ALU.mult)
                    else:
                        last = dve.scalar_tensor_tensor(out=t[:, j, :], in0=t[:, j, :], scalar=m[:, j, 0:1], in1=affine[0],
                                                        op0=ALU.subtract, op1=ALU.mult)
                if affine is not None:
                    seq(last)
                    for j in range(nb):
                        last = dve.scalar_tensor_tensor(out=to(j), in0=t[:, j, :], scalar=r[:, j:j + 1], in1=affine[1],
                                                        op0=ALU.mult, op1=ALU.add)
                return last

            def pass2(g, nb):
                T = nb * P
                normalise(g, nb, xn, R, True).then_inc(xn2_done, 1)
                dve.wait_ge(q_done, g + 1)
                for hh in range(KC):
                    dve.tensor_scalar(out=qneg[:, hh, 0:T], in0=ps[2 + hh][:, 0:T], scalar1=bq_col[:, hh:hh + 1], scalar2=0.0,
                                      op0=ALU.add, op1=ALU.min).then_inc(qneg_done, 1)
                    last = dve.tensor_scalar(out=qphi[:, hh, 0:T], in0=ps[2 + hh][:, 0:T], scalar1=bq_col[:, hh:hh + 1], scalar2=0.0,
                                             op0=ALU.add, op1=ALU.max)
                seq(last)
                for hh in range(KC):
                    dve.wait_ge(qexp_done, g * KC + (hh + 1))
                    last = dve.tensor_tensor(out=qphi[:, hh, 0:T], in0=qphi[:, hh, 0:T], in1=qneg[:, hh, 0:T], op=ALU.add)
                last.then_inc(qphi_done, 1)
                dve.wait_ge(att_done, g + 1)
                for hh in range(KC):
                    last = dve.tensor_scalar(out=attnT[:, hh, 0:T], in0=ps[6 + hh][:, 0:T], scalar1=1e-6, scalar2=None, op0=ALU.add)
                seq(last)
                for hh in range(KC):
                    last = dve.reciprocal(out=attnT[:, hh, 0:T], in_=attnT[:, hh, 0:T])
                seq(last)
                for hh in range(KC):
                    last = dve.tensor_tensor(out=attnT[:, hh, 0:T], in0=ps[4 + hh][:, 0:T], in1=attnT[:, hh, 0:T], op=ALU.mult)
                last.then_inc(attn_done, 1)
                seq(dve.tensor_tensor(out=xn[:, 0:nb, :], in0=xn[:, 0:nb, :], in1=wide(0, nb), op=ALU.add))
                dve.wait_ge(wo_done, g + 1)
                for q in range(-(-nb // 2)):
                    w = min(2, nb - 2 * q)
                    last = dve.tensor_tensor(out=tmp[:, 2 * q:2 * q + w, :], in0=xn[:, 2 * q:2 * q + w, :],
                                             in1=ps[2 + q][:, 0:w * D].rearrange("p (t d) -> p t d", d=D), op=ALU.add)
                seq(last)
                layer_norm(nb, tmp, (row_b[:, 2, :], row_b[:, 3, :]), lambda j: h1[:, j, :], var1_done, std1_done, g).then_inc(h1_done, 1)
                dve.wait_ge(trh_done, g + 1)
                dve.wait_ge(h1_done, g + 1)
                seq(dve.tensor_tensor(out=h1[:, 0:nb, :], in0=h1[:, 0:nb, :], in1=wide(1, nb), op=ALU.add))
                dve.wait_ge(ff2_done, g + 1)
                for q in range(-(-nb // 2)):
                    w = min(2, nb - 2 * q)
                    last = dve.tensor_tensor(out=tmp[:, 2 * q:2 * q + w, :], in0=h1[:, 2 * q:2 * q + w, :],
                                             in1=ps[6 + q][:, 0:w * D].rearrange("p (t d) -> p t d", d=D), op=ALU.add)
                seq(last)
                layer_norm(nb, tmp, (row_b[:, 4, :], row_b[:, 5, :]),
                           lambda j: R[:, ds(g * GB + j, 1), :].rearrange("p a d -> p (a d)"), var2_done, std2_done, g).then_inc(mix_done, 1)

            PASS2_SEQ = 13
            over_groups(dve, seq, PASS2_SEQ, pass2)

            dve.wait_ge(mix_done, FULL + 1)

            def select(it, h, wait_free):
                dve.wait_ge(tab_in[h], it * 16 + 16)
                if wait_free:
                    dve.wait_ge(summed[h], it * HALF_G)
                for k in range(HT):
                    last = dve.tensor_scalar(out=hot[h][:, k, :], in0=iota_row[:, :], scalar1=st_tab[h][:, k, 1:2],
                                             scalar2=st_tab[h][:, k, 2:3], op0=ALU.is_equal, op1=ALU.mult)
                last.then_inc(hot_done[h], 1)

            def carry_on(it, h, wait_stored):
                for q in range(HALF_G):
                    c = h * HALF_G + q
                    dve.wait_ge(summed[h], it * HALF_G + (q + 1))
                    if wait_stored:
                        dve.wait_ge(agg_stored[c], it * 16)
                    dve.scalar_tensor_tensor(out=carry[:, c, :], in0=carry[:, (c - 1) % CARRY, :],
                                             scalar=keep[:, ds(it * CARRY + c, 1)], in1=ps[c][:, 0:D],
                                             op0=ALU.mult, op1=ALU.add).then_inc(carried, 1)
                    dve.wait_ge(carried, it * CARRY + (c + 1))

            def step(it, stored_before, stored):
                select(it, 0, True)
                carry_on(it - 1, 1, stored_before)
                select(it, 1, True)
                carry_on(it, 0, stored)

            select(0, 0, False)
            select(0, 1, False)
            carry_on(0, 0, False)
            step(1, False, True)
            with dve.Fori(2, GATHER_STEPS) as it:
                step(it, True, True)
            carry_on(GATHER_STEPS - 1, 1, True)

            dve.wait_ge(late_in, 16 * LATE_DMAS)

            def route(g, nb):
                dve.wait_ge(rg_in, g * 32 + 32)
                seq(normalise(g, nb, zg, xg, False))
                seq(dve.tensor_tensor(out=ag[:, 0:nb, :], in0=ag[:, 0:nb, :], in1=zg[:, 0:nb, :], op=ALU.add))
                seq(dve.tensor_tensor(out=ag[:, 0:nb, :], in0=ag[:, 0:nb, :], in1=lrow_b[:, 0:1, :].to_broadcast([P, nb, D]), op=ALU.add))
                seq(dve.scalar_tensor_tensor(out=ag[:, 0:nb, :], in0=ag[:, 0:nb, :], scalar=0.0, in1=xg[:, 0:nb, :],
                                             op0=ALU.max, op1=ALU.add))
                seq(dve.tensor_tensor(out=R[:, ds(g * GB, nb), :], in0=R[:, ds(g * GB, nb), :], in1=ag[:, 0:nb, :], op=ALU.add))
                dve.sem_inc(rx_done, 1)
                seq(dve.tensor_copy(out=zg[:, 0:nb, :], in_=R[:, ds(g * GB, nb), :]))
                seq(layer_norm(nb, zg, None, lambda j: zg[:, j, :], varA_done, stdA_done, g, lstats, lmv, lrs))
                layer_norm(nb, zg, (lrow_b[:, 1, :], lrow_b[:, 2, :]), lambda j: zg[:, j, :], varB_done, stdB_done, g,
                           lstats, lmv, lrs).then_inc(z_done, 1)
                dve.wait_ge(logit_done, g + 1)
                seq(dve.tensor_tensor(out=logit[:, 0:nb, :], in0=ps[4][:, 0:nb * E].rearrange("p (t e) -> p t e", e=E),
                                      in1=br_b[:, None, :].to_broadcast([P, nb, E]), op=ALU.add), apart=True)
                for j in range(nb):
                    seq(dve.max(out=top[:, j, :], in_=logit[:, j, :]), apart=True)
                    seq(dve.max_index(out=topi[:, j, :], in_max=top[:, j, :], in_values=logit[:, j, :]), apart=True)
                seq(dve.tensor_tensor(out=gw[:, ds(g * GB, nb), 0], in0=top[:, 0:nb, 1], in1=top[:, 0:nb, 0], op=ALU.subtract))
                seq(dve.tensor_copy(out=topf[:, ds(g * GB, nb), :], in_=topi[:, 0:nb, 0:2]))

            over_groups(dve, seq, 6 + 2 + 1 + 3 + 1 + 2 * GB + 2, route)

            dve.sem_inc(gap_done, 1)
            dve.wait_ge(gexp_done, 1)
            seq(dve.tensor_scalar(out=gw[:, :, 2], in0=gw[:, :, 1], scalar1=1.0, scalar2=None, op0=ALU.add))
            seq(dve.reciprocal(out=gw[:, :, 2], in_=gw[:, :, 2]))
            seq(dve.tensor_tensor(out=gw[:, :, 3], in0=gw[:, :, 1], in1=gw[:, :, 2], op=ALU.mult))

            def spread(to, k):
                seq(dve.tensor_tensor(out=to[:, :, :], in0=iota_row[:, None, 0:E].to_broadcast([P, NB, E]),
                                      in1=topf[:, :, k:k + 1].to_broadcast([P, NB, E]), op=ALU.is_equal))
                seq(dve.tensor_tensor(out=to[:, :, :], in0=to[:, :, :], in1=gw[:, :, 2 + k:3 + k].to_broadcast([P, NB, E]), op=ALU.mult))
            spread(wfull, 0)
            spread(wtmp, 1)
            dve.tensor_tensor(out=wfull[:, :, :], in0=wfull[:, :, :], in1=wtmp[:, :, :], op=ALU.add).then_inc(wfull_done, 1)
            dve.wait_ge(wfull_done, 1)

            def experts(g, nb):
                def block_of(a, j):
                    return a[:, ds(g * GB + j, 1), :].rearrange("p a d -> p (a d)")
                dve.tensor_copy(out=wfg[:, 0:nb, :], in_=wfull[:, ds(g * GB, nb), :]).then_inc(wfg_done, 1)
                dve.wait_ge(bias_done, g + 1)
                for j in range(nb):
                    dve.tensor_tensor(out=block_of(R, j), in0=block_of(R, j), in1=ps[4 + j][:, 0:D], op=ALU.add).then_inc(bias_read, 1)
                dve.wait_ge(bias_read, g * GB + nb)
                for e in range(E):
                    for j in range(nb):
                        n = g * (E * GB) + (e * nb + j + 1)
                        dve.wait_ge(down_done, n)
                        if e:
                            dve.wait_ge(down_read, n - nb)
                        dve.scalar_tensor_tensor(out=block_of(R, j), in0=ps[4 + j][:, 0:D],
                                                 scalar=wfull[:, ds(g * GB + j, 1), e:e + 1].rearrange("p a e -> p (a e)"),
                                                 in1=block_of(R, j), op0=ALU.mult, op1=ALU.add).then_inc(down_read, 1)
                dve.wait_ge(down_read, g * (E * GB) + E * nb)
                dve.sem_inc(y_done, 1)

            over_groups(dve, None, 0, experts)


_OUT = ("out", (N, D))
_NAMES = ["x", "src", "dst", "edge_weight", "L0_gnn_weight", "L0_gnn_bias", "L0_mix_Wq", "L0_mix_bq", "L0_mix_Wk",
          "L0_mix_bk", "L0_mix_Wv", "L0_mix_bv", "L0_mix_Wo", "L0_mix_bo", "L0_mix_W1", "L0_mix_b1", "L0_mix_W2",
          "L0_mix_b2", "L0_mix_ln1_g", "L0_mix_ln1_b", "L0_mix_ln2_g", "L0_mix_ln2_b", "L0_ffn_gamma", "L0_ffn_beta",
          "L0_ffn_Wr", "L0_ffn_br", "L0_ffn_W1", "L0_ffn_b1", "L0_ffn_W2", "L0_ffn_b2"]


def kernel(**inputs):
    import numpy as np
    import concourse.bacc as bacc
    from concourse.bass_utils import run_bass_kernel_spmd

    nc = bacc.Bacc("TRN2", target_bir_lowering=False, num_devices=1)
    arrays, args = {}, []
    for name in _NAMES:
        a = np.ascontiguousarray(inputs[name])
        arrays["in_" + name] = a
        args.append(nc.dram_tensor("in_" + name, a.shape, mybir.dt.from_np(a.dtype), kind="ExternalInput").ap())
    out = nc.dram_tensor(_OUT[0], _OUT[1], F32, kind="ExternalOutput").ap()
    program(nc, *args, out)
    result = run_bass_kernel_spmd(nc, [arrays], core_ids=[0])
    return result.results[0][_OUT[0]]
```

```python
import concourse.bass as bass
from concourse import mybir
from contextlib import ExitStack

F32 = mybir.dt.float32
F32R = mybir.dt.float32r
I32 = mybir.dt.int32
U32 = mybir.dt.uint32
ALU = mybir.AluOpType
ACT = mybir.ActivationFunctionType
ds = bass.ds

P = 128
N = 6250
NE = 200000
D = 256
KC = D // P
NH = 8
DH = D // NH
FF = 1024
FC = FF // P
E = 8
H = 512
HC = H // P
EPS = 1e-5

NB = -(-N // P)
LASTN = N - (NB - 1) * P
GB = 4
FULL = NB // GB
assert NB == FULL * GB + 1

EC = -(-NE // P)
TAILE = NE - (P - 1) * EC
SH = 8
SCAT_STEPS = -(-EC // (2 * SH))
ECP = SCAT_STEPS * 2 * SH

GT = 4
GS = GT * P
NG = (P * EC + GS * NB) // GS
HALF_G = 2
GATHER_STEPS = -(-NG // (2 * HALF_G))
NG = GATHER_STEPS * 2 * HALF_G
NT = NG * GT
HT = HALF_G * GT
CARRY = 2 * HALF_G
ZERO_DMAS = 16
STATB = 7
assert NB % STATB == 0


def wait(eng, sem, value, passed=None):
    eng.wait_ge(sem, value)


def wait_apart(eng, sem, value, passed):
    eng.wait_ge(sem, value)
    eng.sem_inc(passed, 1)


class Chain:

    def __init__(self, eng, sem, passed=None):
        self.eng, self.sem, self.base, self.off, self.k, self.passed = eng, sem, 0, 0, 0, passed

    def __call__(self, ins, apart=False):
        self.k += 1
        ins.then_inc(self.sem, 1)
        (wait_apart if apart else wait)(self.eng, self.sem, self.off + (self.base + self.k), self.passed)

    def turn(self, i, per):
        self.base, self.off, self.k = self.base + self.k, i * per, 0

    def end_turn(self, per):
        assert self.k == per, (self.k, per)

    def after(self, turns, per):
        self.base, self.off, self.k = self.base + turns * per, 0, 0


def over_groups(eng, chain, per, body):
    if chain is not None:
        chain.turn(0, 0)
    with eng.Fori(0, FULL) as g:
        if chain is not None:
            chain.off, chain.k = g * per, 0
        body(g, GB)
        if chain is not None:
            chain.end_turn(per)
    if chain is not None:
        chain.after(FULL, per)
    body(FULL, 1)


LO_CREDIT, GELU_CREDIT, DOWN_CREDIT, READ_CREDIT = 2, 1, 2 * GB, GB
PREPARE_SEQ = 4 + 2 + 3 + 4 + 4


def over_pairs(eng, chain, per, body):
    assert FULL % 2 == 0
    if chain is not None:
        chain.turn(0, 0)
    with eng.Fori(0, FULL // 2 - 1) as i:
        if chain is not None:
            chain.off, chain.k = i * per, 0
        over_pairs.turn = i
        for k in range(2):
            body(i * 2 + k, k, GB, GB)
        if chain is not None:
            chain.end_turn(per)
    if chain is not None:
        chain.after(FULL // 2 - 1, per)
    body(FULL - 2, 0, GB, GB)
    body(FULL - 1, 1, GB, 1)
    body(FULL, 0, 1, 0)


def program(nc, x, src, dst, edge_weight, gnn_w, gnn_b, Wq, bq, Wk, bk, Wv, bv, Wo, bo,
            W1, b1, W2, b2, ln1_g, ln1_b, ln2_g, ln2_b, gamma, beta, Wr, br, eW1, eb1, eW2, eb2, out):
    support = nc.dram_tensor("support", (NB * P, D), F32).ap()
    slots = nc.dram_tensor("slots", (P * NT + (ECP - EC) * P, 4), F32).ap()
    xnb = nc.dram_tensor("xnb", (NB * P, D), F32).ap()
    resid = nc.dram_tensor("resid", (NB * P, D), F32).ap()
    agg = nc.dram_tensor("agg", ((NB + NG) * P, D), F32).ap()

    ctx = ExitStack()
    with ctx:
        def sem(name):
            return ctx.enter_context(nc.semaphore(name))

        def alloc(stack, name, shape, dt=F32):
            return stack.enter_context(nc.sbuf_tensor(name, shape, dt))

        ident = alloc(ctx, "ident", [P, P])
        iota_row = alloc(ctx, "iota_row", [P, P])
        ones = alloc(ctx, "ones", [P, P])
        eps_col = alloc(ctx, "eps_col", [P, 1])
        ps = [ctx.enter_context(nc.psum_tensor(f"ps{i}", [P, 512], F32)) for i in range(8)]

        early = ExitStack()
        R = alloc(early, "R", [P, NB, D])
        mv = alloc(early, "mv", [P, NB, 2])
        rstd = alloc(early, "rstd", [P, NB])
        rec = alloc(early, "rec", [P, ECP, 4])
        pos_i = alloc(early, "pos_i", [P, ECP], I32)
        cnt = alloc(early, "cnt", [P, NB])
        base = alloc(early, "base", [P, NB])
        prefix = alloc(early, "prefix", [P, NB])
        gcount = alloc(early, "gcount", [P, NB])
        gint = alloc(early, "gint", [P, NB], I32)
        gcol = alloc(early, "gcol", [P, 4])
        gcol_i = alloc(early, "gcol_i", [P, 1], I32)
        iota_g = alloc(early, "iota_g", [P, NG])
        keep = alloc(early, "keep", [P, NG])
        dest_f = alloc(early, "dest_f", [P, NG])
        dest_i = alloc(early, "dest_i", [P, NG], I32)
        tri = alloc(early, "tri", [P, P])
        blockones = alloc(early, "blockones", [P, P])
        zeros = alloc(early, "zeros", [P, NT * 4 // ZERO_DMAS])
        st_rec = [alloc(early, f"st_rec{h}", [P, SH, 4]) for h in range(2)]
        st_pos = [alloc(early, f"st_pos{h}", [P, SH], I32) for h in range(2)]
        st_tab = [alloc(early, f"st_tab{h}", [P, HT, 4]) for h in range(2)]
        big = alloc(early, "big", [P, 2, HT, D])
        rows = [big[:, h, :, :] for h in range(2)]
        uT = big[:, :, :, :].rearrange("p h t d -> p (h t d)").rearrange("p (f t) -> p f t", f=FC)
        mid = alloc(early, "mid", [P, 2, HT * P])
        hot = [mid[:, h, :].rearrange("p (t n) -> p t n", t=HT) for h in range(2)]
        xn = mid[:, 0, :].rearrange("p (t d) -> p t d", t=GB)
        xnT = mid[:, 1, :].rearrange("p (c t) -> p c t", c=KC)
        carry = alloc(early, "carry", [P, CARRY, D])

        wg_sb = alloc(early, "wg_sb", [P, KC, D])
        wkv_sb = alloc(early, "wkv_sb", [P, KC, 2 * D])
        wq_sb = alloc(early, "wq_sb", [P, KC, D])
        wo_sb = alloc(early, "wo_sb", [P, KC, D])
        w1_sb = alloc(early, "w1_sb", [P, KC, FF])
        w2_sb = alloc(early, "w2_sb", [P, FC, D])
        bkv_b = alloc(early, "bkv_b", [P, 2 * D])
        row_b = alloc(early, "row_b", [P, 7, D])
        bq_col = alloc(early, "bq_col", [P, KC])
        b1_col = alloc(early, "b1_col", [P, FC])
        kraw = alloc(early, "kraw", [P, 2, D])
        kneg = alloc(early, "kneg", [P, 2, D])
        kphi = alloc(early, "kphi", [P, 2, D])
        vaug = alloc(early, "vaug", [P, 2, KC, P + 4])
        sup_sb = alloc(early, "sup_sb", [P, GB, D])
        kvbd = alloc(early, "kvbd", [P, KC, P])
        ksum = alloc(early, "ksum", [P, KC])
        ksel = alloc(early, "ksel", [P, KC, P])
        stats = alloc(early, "stats", [P, STATB, 6])
        smv = alloc(early, "smv", [P, STATB, 2])
        gmv = alloc(early, "gmv", [P, GB, 2])
        grs = alloc(early, "grs", [P, GB])
        edge = ExitStack()
        hi = alloc(edge, "hi", [P, EC])
        ea = alloc(edge, "ea", [P, EC])
        eb = alloc(edge, "eb", [P, EC])
        ec = alloc(edge, "ec", [P, EC])
        gflags = ea[:, 0:3 * NG].rearrange("p (k g) -> p k g", k=3)
        edge.close()
        qneg = alloc(early, "qneg", [P, KC, GB * P])
        qphi = alloc(early, "qphi", [P, KC, GB * P])
        attnT = alloc(early, "attnT", [P, KC, GB * P])
        h1 = alloc(early, "h1", [P, GB, D])
        tmp = alloc(early, "tmp", [P, GB, D])
        hT = alloc(early, "hT", [P, KC, GB * P])
        early.close()

        late = ExitStack()
        up_w = [alloc(late, f"up_w{k}", [P, E, KC, H], F32R) for k in range(2)]
        down_w = [alloc(late, f"down_w{k}", [P, E, HC, D], F32R) for k in range(2)]
        hid = alloc(late, "hid", [P, 2, GB * P])
        hid_s = [alloc(late, f"hid_s{k}", [P, 2, HC, GB * P], F32R) for k in range(2)]
        z_s = [alloc(late, f"z_s{k}", [P, 2, KC, GB * P], F32R) for k in range(2)]
        work = alloc(late, "work", [P, 4, GB * D])
        y = [work[:, k, :].rearrange("p (t d) -> p t d", d=D) for k in range(2)]
        ag = work[:, 2, :].rearrange("p (t d) -> p t d", d=D)
        xb = work[:, 3, :].rearrange("p (t d) -> p t d", d=D)
        router_f = alloc(late, "router_f", [P, KC, E])
        router_w = [alloc(late, f"router_w{k}", [P, KC, E], F32R) for k in range(2)]
        eb1_col = alloc(late, "eb1_col", [P, E * HC])
        eb2_sb = alloc(late, "eb2_sb", [E, D])
        br_b = alloc(late, "br_b", [P, E])
        lrow_b = alloc(late, "lrow_b", [P, 2, D])
        lstats = alloc(late, "lstats", [P, GB, 6])
        lmv = alloc(late, "lmv", [P, GB, 2])
        lrs = alloc(late, "lrs", [P, GB])
        logit = alloc(late, "logit", [P, GB, E])
        top = alloc(late, "top", [P, GB, 8])
        topi = alloc(late, "topi", [P, GB, 8], U32)
        topf = alloc(late, "topf", [P, GB, 2])
        gw = alloc(late, "gw", [P, GB, 4])
        wfull = [alloc(late, f"wfull{k}", [P, GB, E]) for k in range(2)]
        wtmp = alloc(late, "wtmp", [P, GB, E])
        wfT = alloc(late, "wfT", [E, GB * P])
        late.close()

        edges_in = sem("edges_in")
        x_in = sem("x_in")
        mixw_in = sem("mixw_in")
        slots_zero = sem("slots_zero")
        consts = sem("consts")
        pool_seq = sem("pool_seq")
        dve_seq = sem("dve_seq")
        pool_passed = sem("pool_passed")
        dve_passed = sem("dve_passed")
        act_seq = sem("act_seq")
        r_ready = sem("r_ready")
        e_ready = sem("e_ready")
        z_ready = sem("z_ready")
        counts_done = sem("counts_done")
        sums_ready = sem("sums_ready")
        gb_done = sem("gb_done")
        sg_ready = sem("sg_ready")
        flags_done = sem("flags_done")
        flags_summed = sem("flags_summed")
        pos_done = sem("pos_done")
        dest_done = sem("dest_done")
        staged = [sem(f"staged{h}") for h in range(2)]
        scattered = [sem(f"scattered{h}") for h in range(2)]
        var_done = sem("var_done")
        std_done = sem("std_done")
        xn_done = sem("xn_done")
        tr_done = sem("tr_done")
        trc_done = sem("trc_done")
        kv_done = sem("kv_done")
        kv_read = sem("kv_read")
        kneg_done = sem("kneg_done")
        kexp_done = sem("kexp_done")
        kphi_done = sem("kphi_done")
        acc_done = sem("acc_done")
        sup_done = sem("sup_done")
        sup_read = sem("sup_read")
        sup_stored = sem("sup_stored")
        kvacc_done = sem("kvacc_done")
        kvbd_done = sem("kvbd_done")
        xn2_done = sem("xn2_done")
        tr2_done = sem("tr2_done")
        trc2_done = sem("trc2_done")
        q_done = sem("q_done")
        qneg_done = sem("qneg_done")
        qexp_done = sem("qexp_done")
        qphi_done = sem("qphi_done")
        att_done = sem("att_done")
        attn_done = sem("attn_done")
        wo_done = sem("wo_done")
        var1_done = sem("var1_done")
        std1_done = sem("std1_done")
        h1_done = sem("h1_done")
        trh_done = sem("trh_done")
        trhc_done = sem("trhc_done")
        ff1_done = sem("ff1_done")
        relu_done = sem("relu_done")
        ff2_done = sem("ff2_done")
        var2_done = sem("var2_done")
        std2_done = sem("std2_done")
        mix_done = sem("mix_done")
        tab_in = [sem(f"tab_in{h}") for h in range(2)]
        gathered = [sem(f"gathered{h}") for h in range(2)]
        hot_done = [sem(f"hot_done{h}") for h in range(2)]
        summed = [sem(f"summed{h}") for h in range(2)]
        carried = sem("carried")
        agg_stored = [sem(f"agg_stored{c}") for c in range(CARRY)]
        xnb_ready = sem("xnb_ready")
        xnb_stored = sem("xnb_stored")
        resid_stored = sem("resid_stored")
        late_in = sem("late_in")
        stage_in = [sem(f"stage_in{k}") for k in range(2)]
        whi_done = sem("whi_done")
        wlo_done = sem("wlo_done")
        group_in = [sem(f"group_in{k}") for k in range(2)]
        var_t = sem("var_t")
        std_t = sem("std_t")
        z_done = sem("z_done")
        zt_done = sem("zt_done")
        zhi_done = sem("zhi_done")
        zlo_done = sem("zlo_done")
        logit_done = sem("logit_done")
        gap_done = sem("gap_done")
        exp_done = sem("exp_done")
        wfull_done = sem("wfull_done")
        wft_done = sem("wft_done")
        wftc_done = sem("wftc_done")
        bias_done = sem("bias_done")
        bias_read = sem("bias_read")
        up_done = sem("up_done")
        gelu_done = sem("gelu_done")
        hi_done = sem("hi_done")
        lo_done = sem("lo_done")
        down_done = sem("down_done")
        down_read = sem("down_read")
        out_stored = [sem(f"out_stored{k}") for k in range(2)]

        MIXW_DMAS = 18
        LATE_DMAS = 6

        block = ctx.enter_context(nc.Block())

        @block.sync
        def _(sp):
            split = (P - 1) * EC
            sp.wait_ge(e_ready, 1)
            for buf, a in ((eb[:, :].bitcast(I32), src), (ea[:, :].bitcast(I32), dst), (ec[:, :], edge_weight)):
                sp.dma_start(buf[0:P - 1, :], a[0:split].rearrange("(p j) -> p j", p=P - 1)).then_inc(edges_in, 16)
                sp.dma_start(buf[P - 1:P, 0:TAILE], a[split:NE].rearrange("(p j) -> p j", p=1)).then_inc(edges_in, 16)
            sp.wait_ge(r_ready, 1)
            sp.dma_start(R[:, 0:NB - 1, :], x[0:(NB - 1) * P, :].rearrange("(t p) d -> p t d", p=P)).then_inc(x_in, 16)
            sp.dma_start(R[0:LASTN, NB - 1, :], x[(NB - 1) * P:N, :]).then_inc(x_in, 16)
            for w, a in ((wg_sb[:, :, :], gnn_w), (wkv_sb[:, :, 0:D], Wk), (wkv_sb[:, :, D:2 * D], Wv),
                         (wq_sb[:, :, :], Wq), (wo_sb[:, :, :], Wo), (w1_sb[:, :, :], W1), (w2_sb[:, :, :], W2)):
                sp.dma_start(w, a.rearrange("(c p) n -> p c n", p=P)).then_inc(mixw_in, 16)
            for n, a in enumerate((bo, b2, ln1_g, ln1_b, ln2_g, ln2_b, gnn_b)):
                sp.dma_start(row_b[:, n, :], a.partition_broadcast(P)).then_inc(mixw_in, 16)
            sp.dma_start(bkv_b[:, 0:D], bk.partition_broadcast(P)).then_inc(mixw_in, 16)
            sp.dma_start(bkv_b[:, D:2 * D], bv.partition_broadcast(P)).then_inc(mixw_in, 16)
            with nc.allow_non_contiguous_dma(reason="bias columns, a few kilobytes"):
                sp.dma_start(bq_col[:, :], bq.rearrange("(c p) -> p c", p=P)).then_inc(mixw_in, 16)
                sp.dma_start(b1_col[:, :], b1.rearrange("(c p) -> p c", p=P)).then_inc(mixw_in, 16)

            sp.wait_ge(pos_done, 1)

            def stage(it, h):
                col = it * (2 * SH) + h * SH
                sp.dma_start(st_rec[h][:, :, :], rec[:, ds(col, SH), :]).then_inc(staged[h], 16)
                sp.dma_start(st_pos[h][:, :], pos_i[:, ds(col, SH)]).then_inc(staged[h], 16)

            for h in range(2):
                stage(0, h)
            with sp.Fori(1, SCAT_STEPS) as it:
                for h in range(2):
                    sp.wait_ge(scattered[h], it * (16 * SH))
                    stage(it, h)
            for h in range(2):
                sp.wait_ge(scattered[h], SCAT_STEPS * 16 * SH)

            table = slots[0:P * NT, :].rearrange("(p t) c -> p t c", p=P)

            def load_slots(it, h):
                sp.dma_start(st_tab[h][:, :, :], table[:, ds(it * (2 * HT) + h * HT, HT), :]).then_inc(tab_in[h], 16)

            for h in range(2):
                load_slots(0, h)
            with sp.Fori(1, GATHER_STEPS) as it:
                for h in range(2):
                    sp.wait_ge(gathered[h], it * (16 * HT))
                    sp.wait_ge(hot_done[h], it)
                    load_slots(it, h)

            sp.wait_ge(carried, NG)
            for h in range(2):
                sp.wait_ge(gathered[h], GATHER_STEPS * 16 * HT)
            for c in range(CARRY):
                sp.wait_ge(agg_stored[c], NG // CARRY * 16)
            sp.wait_ge(resid_stored, 16 * (FULL + 1))
            sp.wait_ge(xnb_stored, 16 * (FULL + 1))
            for n, a in enumerate((gamma, beta)):
                sp.dma_start(lrow_b[:, n, :], a.partition_broadcast(P)).then_inc(late_in, 16)
            sp.dma_start(br_b[:, :], br.partition_broadcast(P)).then_inc(late_in, 16)
            sp.dma_start(eb2_sb[:, :], eb2).then_inc(late_in, 16)
            sp.dma_start(router_f[:, :, :], Wr.rearrange("(c p) n -> p c n", p=P)).then_inc(late_in, 16)
            with nc.allow_non_contiguous_dma(reason="bias columns, a few kilobytes"):
                sp.dma_start(eb1_col[:, :], eb1.rearrange("e (c p) -> p (e c)", p=P)).then_inc(late_in, 16)
            for e in range(E):
                if e >= 2:
                    sp.wait_ge(wlo_done, 2 * (e - 1) + 1)
                sp.dma_start(work[:, 2 * (e % 2), :].rearrange("p (c n) -> p c n", c=KC),
                             eW1[e, :, :].rearrange("(c p) n -> p c n", p=P)).then_inc(stage_in[e % 2], 16)
                sp.dma_start(work[:, 2 * (e % 2) + 1, :].rearrange("p (c n) -> p c n", c=HC),
                             eW2[e, :, :].rearrange("(c p) n -> p c n", p=P)).then_inc(stage_in[e % 2], 16)
            sp.wait_ge(wlo_done, 2 * E + 1)

            def store_group(g, k, nb):
                sp.wait_ge(down_read, g * (E * GB) + (E * nb + READ_CREDIT))
                if nb == GB:
                    sp.dma_start(out[ds(g * (GB * P), GB * P), :].rearrange("(t p) d -> p t d", p=P),
                                 y[k]).then_inc(out_stored[k], 16)
                else:
                    sp.dma_start(out[g * (GB * P):N, :], y[k][0:LASTN, 0, :]).then_inc(out_stored[k], 16)

            def load_group(n, k, nb, before):
                row = n * (GB * P)
                if before:
                    sp.wait_ge(zt_done, n * KC)
                for to, a in ((ag, agg), (xb, xnb)):
                    sp.dma_start(to[:, 0:nb, :], a[ds(row, nb * P), :].rearrange("(t p) d -> p t d", p=P)).then_inc(group_in[k], 16)
                if before == 2:
                    sp.wait_ge(out_stored[k], (n // 2 if isinstance(n, int) else before_pairs[0]) * 16)
                sp.dma_start(y[k][:, 0:nb, :], resid[ds(row, nb * P), :].rearrange("(t p) d -> p t d", p=P)).then_inc(group_in[k], 16)

            before_pairs = [0]
            load_group(0, 0, GB, 0)
            load_group(1, 1, GB, 1)
            store_group(0, 0, GB)
            with sp.Fori(1, FULL // 2) as i:
                before_pairs[0] = i
                load_group(i * 2, 0, GB, 2)
                store_group(i * 2 - 1, 1, GB)
                load_group(i * 2 + 1, 1, GB, 2)
                store_group(i * 2, 0, GB)
            load_group(FULL, 0, 1, 2)
            store_group(FULL - 1, 1, GB)
            store_group(FULL, 0, 1)
            sp.wait_ge(out_stored[0], 16 * (FULL // 2 + 1))
            sp.wait_ge(out_stored[1], 16 * (FULL // 2))

        @block.gpsimd
        def _(pool):
            seq = Chain(pool, pool_seq)
            seq(pool.memset(ones[:, :], 1.0))
            seq(pool.iota(iota_row[:, :], [[1, P]], base=0, channel_multiplier=0, allow_small_or_imprecise_dtypes=True))
            seq(pool.iota(iota_g[:, :], [[1, NG]], base=0, channel_multiplier=0, allow_small_or_imprecise_dtypes=True))
            seq(pool.affine_select(out=ident[:, :], in_=ones[:, :], compare_op=ALU.is_equal, fill=0.0, base=0,
                                   pattern=[[-1, P]], channel_multiplier=1))
            seq(pool.affine_select(out=tri[:, :], in_=ones[:, :], compare_op=ALU.is_gt, fill=0.0, base=0,
                                   pattern=[[1, P]], channel_multiplier=-1))
            bv3 = blockones[:, :].rearrange("p (h d) -> p h d", d=DH)
            seq(pool.affine_select(out=bv3, in_=ones[:, :].rearrange("p (h d) -> p h d", d=DH), compare_op=ALU.is_ge,
                                   fill=0.0, base=0, pattern=[[-DH, P // DH], [0, DH]], channel_multiplier=1))
            pool.affine_select(out=bv3, in_=bv3, compare_op=ALU.is_ge, fill=0.0, base=DH - 1,
                               pattern=[[DH, P // DH], [0, DH]], channel_multiplier=-1).then_inc(consts, 1)
            if ECP > EC:
                pool.iota(pos_i[:, EC:ECP], [[P, ECP - EC]], base=P * NT, channel_multiplier=1).then_inc(consts, 1)

            pool.wait_ge(slots_zero, 16 * ZERO_DMAS)
            with pool.Fori(0, SCAT_STEPS) as it:
                for h in range(2):
                    wait_apart(pool, staged[h], it * 32 + 32, pool_passed)
                    for j in range(SH):
                        pool.indirect_dma_start(
                            out=slots, out_offset=bass.IndirectOffsetOnAxis(ap=st_pos[h][:, j:j + 1], axis=0),
                            in_=st_rec[h][:, j, :], in_offset=None).then_inc(scattered[h], 16)

            pool.wait_ge(sup_stored, 16 * (FULL + 1))

            def gather(it, h):
                wait_apart(pool, tab_in[h], it * 16 + 16, pool_passed)
                for j in range(HT):
                    pool.indirect_dma_start(
                        out=rows[h][:, j, :], out_offset=None, in_=support,
                        in_offset=bass.IndirectOffsetOnAxis(ap=st_tab[h][:, j, 0:1].bitcast(I32), axis=0)
                    ).then_inc(gathered[h], 16)

            pool.wait_ge(mix_done, FULL + 1)
            for h in range(2):
                gather(0, h)
            with pool.Fori(1, GATHER_STEPS) as it:
                for h in range(2):
                    pool.wait_ge(summed[h], it * HALF_G)
                    gather(it, h)

        @block.tensor
        def _(pe):
            pe.wait_ge(consts, 1)
            pe.wait_ge(counts_done, 1)
            pe.matmul(ps[6][:, 0:NB], lhsT=tri[:, :], rhs=cnt[:, :], start=True, stop=True)
            pe.matmul(ps[6][:, 64:64 + NB], lhsT=ones[:, :], rhs=cnt[:, :], start=True, stop=True)
            pe.matmul(ps[6][0:NB, 128:129], lhsT=cnt[:, :], rhs=ones[:, 0:1], start=True, stop=True).then_inc(sums_ready, 1)
            pe.wait_ge(gb_done, 1)
            pe.matmul(ps[5][0:NB, 0:1], lhsT=tri[0:NB, 0:NB], rhs=gcol[0:NB, 0:1], start=True, stop=True).then_inc(sg_ready, 1)
            pe.wait_ge(flags_done, 1)
            for k, bank in enumerate((6, 7, 5)):
                last = pe.matmul(ps[bank][:, 0:NG], lhsT=ones[0:NB, :], rhs=gflags[0:NB, k, :], start=True, stop=True)
            last.then_inc(flags_summed, 1)
            pe.wait_ge(dest_done, 1)

            def transposes(nb, source, banks, done):
                for c in range(KC):
                    for j in range(nb):
                        last = pe.transpose(ps[banks[c]][:, j * P:(j + 1) * P], source[:, j, c * P:(c + 1) * P], ident[:, :])
                last.then_inc(done, 1)

            pe.wait_ge(mixw_in, 16 * MIXW_DMAS)
            pe.matmul(ps[5][:, 0:2 * (P + 4)], lhsT=zeros[:, 0:P], rhs=zeros[:, 0:2 * (P + 4)], start=True, stop=False)

            def pass1(g, nb):
                rowsn = P if nb == GB else LASTN
                pe.wait_ge(xn_done, g + 1)
                transposes(nb, xn, (0, 1), tr_done)
                pe.wait_ge(trc_done, g + 1)

                def products(j):
                    if j >= 2:
                        pe.wait_ge(kv_read, g * GB + (j - 1))
                        pe.wait_ge(sup_read, g * GB + (j - 1))
                    for c in range(KC):
                        last = pe.matmul(ps[2 + j % 2][:, :], lhsT=xnT[:, c, j * P:(j + 1) * P], rhs=wkv_sb[:, c, :],
                                         start=(c == 0), stop=(c == KC - 1))
                    last.then_inc(kv_done, 1)
                    for c in range(KC):
                        last = pe.matmul(ps[4 + j % 2 * 2][:, 0:D], lhsT=xnT[:, c, j * P:(j + 1) * P],
                                         rhs=wg_sb[:, c, :], start=(c == 0), stop=(c == KC - 1))
                    last.then_inc(sup_done, 1)

                def accumulate(j):
                    pe.wait_ge(kphi_done, g * GB + (j + 1))
                    for c in range(KC):
                        last = pe.matmul(ps[5][:, c * (P + 4):c * (P + 4) + P + 1], lhsT=kphi[0:rowsn, j % 2, c * P:(c + 1) * P],
                                         rhs=vaug[0:rowsn, j % 2, c, 0:P + 1], start=False, stop=False, skip_group_check=True)
                    last.then_inc(acc_done, 1)

                for j in range(nb):
                    products(j)
                    if j:
                        accumulate(j - 1)
                accumulate(nb - 1)

            over_groups(pe, None, 0, pass1)
            pe.matmul(ps[5][:, 0:2 * (P + 4)], lhsT=zeros[:, 0:P], rhs=zeros[:, 0:2 * (P + 4)], start=False, stop=True).then_inc(kvacc_done, 1)

            pe.wait_ge(kvbd_done, 1)

            def pass2(g, nb):
                T = nb * P
                pe.wait_ge(xn2_done, g + 1)
                transposes(nb, xn, (0, 1), tr2_done)
                pe.wait_ge(trc2_done, g + 1)
                for hh in range(KC):
                    for c in range(KC):
                        last = pe.matmul(ps[2 + hh][:, 0:T], lhsT=wq_sb[:, c, hh * P:(hh + 1) * P], rhs=xnT[:, c, 0:T],
                                         start=(c == 0), stop=(c == KC - 1))
                last.then_inc(q_done, 1)
                pe.wait_ge(qphi_done, g + 1)
                for hh in range(KC):
                    pe.matmul(ps[4 + hh][:, 0:T], lhsT=kvbd[:, hh, :], rhs=qphi[:, hh, 0:T], start=True, stop=True)
                    last = pe.matmul(ps[6 + hh][:, 0:T], lhsT=ksel[:, hh, :], rhs=qphi[:, hh, 0:T], start=True, stop=True)
                last.then_inc(att_done, 1)
                pe.wait_ge(attn_done, g + 1)
                for j in range(nb):
                    for c in range(KC):
                        last = pe.matmul(ps[2 + j // 2][:, (j % 2) * D:(j % 2 + 1) * D], lhsT=attnT[:, c, j * P:(j + 1) * P],
                                         rhs=wo_sb[:, c, :], start=(c == 0), stop=(c == KC - 1))
                last.then_inc(wo_done, 1)
                pe.wait_ge(h1_done, g + 1)
                transposes(nb, h1, (0, 1), trh_done)
                pe.wait_ge(trhc_done, g + 1)
                for f in range(FC):
                    if f >= 2:
                        pe.wait_ge(relu_done, g * FC + (f - 1))
                    for c in range(KC):
                        last = pe.matmul(ps[4 + f % 2][:, 0:T], lhsT=w1_sb[:, c, f * P:(f + 1) * P], rhs=hT[:, c, 0:T],
                                         start=(c == 0), stop=(c == KC - 1))
                    last.then_inc(ff1_done, 1)
                pe.wait_ge(relu_done, g * FC + FC)
                for j in range(nb):
                    for f in range(FC):
                        last = pe.matmul(ps[6 + j // 2][:, (j % 2) * D:(j % 2 + 1) * D], lhsT=uT[:, f, j * P:(j + 1) * P],
                                         rhs=w2_sb[:, f, :], start=(f == 0), stop=(f == FC - 1))
                last.then_inc(ff2_done, 1)

            over_groups(pe, None, 0, pass2)

            def sum_half(it, h, wait_free):
                pe.wait_ge(hot_done[h], it + 1)
                pe.wait_ge(gathered[h], it * (16 * HT) + 16 * HT)
                for q in range(HALF_G):
                    c = h * HALF_G + q
                    if wait_free:
                        pe.wait_ge(carried, it * CARRY + (c + 1 - CARRY))
                    for t in range(GT):
                        k = q * GT + t
                        last = pe.matmul(ps[c][:, 0:D], lhsT=hot[h][:, k, :], rhs=rows[h][:, k, :],
                                         start=(t == 0), stop=(t == GT - 1))
                    last.then_inc(summed[h], 1)

            for h in range(2):
                sum_half(0, h, False)
            with pe.Fori(1, GATHER_STEPS) as it:
                for h in range(2):
                    sum_half(it, h, True)

            pe.wait_ge(late_in, 16 * LATE_DMAS)

            def split_product(to, a, b, first=True, last=True):
                for n, (s, m) in enumerate(((0, 0), (0, 1), (1, 0))):
                    ins = pe.matmul(to, lhsT=a(s), rhs=b(m), start=(first and n == 0), stop=(last and n == 2))
                return ins

            def prepare(slot, n, k, nb):
                if slot in (2, 3):
                    c = slot - 2
                    pe.wait_ge(z_done, n + 1)
                    if c:
                        pe.wait_ge(zlo_done, n * KC + 1)
                    for j in range(nb):
                        last = pe.transpose(ps[3][:, j * P:(j + 1) * P], ag[:, j, c * P:(c + 1) * P], ident[:, :])
                    last.then_inc(zt_done, 1)
                if slot == 4:
                    pe.wait_ge(zlo_done, n * KC + KC)
                    pe.wait_ge(wlo_done, 2 * E + 1)
                    for j in range(nb):
                        for c in range(KC):
                            last = split_product(ps[3][:, j * E:(j + 1) * E], lambda s: z_s[s][:, k, c, j * P:(j + 1) * P],
                                                 lambda m: router_w[m][:, c, :], c == 0, c == KC - 1)
                    last.then_inc(logit_done, 1)
                if slot == 6:
                    pe.wait_ge(wfull_done, n + 1)
                    for j in range(nb):
                        last = pe.transpose(ps[3][0:E, j * P:(j + 1) * P], wfull[k][:, j, :], ident[:, :])
                    last.then_inc(wft_done, 1)
                if slot in (7, 8):
                    h = slot - 7
                    if h == 0:
                        pe.wait_ge(wftc_done, n + 1)
                    else:
                        pe.wait_ge(bias_read, n * 2 + 1)
                    for j in range(2 * h, min(nb, 2 * h + 2)):
                        last = pe.matmul(ps[3][:, (j % 2) * D:(j % 2 + 1) * D], lhsT=wfT[:, j * P:(j + 1) * P],
                                         rhs=eb2_sb[:, :], start=True, stop=True)
                    if nb > 2 * h:
                        last.then_inc(bias_done, 1)

            def up(g, e, k, nb):
                T = nb * P
                for f in range(HC):
                    c = e * HC + f
                    if f == 0:
                        pe.wait_ge(gelu_done, g * (E * HC) + (c + GELU_CREDIT))
                    if f == 3:
                        pe.wait_ge(gelu_done, g * (E * HC) + (c - 2 + GELU_CREDIT))
                    for kc in range(KC):
                        last = split_product(ps[f % 3][:, 0:T], lambda s: up_w[s][:, e, kc, f * P:(f + 1) * P],
                                             lambda m: z_s[m][:, k, kc, 0:T], kc == 0, kc == KC - 1)
                    last.then_inc(up_done, 1)

            def down(g, e, nb):
                pe.wait_ge(lo_done, g * (E * HC) + (e * HC + HC + LO_CREDIT))
                for j in range(nb):
                    read = (e - 1) * nb + j + 1 if e else j + 1 - GB
                    pe.wait_ge(down_read, g * (E * GB) + (read + READ_CREDIT))
                    for f in range(HC):
                        last = split_product(ps[4 + j][:, 0:D], lambda s: hid_s[s][:, e % 2, f, j * P:(j + 1) * P],
                                             lambda m: down_w[m][:, e, f, :], f == 0, f == HC - 1)
                    last.then_inc(down_done, 1)

            def group(g, k, nb, nb_next):
                for e in range(E):
                    if e + 1 < E:
                        up(g, e + 1, k, nb)
                    elif nb_next:
                        up(g + 1, 0, 1 - k, nb_next)
                    down(g, e, nb)
                    if e == 0:
                        prepare(8, g, k, nb)
                    if nb_next:
                        prepare(e, g + 1, 1 - k, nb_next)

            for slot in range(8):
                prepare(slot, 0, 0, GB)
            pe.wait_ge(wlo_done, 2 * E + 1)
            up(0, 0, 0, GB)
            over_pairs(pe, None, 0, group)

        @block.scalar
        def _(act):
            seq = Chain(act, act_seq)
            act.wait_ge(z_ready, 1)
            for k in range(ZERO_DMAS):
                act.dma_start(slots[0:P * NT, :].rearrange("(p a t) c -> a p (t c)", p=P, a=ZERO_DMAS)[k, :, :],
                              zeros[:, :]).then_inc(slots_zero, 16)
            act.wait_ge(var_done, 1)
            act.activation(rstd[:, :], mv[:, :, 1], ACT.Sqrt, bias=eps_col[:, 0:1]).then_inc(std_done, 1)

            def copy_transposed(g, nb, wait, to, done):
                T = nb * P
                act.wait_ge(wait, g + 1)
                act.activation(to[:, 0, 0:T], ps[0][:, 0:T], ACT.Copy)
                act.activation(to[:, 1, 0:T], ps[1][:, 0:T], ACT.Copy).then_inc(done, 1)

            def pass1(g, nb):
                copy_transposed(g, nb, tr_done, xnT, trc_done)
                for j in range(nb):
                    n = g * GB + (j + 1)
                    act.wait_ge(kneg_done, n)
                    act.activation(kneg[:, j % 2, :], kneg[:, j % 2, :], ACT.Exp).then_inc(kexp_done, 1)
                    act.wait_ge(sup_done, n)
                    act.activation(sup_sb[:, j, :], ps[4 + j % 2 * 2][:, 0:D], ACT.Copy).then_inc(sup_read, 1)
                act.wait_ge(sup_read, g * GB + nb)
                act.dma_start(support[ds(g * (GB * P), nb * P), :].rearrange("(t p) d -> p t d", p=P),
                              sup_sb[:, 0:nb, :]).then_inc(sup_stored, 16)
                act.wait_ge(sup_stored, g * 16 + 16)

            over_groups(act, None, 0, pass1)

            def pass2(g, nb):
                T = nb * P
                copy_transposed(g, nb, tr2_done, xnT, trc2_done)
                act.wait_ge(xnb_ready, g + 1)
                act.dma_start(xnb[ds(g * (GB * P), T), :].rearrange("(t p) d -> p t d", p=P), sup_sb[:, 0:nb, :]).then_inc(xnb_stored, 16)
                for hh in range(KC):
                    act.wait_ge(qneg_done, g * KC + (hh + 1))
                    act.activation(qneg[:, hh, 0:T], qneg[:, hh, 0:T], ACT.Exp).then_inc(qexp_done, 1)
                act.wait_ge(var1_done, g + 1)
                act.activation(grs[:, 0:nb], gmv[:, 0:nb, 1], ACT.Sqrt, bias=eps_col[:, 0:1]).then_inc(std1_done, 1)
                copy_transposed(g, nb, trh_done, hT, trhc_done)
                for f in range(FC):
                    act.wait_ge(ff1_done, g * FC + (f + 1))
                    act.activation(uT[:, f, 0:T], ps[4 + f % 2][:, 0:T], ACT.Relu, bias=b1_col[:, f:f + 1]).then_inc(relu_done, 1)
                act.wait_ge(var2_done, g + 1)
                act.wait_ge(xnb_stored, g * 16 + 16)
                act.activation(grs[:, 0:nb], gmv[:, 0:nb, 1], ACT.Sqrt, bias=eps_col[:, 0:1]).then_inc(std2_done, 1)
                act.wait_ge(mix_done, g + 1)
                act.dma_start(resid[ds(g * (GB * P), T), :].rearrange("(t p) d -> p t d", p=P), h1[:, 0:nb, :]).then_inc(resid_stored, 16)
                act.wait_ge(resid_stored, g * 16 + 16)

            over_groups(act, None, 0, pass2)

            act.wait_ge(dest_done, 1)
            with act.Fori(0, GATHER_STEPS) as it:
                for c in range(CARRY):
                    where = act.value_load(dest_i[0:1, ds(it * CARRY + c, 1)], min_val=0, max_val=NB + NG - 1)
                    act.wait_ge(carried, it * CARRY + (c + 1))
                    act.dma_start(agg[ds(where * P, P), :], carry[:, c, :]).then_inc(agg_stored[c], 16)

            act.wait_ge(late_in, 16 * LATE_DMAS)
            act.activation(router_w[0][:, :, :], router_f[:, :, :], ACT.Copy).then_inc(whi_done, 1)
            for e in range(E):
                act.wait_ge(stage_in[e % 2], 32 * (e // 2 + 1))
                for n, w in enumerate((up_w, down_w)):
                    act.activation(w[0][:, e, :, :].rearrange("p c n -> p (c n)"), work[:, 2 * (e % 2) + n, :],
                                   ACT.Copy).then_inc(whi_done, 1)

            def prepare(slot, n, k, nb):
                T = nb * P
                if slot == 0:
                    act.wait_ge(var_t, n + 1)
                    act.activation(lrs[:, 0:nb], lrs[:, 0:nb], ACT.Sqrt).then_inc(std_t, 1)
                if slot in (2, 3):
                    c = slot - 2
                    act.wait_ge(zt_done, n * KC + (c + 1))
                    act.activation(z_s[0][:, k, c, 0:T], ps[3][:, 0:T], ACT.Copy).then_inc(zhi_done, 1)
                if slot == 5:
                    act.wait_ge(gap_done, n + 1)
                    act.activation(gw[:, 0:nb, 1], gw[:, 0:nb, 0], ACT.Exp).then_inc(exp_done, 1)
                if slot == 6:
                    act.wait_ge(wft_done, n + 1)
                    act.activation(wfT[:, 0:T], ps[3][0:E, 0:T], ACT.Copy).then_inc(wftc_done, 1)

            def hidden(g, e, nb):
                T = nb * P
                for f in range(HC):
                    n = e * HC + f + 1
                    act.wait_ge(up_done, g * (E * HC) + n)
                    act.wait_ge(lo_done, g * (E * HC) + (n - 2 + LO_CREDIT))
                    act.activation(hid[:, f % 2, 0:T], ps[f % 3][:, 0:T], ACT.Gelu,
                                   bias=eb1_col[:, e * HC + f:e * HC + f + 1]).then_inc(gelu_done, 1)
                    if f == 0:
                        used = (e - 1) * nb if e >= 2 else (e - 1) * GB
                        act.wait_ge(down_done, g * (E * GB) + (used + DOWN_CREDIT))
                    act.wait_ge(gelu_done, g * (E * HC) + (n + GELU_CREDIT))
                    act.activation(hid_s[0][:, e % 2, f, 0:T], hid[:, f % 2, 0:T], ACT.Copy).then_inc(hi_done, 1)

            def group(g, k, nb, nb_next):
                for e in range(E):
                    if e + 1 < E:
                        hidden(g, e + 1, nb)
                    elif nb_next:
                        hidden(g + 1, 0, nb_next)
                    if nb_next:
                        prepare(e, g + 1, 1 - k, nb_next)

            for slot in range(8):
                prepare(slot, 0, 0, GB)
            hidden(0, 0, GB)
            over_pairs(act, None, 0, group)

        @block.vector
        def _(dve):
            seq = Chain(dve, dve_seq, dve_passed)
            ebi, eai, eci = eb[:, :].bitcast(I32), ea[:, :].bitcast(I32), ec[:, :].bitcast(I32)
            seq(dve.memset(ebi[:, TAILE:EC], N))
            seq(dve.memset(eai[:, TAILE:EC], 0))
            dve.memset(ec[:, TAILE:EC], 0.0).then_inc(e_ready, 1)
            dve.memset(R[:, NB - 1, :], 0.0).then_inc(r_ready, 1)
            dve.memset(zeros[:, :], 0.0).then_inc(z_ready, 1)
            dve.memset(eps_col[:, :], EPS)
            dve.memset(vaug[:, :, :, P:P + 1], 1.0)
            dve.memset(carry[:, CARRY - 1, :], 0.0)
            seq(dve.memset(rec[:, :, :], 0.0))

            dve.wait_ge(edges_in, 16 * 6)
            dve.tensor_copy(out=rec[:, 0:EC, 0].bitcast(I32), in_=eai)
            seq(dve.tensor_copy(out=rec[:, 0:EC, 2], in_=ec[:, :]))
            dve.tensor_scalar(out=eai, in0=ebi, scalar1=7, scalar2=None, op0=ALU.logical_shift_right)
            seq(dve.tensor_scalar(out=eci, in0=ebi, scalar1=127, scalar2=None, op0=ALU.bitwise_and))
            dve.tensor_copy(out=hi[:, :], in_=eai)
            seq(dve.tensor_copy(out=rec[:, 0:EC, 1], in_=eci))

            dve.wait_ge(consts, 1)
            seq.turn(0, 0)
            with dve.Fori(0, NB) as b:
                seq.off, seq.k = b * 1, 0
                seq(dve.tensor_scalar(out=ea[:, :], in0=hi[:, :], scalar1=iota_row[:, ds(b, 1)], scalar2=None,
                                      op0=ALU.is_equal, op1=ALU.add, accum_out=cnt[:, ds(b, 1)]))
            seq.after(NB, 1)
            dve.sem_inc(counts_done, 1)

            dve.wait_ge(sums_ready, 1)
            def groups_of(count, out_f, out_i):
                seq(dve.tensor_scalar(out=out_i, in0=count, scalar1=float(GS - 1), scalar2=None, op0=ALU.add))
                seq(dve.tensor_scalar(out=out_i, in0=out_i, scalar1=GS.bit_length() - 1, scalar2=None, op0=ALU.logical_shift_right))
                seq(dve.tensor_scalar(out=out_f, in0=out_i, scalar1=1.0, scalar2=None, op0=ALU.max))
            groups_of(ps[6][0:NB, 128:129], gcol[0:NB, 0:1], gcol_i[0:NB, :])
            dve.sem_inc(gb_done, 1)
            groups_of(ps[6][:, 64:64 + NB], gcount[:, :], gint[:, :])
            seq(dve.tensor_tensor_scan(out=prefix[:, :], data0=ones[:, 0:NB], data1=gcount[:, :], initial=0.0,
                                       op0=ALU.mult, op1=ALU.add))
            seq(dve.tensor_tensor(out=prefix[:, :], in0=prefix[:, :], in1=gcount[:, :], op=ALU.subtract))
            seq(dve.tensor_scalar(out=base[:, :], in0=prefix[:, :], scalar1=float(GS), scalar2=-1.0, op0=ALU.mult, op1=ALU.add))
            seq(dve.tensor_tensor(out=base[:, :], in0=base[:, :], in1=ps[6][:, 0:NB], op=ALU.add))

            dve.wait_ge(sg_ready, 1)
            seq(dve.tensor_copy(out=gcol[0:NB, 1:2], in_=ps[5][0:NB, 0:1]))
            seq(dve.tensor_tensor(out=gcol[0:NB, 2:3], in0=gcol[0:NB, 1:2], in1=gcol[0:NB, 0:1], op=ALU.add))
            seq(dve.tensor_scalar(out=gcol[0:NB, 3:4], in0=gcol[0:NB, 2:3], scalar1=-1.0, scalar2=None, op0=ALU.add))
            for k, (col, op) in enumerate(((2, ALU.is_ge), (1, ALU.is_equal), (3, ALU.is_equal))):
                seq(dve.tensor_scalar(out=gflags[0:NB, k, :], in0=iota_g[0:NB, :], scalar1=gcol[0:NB, col:col + 1],
                                      scalar2=None, op0=op))
            dve.sem_inc(flags_done, 1)

            dve.wait_ge(flags_summed, 1)
            seq.turn(0, 0)
            with dve.Fori(0, NB) as b:
                seq.off, seq.k = b * 3, 0
                seq(dve.tensor_scalar(out=ea[:, :], in0=hi[:, :], scalar1=iota_row[:, ds(b, 1)], scalar2=None, op0=ALU.is_equal))
                seq(dve.tensor_tensor_scan(out=ec[:, :], data0=ones[:, 0:1].to_broadcast([P, EC]), data1=ea[:, :],
                                           initial=base[:, ds(b, 1)], op0=ALU.mult, op1=ALU.add), apart=True)
                seq(dve.copy_predicated(eb[:, :], eai, ec[:, :]))
            seq.after(NB, 3)
            seq(dve.tensor_copy(out=eai, in_=eb[:, :]))
            seq(dve.tensor_scalar(out=eci, in0=eai, scalar1=2, scalar2=127, op0=ALU.logical_shift_right, op1=ALU.bitwise_and))
            seq(dve.tensor_scalar(out=eb[:, :], in0=eci, scalar1=float(NT), scalar2=None, op0=ALU.mult))
            seq(dve.tensor_scalar(out=eci, in0=eai, scalar1=9, scalar2=None, op0=ALU.logical_shift_right))
            seq(dve.scalar_tensor_tensor(out=eb[:, :], in0=eci, scalar=float(GT), in1=eb[:, :], op0=ALU.mult, op1=ALU.add))
            seq(dve.tensor_scalar(out=eci, in0=eai, scalar1=3, scalar2=None, op0=ALU.bitwise_and))
            dve.wait_ge(consts, 1 + (ECP > EC))
            dve.tensor_tensor(out=pos_i[:, 0:EC], in0=eci, in1=eb[:, :], op=ALU.add).then_inc(pos_done, 1)

            dve.wait_ge(flags_summed, 1)
            dve.tensor_scalar(out=keep[:, :], in0=ps[7][:, 0:NG], scalar1=-1.0, scalar2=1.0, op0=ALU.mult, op1=ALU.add)
            seq(dve.tensor_scalar(out=iota_g[:, :], in0=iota_g[:, :], scalar1=float(NB), scalar2=None, op0=ALU.add))
            seq(dve.tensor_tensor(out=dest_f[:, :], in0=ps[6][:, 0:NG], in1=iota_g[:, :], op=ALU.subtract))
            seq(dve.tensor_tensor(out=dest_f[:, :], in0=dest_f[:, :], in1=ps[5][:, 0:NG], op=ALU.mult))
            dve.tensor_tensor(out=dest_i[:, :], in0=dest_f[:, :], in1=iota_g[:, :], op=ALU.add).then_inc(dest_done, 1)

            dve.wait_ge(x_in, 32)
            seq.turn(0, 0)
            with dve.Fori(0, NB // STATB) as t:
                seq.off, seq.k = t * 3, 0
                for j in range(STATB):
                    last = dve.bn_stats(out=stats[:, j, :], in_=R[:, ds(t * STATB + j, 1), :].rearrange("p a d -> p (a d)"))
                seq(last, apart=True)
                for j in range(STATB):
                    last = dve.bn_aggr(out=smv[:, j, :], in_=stats[:, j, :])
                seq(last)
                seq(dve.tensor_copy(out=mv[:, ds(t * STATB, STATB), :], in_=smv[:, :, :]))
            seq.after(NB // STATB, 3)
            dve.sem_inc(var_done, 1)
            dve.wait_ge(std_done, 1)
            seq(dve.reciprocal(out=rstd[:, :], in_=rstd[:, :]))

            def normalise(g, nb, to, source, dynamic):
                for j in range(nb):
                    n = g * GB + j
                    s = source[:, ds(n, 1), :].rearrange("p a d -> p (a d)") if dynamic else source[:, j, :]
                    last = dve.tensor_scalar(out=to[:, j, :], in0=s, scalar1=mv[:, ds(n, 1), 0:1].rearrange("p a d -> p (a d)"),
                                             scalar2=rstd[:, ds(n, 1)], op0=ALU.subtract, op1=ALU.mult)
                return last

            dve.wait_ge(mixw_in, 16 * MIXW_DMAS)

            def pass1(g, nb):
                normalise(g, nb, xn, R, True).then_inc(xn_done, 1)
                for j in range(nb):
                    n = g * GB + (j + 1)
                    dve.wait_ge(kv_done, n)
                    if j >= 2:
                        dve.wait_ge(acc_done, g * GB + (j - 1))
                    bank = ps[2 + j % 2]
                    seq(dve.tensor_tensor(out=kraw[:, j % 2, :], in0=bank[:, 0:D], in1=bkv_b[:, 0:D], op=ALU.add))
                    dve.tensor_scalar(out=kneg[:, j % 2, :], in0=kraw[:, j % 2, :], scalar1=0.0, scalar2=None,
                                      op0=ALU.min).then_inc(kneg_done, 1)
                    dve.tensor_tensor(out=vaug[:, j % 2, :, 0:P], in0=bank[:, D:2 * D].rearrange("p (c e) -> p c e", c=KC),
                                      in1=bkv_b[:, D:2 * D].rearrange("p (c e) -> p c e", c=KC), op=ALU.add).then_inc(kv_read, 1)
                    dve.wait_ge(kexp_done, n)
                    dve.scalar_tensor_tensor(out=kphi[:, j % 2, :], in0=kraw[:, j % 2, :], scalar=0.0, in1=kneg[:, j % 2, :],
                                             op0=ALU.max, op1=ALU.add).then_inc(kphi_done, 1)

            over_groups(dve, seq, GB, pass1)

            dve.wait_ge(kvacc_done, 1)
            for c in range(KC):
                o = c * (P + 4)
                dve.tensor_tensor(out=kvbd[:, c, :], in0=ps[5][:, o:o + P], in1=blockones[:, :], op=ALU.mult)
                seq(dve.tensor_copy(out=ksum[:, c:c + 1], in_=ps[5][:, o + P:o + P + 1]))
            for c in range(KC):
                last = dve.tensor_scalar(out=ksel[:, c, :], in0=blockones[:, :], scalar1=ksum[:, c:c + 1], scalar2=None, op0=ALU.mult)
            last.then_inc(kvbd_done, 1)

            def wide(row, nb):
                return row_b[:, row:row + 1, :].to_broadcast([P, nb, D])

            def layer_norm(nb, t, affine, to, var_ready, std_ready, g, s=stats, m=gmv, r=grs):
                for j in range(nb):
                    last = dve.bn_stats(out=s[:, j, :], in_=t[:, j, :])
                seq(last, apart=True)
                for j in range(nb):
                    last = dve.bn_aggr(out=m[:, j, :], in_=s[:, j, :])
                last.then_inc(var_ready, 1)
                dve.wait_ge(std_ready, g + 1)
                seq(dve.reciprocal(out=r[:, 0:nb], in_=r[:, 0:nb]))
                for j in range(nb):
                    if affine is None:
                        last = dve.tensor_scalar(out=to(j), in0=t[:, j, :], scalar1=m[:, j, 0:1], scalar2=r[:, j:j + 1],
                                                 op0=ALU.subtract, op1=ALU.mult)
                    else:
                        last = dve.scalar_tensor_tensor(out=t[:, j, :], in0=t[:, j, :], scalar=m[:, j, 0:1], in1=affine[0],
                                                        op0=ALU.subtract, op1=ALU.mult)
                if affine is not None:
                    seq(last)
                    for j in range(nb):
                        last = dve.scalar_tensor_tensor(out=to(j), in0=t[:, j, :], scalar=r[:, j:j + 1], in1=affine[1],
                                                        op0=ALU.mult, op1=ALU.add)
                return last

            def pass2(g, nb):
                T = nb * P
                normalise(g, nb, xn, R, True).then_inc(xn2_done, 1)
                dve.wait_ge(xn2_done, g + 1)
                dve.tensor_tensor(out=sup_sb[:, 0:nb, :], in0=xn[:, 0:nb, :], in1=wide(6, nb), op=ALU.add).then_inc(xnb_ready, 1)
                dve.wait_ge(q_done, g + 1)
                for hh in range(KC):
                    dve.tensor_scalar(out=qneg[:, hh, 0:T], in0=ps[2 + hh][:, 0:T], scalar1=bq_col[:, hh:hh + 1], scalar2=0.0,
                                      op0=ALU.add, op1=ALU.min).then_inc(qneg_done, 1)
                    last = dve.tensor_scalar(out=qphi[:, hh, 0:T], in0=ps[2 + hh][:, 0:T], scalar1=bq_col[:, hh:hh + 1], scalar2=0.0,
                                             op0=ALU.add, op1=ALU.max)
                seq(last)
                for hh in range(KC):
                    dve.wait_ge(qexp_done, g * KC + (hh + 1))
                    last = dve.tensor_tensor(out=qphi[:, hh, 0:T], in0=qphi[:, hh, 0:T], in1=qneg[:, hh, 0:T], op=ALU.add)
                last.then_inc(qphi_done, 1)
                dve.wait_ge(att_done, g + 1)
                for hh in range(KC):
                    last = dve.tensor_scalar(out=attnT[:, hh, 0:T], in0=ps[6 + hh][:, 0:T], scalar1=1e-6, scalar2=None, op0=ALU.add)
                seq(last)
                for hh in range(KC):
                    last = dve.reciprocal(out=attnT[:, hh, 0:T], in_=attnT[:, hh, 0:T])
                seq(last)
                for hh in range(KC):
                    last = dve.tensor_tensor(out=attnT[:, hh, 0:T], in0=ps[4 + hh][:, 0:T], in1=attnT[:, hh, 0:T], op=ALU.mult)
                last.then_inc(attn_done, 1)
                seq(dve.tensor_tensor(out=xn[:, 0:nb, :], in0=xn[:, 0:nb, :], in1=wide(0, nb), op=ALU.add))
                dve.wait_ge(wo_done, g + 1)
                for q in range(-(-nb // 2)):
                    w = min(2, nb - 2 * q)
                    last = dve.tensor_tensor(out=tmp[:, 2 * q:2 * q + w, :], in0=xn[:, 2 * q:2 * q + w, :],
                                             in1=ps[2 + q][:, 0:w * D].rearrange("p (t d) -> p t d", d=D), op=ALU.add)
                seq(last)
                layer_norm(nb, tmp, (row_b[:, 2, :], row_b[:, 3, :]), lambda j: h1[:, j, :], var1_done, std1_done, g).then_inc(h1_done, 1)
                dve.wait_ge(trh_done, g + 1)
                dve.wait_ge(h1_done, g + 1)
                seq(dve.tensor_tensor(out=h1[:, 0:nb, :], in0=h1[:, 0:nb, :], in1=wide(1, nb), op=ALU.add))
                dve.wait_ge(ff2_done, g + 1)
                for q in range(-(-nb // 2)):
                    w = min(2, nb - 2 * q)
                    last = dve.tensor_tensor(out=tmp[:, 2 * q:2 * q + w, :], in0=h1[:, 2 * q:2 * q + w, :],
                                             in1=ps[6 + q][:, 0:w * D].rearrange("p (t d) -> p t d", d=D), op=ALU.add)
                seq(last)
                seq(layer_norm(nb, tmp, (row_b[:, 4, :], row_b[:, 5, :]), lambda j: tmp[:, j, :], var2_done, std2_done, g))
                dve.tensor_tensor(out=h1[:, 0:nb, :], in0=tmp[:, 0:nb, :], in1=R[:, ds(g * GB, nb), :], op=ALU.add).then_inc(mix_done, 1)

            PASS2_SEQ = 14
            dve.wait_ge(sup_stored, 16 * (FULL + 1))
            over_groups(dve, seq, PASS2_SEQ, pass2)

            dve.wait_ge(mix_done, FULL + 1)

            def select(it, h, wait_free):
                dve.wait_ge(tab_in[h], it * 16 + 16)
                if wait_free:
                    dve.wait_ge(summed[h], it * HALF_G)
                for k in range(HT):
                    last = dve.tensor_scalar(out=hot[h][:, k, :], in0=iota_row[:, :], scalar1=st_tab[h][:, k, 1:2],
                                             scalar2=st_tab[h][:, k, 2:3], op0=ALU.is_equal, op1=ALU.mult)
                last.then_inc(hot_done[h], 1)

            def carry_on(it, h, wait_stored):
                for q in range(HALF_G):
                    c = h * HALF_G + q
                    dve.wait_ge(summed[h], it * HALF_G + (q + 1))
                    if wait_stored:
                        dve.wait_ge(agg_stored[c], it * 16)
                    dve.scalar_tensor_tensor(out=carry[:, c, :], in0=carry[:, (c - 1) % CARRY, :],
                                             scalar=keep[:, ds(it * CARRY + c, 1)], in1=ps[c][:, 0:D],
                                             op0=ALU.mult, op1=ALU.add).then_inc(carried, 1)
                    dve.wait_ge(carried, it * CARRY + (c + 1))

            def step(it, stored_before, stored):
                select(it, 0, True)
                carry_on(it - 1, 1, stored_before)
                select(it, 1, True)
                carry_on(it, 0, stored)

            select(0, 0, False)
            select(0, 1, False)
            carry_on(0, 0, False)
            step(1, False, True)
            with dve.Fori(2, GATHER_STEPS) as it:
                step(it, True, True)
            carry_on(GATHER_STEPS - 1, 1, True)

            dve.sem_inc(lo_done, LO_CREDIT)
            dve.sem_inc(gelu_done, GELU_CREDIT)
            dve.sem_inc(down_done, DOWN_CREDIT)
            dve.sem_inc(down_read, READ_CREDIT)
            dve.wait_ge(whi_done, 1)
            dve.tensor_tensor(out=router_w[1][:, :, :], in0=router_f[:, :, :], in1=router_w[0][:, :, :].bitcast(F32),
                              op=ALU.subtract).then_inc(wlo_done, 1)
            for e in range(E):
                for n, w in enumerate((up_w, down_w)):
                    dve.wait_ge(whi_done, 2 * e + n + 2)
                    dve.tensor_tensor(out=w[1][:, e, :, :].rearrange("p c n -> p (c n)"), in0=work[:, 2 * (e % 2) + n, :],
                                      in1=w[0][:, e, :, :].rearrange("p c n -> p (c n)").bitcast(F32),
                                      op=ALU.subtract).then_inc(wlo_done, 1)

            def prepare(slot, n, k, nb, pair):
                T = nb * P
                if slot == 0:
                    dve.wait_ge(group_in[k], pair * 48 + 48)
                    seq(dve.tensor_tensor(out=xb[:, 0:nb, :], in0=ag[:, 0:nb, :], in1=xb[:, 0:nb, :], op=ALU.add))
                    seq(dve.scalar_tensor_tensor(out=y[k][:, 0:nb, :], in0=xb[:, 0:nb, :], scalar=0.0, in1=y[k][:, 0:nb, :],
                                                 op0=ALU.max, op1=ALU.add))
                    for j in range(nb):
                        last = dve.bn_stats(out=lstats[:, j, :], in_=y[k][:, j, :])
                    seq(last, apart=True)
                    for j in range(nb):
                        last = dve.bn_aggr(out=lmv[:, j, :], in_=lstats[:, j, :])
                    seq(last)
                    dve.tensor_scalar(out=lrs[:, 0:nb], in0=lmv[:, 0:nb, 1], scalar1=1.0 + EPS, scalar2=EPS * EPS,
                                      op0=ALU.mult, op1=ALU.add).then_inc(var_t, 1)
                if slot == 1:
                    dve.wait_ge(std_t, n + 1)
                    seq(dve.reciprocal(out=lrs[:, 0:nb], in_=lrs[:, 0:nb]))
                    for j in range(nb):
                        last = dve.scalar_tensor_tensor(out=ag[:, j, :], in0=y[k][:, j, :], scalar=lmv[:, j, 0:1],
                                                        in1=lrow_b[:, 0, :], op0=ALU.subtract, op1=ALU.mult)
                    seq(last)
                    for j in range(nb):
                        last = dve.scalar_tensor_tensor(out=ag[:, j, :], in0=ag[:, j, :], scalar=lrs[:, j:j + 1],
                                                        in1=lrow_b[:, 1, :], op0=ALU.mult, op1=ALU.add)
                    last.then_inc(z_done, 1)
                if slot in (2, 3):
                    c = slot - 2
                    dve.wait_ge(zhi_done, n * KC + (c + 1))
                    dve.tensor_tensor(out=z_s[1][:, k, c, 0:T], in0=ps[3][:, 0:T], in1=z_s[0][:, k, c, 0:T].bitcast(F32),
                                      op=ALU.subtract).then_inc(zlo_done, 1)
                if slot == 4:
                    dve.wait_ge(logit_done, n + 1)
                    seq(dve.tensor_tensor(out=logit[:, 0:nb, :], in0=ps[3][:, 0:nb * E].rearrange("p (t e) -> p t e", e=E),
                                          in1=br_b[:, None, :].to_broadcast([P, nb, E]), op=ALU.add), apart=True)
                    for j in range(nb):
                        last = dve.max(out=top[:, j, :], in_=logit[:, j, :])
                    seq(last, apart=True)
                    for j in range(nb):
                        last = dve.max_index(out=topi[:, j, :], in_max=top[:, j, :], in_values=logit[:, j, :])
                    seq(last)
                    dve.tensor_tensor(out=gw[:, 0:nb, 0], in0=top[:, 0:nb, 1], in1=top[:, 0:nb, 0], op=ALU.subtract).then_inc(gap_done, 1)
                if slot == 5:
                    seq(dve.tensor_copy(out=topf[:, 0:nb, :], in_=topi[:, 0:nb, 0:2]))
                    dve.wait_ge(exp_done, n + 1)
                    seq(dve.tensor_scalar(out=gw[:, 0:nb, 2], in0=gw[:, 0:nb, 1], scalar1=1.0, scalar2=None, op0=ALU.add))
                    seq(dve.reciprocal(out=gw[:, 0:nb, 2], in_=gw[:, 0:nb, 2]))
                    seq(dve.tensor_tensor(out=gw[:, 0:nb, 3], in0=gw[:, 0:nb, 1], in1=gw[:, 0:nb, 2], op=ALU.mult))
                    for m, to in enumerate((wfull[k], wtmp)):
                        seq(dve.tensor_tensor(out=to[:, 0:nb, :], in0=iota_row[:, None, 0:E].to_broadcast([P, nb, E]),
                                              in1=topf[:, 0:nb, m:m + 1].to_broadcast([P, nb, E]), op=ALU.is_equal))
                        seq(dve.tensor_tensor(out=to[:, 0:nb, :], in0=to[:, 0:nb, :],
                                              in1=gw[:, 0:nb, 2 + m:3 + m].to_broadcast([P, nb, E]), op=ALU.mult))
                    dve.tensor_tensor(out=wfull[k][:, 0:nb, :], in0=wfull[k][:, 0:nb, :], in1=wtmp[:, 0:nb, :],
                                      op=ALU.add).then_inc(wfull_done, 1)
                    dve.wait_ge(wfull_done, n + 1)
                if slot in (7, 8):
                    h = slot - 7
                    if nb > 2 * h:
                        w = min(2, nb - 2 * h)
                        dve.wait_ge(bias_done, n * 2 + (h + 1))
                        dve.tensor_tensor(out=y[k][:, 2 * h:2 * h + w, :], in0=y[k][:, 2 * h:2 * h + w, :],
                                          in1=ps[3][:, 0:w * D].rearrange("p (t d) -> p t d", d=D), op=ALU.add).then_inc(bias_read, 1)
                        dve.wait_ge(bias_read, n * 2 + (h + 1))

            def low_parts(g, e, nb):
                for f in range(HC):
                    dve.wait_ge(hi_done, g * (E * HC) + (e * HC + f + 1))
                    dve.tensor_tensor(out=hid_s[1][:, e % 2, f, 0:nb * P], in0=hid[:, f % 2, 0:nb * P],
                                      in1=hid_s[0][:, e % 2, f, 0:nb * P].bitcast(F32), op=ALU.subtract).then_inc(lo_done, 1)

            def add_expert(g, e, k, nb):
                for j in range(nb):
                    n = e * nb + j + 1
                    dve.wait_ge(down_done, g * (E * GB) + (n + DOWN_CREDIT))
                    if e:
                        dve.wait_ge(down_read, g * (E * GB) + (n - nb + READ_CREDIT))
                    dve.scalar_tensor_tensor(out=y[k][:, j, :], in0=ps[4 + j][:, 0:D], scalar=wfull[k][:, j, e:e + 1],
                                             in1=y[k][:, j, :], op0=ALU.mult, op1=ALU.add).then_inc(down_read, 1)

            def group(g, k, nb, nb_next):
                pair = g // 2 if isinstance(g, int) else over_pairs.turn
                for e in range(E):
                    if e + 1 < E:
                        low_parts(g, e + 1, nb)
                    elif nb_next:
                        low_parts(g + 1, 0, nb_next)
                    add_expert(g, e, k, nb)
                    if e == 0:
                        dve.wait_ge(down_read, g * (E * GB) + (nb + READ_CREDIT))
                        prepare(8, g, k, nb, pair)
                    if nb_next:
                        prepare(e, g + 1, 1 - k, nb_next, pair + k)

            for slot in range(8):
                prepare(slot, 0, 0, GB, 0)
            low_parts(0, 0, GB)
            over_pairs(dve, seq, 2 * PREPARE_SEQ, group)


_OUT = ("out", (N, D))
_NAMES = ["x", "src", "dst", "edge_weight", "L0_gnn_weight", "L0_gnn_bias", "L0_mix_Wq", "L0_mix_bq", "L0_mix_Wk",
          "L0_mix_bk", "L0_mix_Wv", "L0_mix_bv", "L0_mix_Wo", "L0_mix_bo", "L0_mix_W1", "L0_mix_b1", "L0_mix_W2",
          "L0_mix_b2", "L0_mix_ln1_g", "L0_mix_ln1_b", "L0_mix_ln2_g", "L0_mix_ln2_b", "L0_ffn_gamma", "L0_ffn_beta",
          "L0_ffn_Wr", "L0_ffn_br", "L0_ffn_W1", "L0_ffn_b1", "L0_ffn_W2", "L0_ffn_b2"]


def kernel(**inputs):
    import numpy as np
    import concourse.bacc as bacc
    from concourse.bass_utils import run_bass_kernel_spmd

    nc = bacc.Bacc("TRN2", target_bir_lowering=False, num_devices=1)
    arrays, args = {}, []
    for name in _NAMES:
        a = np.ascontiguousarray(inputs[name])
        arrays["in_" + name] = a
        args.append(nc.dram_tensor("in_" + name, a.shape, mybir.dt.from_np(a.dtype), kind="ExternalInput").ap())
    out = nc.dram_tensor(_OUT[0], _OUT[1], F32, kind="ExternalOutput").ap()
    program(nc, *args, out)
    result = run_bass_kernel_spmd(nc, [arrays], core_ids=[0])
    return result.results[0][_OUT[0]]
```

```python
import concourse.bass as bass
from concourse import mybir
from contextlib import ExitStack

F32 = mybir.dt.float32
BF16 = mybir.dt.bfloat16
F32R = mybir.dt.float32r
I32 = mybir.dt.int32
U32 = mybir.dt.uint32
ALU = mybir.AluOpType
ACT = mybir.ActivationFunctionType
ds = bass.ds

P = 128
N = 6250
NE = 200000
D = 256
KC = D // P
NH = 8
DH = D // NH
FF = 1024
FC = FF // P
E = 8
H = 512
HC = H // P
EPS = 1e-5

NB = -(-N // P)
LASTN = N - (NB - 1) * P
GB = 4
FULL = NB // GB
assert NB == FULL * GB + 1

EC = -(-NE // P)
TAILE = NE - (P - 1) * EC
SH = 8
SCAT_STEPS = -(-EC // (2 * SH))
ECP = SCAT_STEPS * 2 * SH
PARTS = 7
PART_STEPS = SCAT_STEPS // PARTS
PC = ECP // PARTS
FIRST_STEPS = (2, 4, 8)
assert sum(FIRST_STEPS) == PART_STEPS
LANES = 7
assert NB % LANES == 0 and LANES * PC <= ECP
assert SCAT_STEPS == PARTS * PART_STEPS and ECP - PC < EC

GT = 2
GS = GT * P
NG = (P * EC + GS * NB) // GS
HALF_G = 4
GATHER_STEPS = -(-NG // (2 * HALF_G))
NG = GATHER_STEPS * 2 * HALF_G
NT = NG * GT
HT = HALF_G * GT
CARRY = 2 * HALF_G
assert NG % 2 == 0 and NG // 2 <= 512
ZERO_DMAS = 16
STATB = 7
assert NB % STATB == 0
EARLY_E = 6
assert KC * H == HC * D and EARLY_E % 2 == 0


def wait(eng, sem, value, passed=None):
    eng.wait_ge(sem, value)


def wait_apart(eng, sem, value, passed):
    eng.wait_ge(sem, value)
    eng.sem_inc(passed, 1)


class Chain:

    def __init__(self, eng, sem, passed=None):
        self.eng, self.sem, self.base, self.off, self.k, self.passed = eng, sem, 0, 0, 0, passed

    def __call__(self, ins, apart=False):
        self.k += 1
        ins.then_inc(self.sem, 1)
        (wait_apart if apart else wait)(self.eng, self.sem, self.off + (self.base + self.k), self.passed)

    def turn(self, i, per):
        self.base, self.off, self.k = self.base + self.k, i * per, 0

    def end_turn(self, per):
        assert self.k == per, (self.k, per)

    def after(self, turns, per):
        self.base, self.off, self.k = self.base + turns * per, 0, 0


def over_groups(eng, chain, per, body):
    if chain is not None:
        chain.turn(0, 0)
    with eng.Fori(0, FULL) as g:
        if chain is not None:
            chain.off, chain.k = g * per, 0
        body(g, GB)
        if chain is not None:
            chain.end_turn(per)
    if chain is not None:
        chain.after(FULL, per)
    body(FULL, 1)


def over_stages(eng, chain, per, body):
    body(0, GB, None, 0)
    body(1, GB, 0, GB)
    if chain is not None:
        chain.turn(0, 0)
        chain.base -= per
    with eng.Fori(1, FULL - 1) as g:
        if chain is not None:
            chain.off, chain.k = g * per, 0
        body(g + 1, GB, g, GB)
        if chain is not None:
            chain.end_turn(per)
    if chain is not None:
        chain.after(FULL - 1, per)
    body(FULL, 1, FULL - 1, GB)
    body(None, 0, FULL, 1)


KEPT_CREDIT = 1
LO_CREDIT, GELU_CREDIT, DOWN_CREDIT, READ_CREDIT = HC, 1, 2 * GB, GB
PREPARE_SEQ = 4 + 2 + 3 + 4 + 4


def over_pairs(eng, chain, per, body):
    assert FULL % 2 == 0
    if chain is not None:
        chain.turn(0, 0)
    with eng.Fori(0, FULL // 2 - 1) as i:
        if chain is not None:
            chain.off, chain.k = i * per, 0
        for k in range(2):
            body(i * 2 + k, k, GB, GB, i)
        if chain is not None:
            chain.end_turn(per)
    if chain is not None:
        chain.after(FULL // 2 - 1, per)
    body(FULL - 2, 0, GB, GB, FULL // 2 - 1)
    body(FULL - 1, 1, GB, 1, FULL // 2 - 1)
    body(FULL, 0, 1, 0, FULL // 2)


def program(nc, x, src, dst, edge_weight, gnn_w, gnn_b, Wq, bq, Wk, bk, Wv, bv, Wo, bo,
            W1, b1, W2, b2, ln1_g, ln1_b, ln2_g, ln2_b, gamma, beta, Wr, br, eW1, eb1, eW2, eb2, out):
    support = nc.dram_tensor("support", (NB * P, D), F32).ap()
    slots = nc.dram_tensor("slots", (P * NT + (ECP - EC) * P, 4), F32).ap()
    xnb = nc.dram_tensor("xnb", (NB * P, D), F32).ap()
    resid = nc.dram_tensor("resid", (NB * P, D), F32).ap()
    agg = nc.dram_tensor("agg", (NB * P, D), F32).ap()

    ctx = ExitStack()
    with ctx:
        def sem(name):
            return ctx.enter_context(nc.semaphore(name))

        def alloc(stack, name, shape, dt=F32):
            return stack.enter_context(nc.sbuf_tensor(name, shape, dt))

        ident = alloc(ctx, "ident", [P, P])
        iota_row = alloc(ctx, "iota_row", [P, P])
        ones = alloc(ctx, "ones", [P, P])
        eps_col = alloc(ctx, "eps_col", [P, 1])
        ps = [ctx.enter_context(nc.psum_tensor(f"ps{i}", [P, 512], F32)) for i in range(8)]

        early = ExitStack()
        mv = alloc(early, "mv", [P, NB, 2])
        rstd = alloc(early, "rstd", [P, NB])
        rec = alloc(early, "rec", [P, ECP, 4])
        pos_i = alloc(early, "pos_i", [P, ECP], I32)
        cnt = alloc(early, "cnt", [P, NB])
        base = alloc(early, "base", [P, NB])
        prefix = alloc(early, "prefix", [P, NB])
        gcount = alloc(early, "gcount", [P, NB])
        gint = alloc(early, "gint", [P, NB], I32)
        gcol = alloc(early, "gcol", [P, 4])
        gcol_i = alloc(early, "gcol_i", [P, 1], I32)
        iota_g = alloc(early, "iota_g", [P, NG])
        dest_f = alloc(early, "dest_f", [P, NG])
        tri = alloc(early, "tri", [P, P])
        blockones = alloc(early, "blockones", [P, P])
        zeros = alloc(early, "zeros", [P, NT * 4 // ZERO_DMAS])
        st_rec = [alloc(early, f"st_rec{h}", [P, SH, 4]) for h in range(2)]
        st_pos = [alloc(early, f"st_pos{h}", [P, SH], I32) for h in range(2)]

        wg_sb = alloc(early, "wg_sb", [P, KC, D])
        wkv_sb = alloc(early, "wkv_sb", [P, KC, 2 * D])
        wq_sb = alloc(early, "wq_sb", [P, KC, D])
        wo_sb = alloc(early, "wo_sb", [P, KC, D])
        w1_sb = alloc(early, "w1_sb", [P, KC, FF])
        w2_sb = alloc(early, "w2_sb", [P, FC, D])
        bkv_b = alloc(early, "bkv_b", [P, 2 * D])
        row_b = alloc(early, "row_b", [P, 7, D])
        bq_col = alloc(early, "bq_col", [P, KC])
        b1_col = alloc(early, "b1_col", [P, FC])
        kraw = alloc(early, "kraw", [P, 2, D])
        kneg = alloc(early, "kneg", [P, 2, D])
        kphi = alloc(early, "kphi", [P, 2, D])
        vaug = alloc(early, "vaug", [P, 2, KC, P + 4])
        sup_sb = alloc(early, "sup_sb", [P, GB, D])
        kvbd = alloc(early, "kvbd", [P, KC, P])
        ksum = alloc(early, "ksum", [P, KC])
        ksel = alloc(early, "ksel", [P, KC, P])
        stats = alloc(early, "stats", [P, STATB, 6])
        smv = alloc(early, "smv", [P, STATB, 2])
        gmv = alloc(early, "gmv", [P, GB, 2])
        grs = alloc(early, "grs", [P, GB])
        pads = alloc(early, "pads", [P, ECP - EC], I32)
        edge = ExitStack()
        hi = alloc(edge, "hi", [P, ECP], BF16)
        ea = alloc(edge, "ea", [P, ECP])
        eb = alloc(edge, "eb", [P, ECP])
        ec = alloc(edge, "ec", [P, ECP])
        edge.close()
        qneg = alloc(early, "qneg", [P, KC, GB * P])
        qphi = alloc(early, "qphi", [P, KC, GB * P])
        attnT = alloc(early, "attnT", [P, KC, GB * P])
        h1 = alloc(early, "h1", [P, GB, D])
        tmp = alloc(early, "tmp", [P, GB, D])
        hT = alloc(early, "hT", [P, KC, GB * P])
        R = alloc(early, "R", [P, NB + 1, D])
        keep = alloc(early, "keep", [P, NG])
        dest_i = alloc(early, "dest_i", [P, NG], I32)
        st_tab = [alloc(early, f"st_tab{h}", [P, HT, 4]) for h in range(2)]
        big = alloc(early, "big", [P, 2, HT, D])
        rows = [big[:, h, :, :] for h in range(2)]
        uT = big[:, :, :, :].rearrange("p h t d -> p (h t d)").rearrange("p (f t) -> p f t", f=FC)
        gflags = big[:, :, :, :].rearrange("p h t d -> p (h t d)")[:, 0:3 * NG].rearrange("p (k g) -> p k g", k=3)
        mid = alloc(early, "mid", [P, 2, HT * P])
        hot = [mid[:, h, :].rearrange("p (t n) -> p t n", t=HT) for h in range(2)]
        xn = mid[:, 0, :].rearrange("p (t d) -> p t d", t=GB)
        xnT = mid[:, 1, :].rearrange("p (c t) -> p c t", c=KC)
        carry = alloc(early, "carry", [P, CARRY, D])
        h1b = carry[:, 0:GB, :]
        mixed = carry[:, GB:2 * GB, :]
        assert CARRY == 2 * GB
        early.close()

        late = ExitStack()
        w_first = alloc(late, "w_first", [P, EARLY_E, 2, 2, HC * D], F32R)
        work = alloc(late, "work", [P, 4, GB * D])
        w_rest = alloc(late, "w_rest", [P, E - EARLY_E, 2, 2, HC * D], F32R)
        hid = alloc(late, "hid", [P, HC, GB * P])
        hid_hi = alloc(late, "hid_hi", [P, 2, HC, GB * P], F32R)
        y = [work[:, k, :].rearrange("p (t d) -> p t d", d=D) for k in range(2)]
        ag = work[:, 2, :].rearrange("p (t d) -> p t d", d=D)
        xb = work[:, 3, :].rearrange("p (t d) -> p t d", d=D)
        router_f = alloc(late, "router_f", [P, KC, E])
        router_w = [alloc(late, f"router_w{k}", [P, KC, E], F32R) for k in range(2)]
        eb1_col = alloc(late, "eb1_col", [P, E * HC])
        eb2_sb = alloc(late, "eb2_sb", [E, D])
        br_b = alloc(late, "br_b", [P, E])
        lrow_b = alloc(late, "lrow_b", [P, 2, D])
        lstats = alloc(late, "lstats", [P, GB, 6])
        lmv = alloc(late, "lmv", [P, GB, 2])
        lrs = alloc(late, "lrs", [P, GB])
        logit = alloc(late, "logit", [P, GB, E])
        top = alloc(late, "top", [P, GB, 8])
        topi = alloc(late, "topi", [P, GB, 8], U32)
        topf = alloc(late, "topf", [P, GB, 2])
        gw = alloc(late, "gw", [P, GB, 4])
        wfull = [alloc(late, f"wfull{k}", [P, GB, E]) for k in range(2)]
        wtmp = logit
        wfT = alloc(late, "wfT", [E, GB * P])
        z_s = [alloc(late, f"z_s{k}", [P, 2, KC, GB * P], F32R) for k in range(2)]
        rest = ExitStack()
        stage_rest = alloc(rest, "stage_rest", [P, 4, GB * D])
        rest.close()
        hid_lo = alloc(late, "hid_lo", [P, 2, HC, GB * P], F32R)
        hid_s = [hid_hi, hid_lo]
        late.close()

        def weights(e, part, which):
            return w_first[:, e, part, which, :] if e < EARLY_E else w_rest[:, e - EARLY_E, part, which, :]

        def up_w(e, part, c, f):
            return weights(e, part, 0)[:, c * H + f * P:c * H + (f + 1) * P]

        def down_w(e, part, f):
            return weights(e, part, 1)[:, f * D:(f + 1) * D]

        edges_in = sem("edges_in")
        x_in = sem("x_in")
        mixw_in = sem("mixw_in")
        slots_zero = sem("slots_zero")
        consts = sem("consts")
        pool_seq = sem("pool_seq")
        dve_seq = sem("dve_seq")
        pool_passed = sem("pool_passed")
        dve_passed = sem("dve_passed")
        r_ready = sem("r_ready")
        e_ready = sem("e_ready")
        z_ready = sem("z_ready")
        counts_done = sem("counts_done")
        sums_ready = sem("sums_ready")
        gb_done = sem("gb_done")
        sg_ready = sem("sg_ready")
        flags_done = sem("flags_done")
        flags_summed = sem("flags_summed")
        pos_done = sem("pos_done")
        dest_done = sem("dest_done")
        staged = [sem(f"staged{h}") for h in range(2)]
        scattered = [sem(f"scattered{h}") for h in range(2)]
        var_done = sem("var_done")
        std_done = sem("std_done")
        xn_done = sem("xn_done")
        tr_done = sem("tr_done")
        trc_done = sem("trc_done")
        kv_done = sem("kv_done")
        kv_read = sem("kv_read")
        kneg_done = sem("kneg_done")
        kexp_done = sem("kexp_done")
        kphi_done = sem("kphi_done")
        acc_done = sem("acc_done")
        sup_done = sem("sup_done")
        sup_read = sem("sup_read")
        sup_stored = sem("sup_stored")
        kvacc_done = sem("kvacc_done")
        kvbd_done = sem("kvbd_done")
        xn2_done = sem("xn2_done")
        tr2_done = sem("tr2_done")
        trc2_done = sem("trc2_done")
        q_done = sem("q_done")
        qneg_done = sem("qneg_done")
        qexp_done = sem("qexp_done")
        qphi_done = sem("qphi_done")
        att_done = sem("att_done")
        attn_done = sem("attn_done")
        wo_done = sem("wo_done")
        var1_done = sem("var1_done")
        std1_done = sem("std1_done")
        h1_done = sem("h1_done")
        trh_done = sem("trh_done")
        trhc_done = sem("trhc_done")
        ff1_done = sem("ff1_done")
        relu_done = sem("relu_done")
        ff2_done = sem("ff2_done")
        var2_done = sem("var2_done")
        std2_done = sem("std2_done")
        mix_done = sem("mix_done")
        tab_in = [sem(f"tab_in{h}") for h in range(2)]
        gathered = [sem(f"gathered{h}") for h in range(2)]
        hot_done = [sem(f"hot_done{h}") for h in range(2)]
        summed = [sem(f"summed{h}") for h in range(2)]
        carried = sem("carried")
        sum_kept = sem("sum_kept")
        agg_stored = [sem(f"agg_stored{k}") for k in range(2)]
        xnb_ready = sem("xnb_ready")
        xnb_stored = sem("xnb_stored")
        resid_stored = sem("resid_stored")
        late_in = sem("late_in")
        stage_in = [sem(f"stage_in{k}") for k in range(2)]
        whi_done = sem("whi_done")
        wlo_done = sem("wlo_done")
        group_in = [sem(f"group_in{k}") for k in range(2)]
        var_t = sem("var_t")
        std_t = sem("std_t")
        z_done = sem("z_done")
        zt_done = sem("zt_done")
        zhi_done = sem("zhi_done")
        zlo_done = sem("zlo_done")
        logit_done = sem("logit_done")
        gap_done = sem("gap_done")
        exp_done = sem("exp_done")
        wfull_done = sem("wfull_done")
        wft_done = sem("wft_done")
        wftc_done = sem("wftc_done")
        bias_done = sem("bias_done")
        bias_read = sem("bias_read")
        up_done = sem("up_done")
        gelu_done = sem("gelu_done")
        hi_done = sem("hi_done")
        lo_done = sem("lo_done")
        down_done = sem("down_done")
        down_read = sem("down_read")
        out_stored = [sem(f"out_stored{k}") for k in range(2)]

        MIXW_DMAS = 18
        LATE_DMAS = 6

        block = ctx.enter_context(nc.Block())

        @block.sync
        def _(sp):
            split = (P - 1) * EC
            sp.wait_ge(e_ready, 1)
            for buf, a in ((eb[:, 0:EC].bitcast(I32), src), (ea[:, 0:EC].bitcast(I32), dst), (ec[:, 0:EC], edge_weight)):
                sp.dma_start(buf[0:P - 1, :], a[0:split].rearrange("(p j) -> p j", p=P - 1)).then_inc(edges_in, 16)
                sp.dma_start(buf[P - 1:P, 0:TAILE], a[split:NE].rearrange("(p j) -> p j", p=1)).then_inc(edges_in, 16)
            sp.wait_ge(r_ready, 1)
            sp.dma_start(R[:, 0:NB - 1, :], x[0:(NB - 1) * P, :].rearrange("(t p) d -> p t d", p=P)).then_inc(x_in, 16)
            sp.dma_start(R[0:LASTN, NB - 1, :], x[(NB - 1) * P:N, :]).then_inc(x_in, 16)
            for w, a in ((wg_sb[:, :, :], gnn_w), (wkv_sb[:, :, 0:D], Wk), (wkv_sb[:, :, D:2 * D], Wv),
                         (wq_sb[:, :, :], Wq), (wo_sb[:, :, :], Wo), (w1_sb[:, :, :], W1), (w2_sb[:, :, :], W2)):
                sp.dma_start(w, a.rearrange("(c p) n -> p c n", p=P)).then_inc(mixw_in, 16)
            for n, a in enumerate((bo, b2, ln1_g, ln1_b, ln2_g, ln2_b, gnn_b)):
                sp.dma_start(row_b[:, n, :], a.partition_broadcast(P)).then_inc(mixw_in, 16)
            sp.dma_start(bkv_b[:, 0:D], bk.partition_broadcast(P)).then_inc(mixw_in, 16)
            sp.dma_start(bkv_b[:, D:2 * D], bv.partition_broadcast(P)).then_inc(mixw_in, 16)
            with nc.allow_non_contiguous_dma(reason="bias columns, a few kilobytes"):
                sp.dma_start(bq_col[:, :], bq.rearrange("(c p) -> p c", p=P)).then_inc(mixw_in, 16)
                sp.dma_start(b1_col[:, :], b1.rearrange("(c p) -> p c", p=P)).then_inc(mixw_in, 16)

            def stage(it, h):
                col = it * (2 * SH) + h * SH
                sp.dma_start(st_rec[h][:, :, :], rec[:, ds(col, SH), :]).then_inc(staged[h], 16)
                sp.dma_start(st_pos[h][:, :], pos_i[:, ds(col, SH)]).then_inc(staged[h], 16)

            def restage(it):
                for h in range(2):
                    sp.wait_ge(scattered[h], it * (16 * SH))
                    stage(it, h)

            sp.wait_ge(pos_done, 1)
            for h in range(2):
                stage(0, h)
            done = 0
            for n, steps in enumerate(FIRST_STEPS):
                sp.wait_ge(pos_done, n + 1)
                with sp.Fori(max(done, 1), done + steps) as it:
                    restage(it)
                done += steps
            with sp.Fori(1, PARTS - 1) as part:
                with sp.Fori(0, PART_STEPS) as it:
                    sp.wait_ge(pos_done, part + len(FIRST_STEPS))
                    restage(part * PART_STEPS + it)
            sp.wait_ge(pos_done, PARTS + len(FIRST_STEPS))
            with sp.Fori(SCAT_STEPS - PART_STEPS, SCAT_STEPS) as it:
                restage(it)
            for h in range(2):
                sp.wait_ge(scattered[h], SCAT_STEPS * 16 * SH)

            table = slots[0:P * NT, :].rearrange("(p t) c -> p t c", p=P)

            def load_slots(it, h):
                sp.dma_start(st_tab[h][:, :, :], table[:, ds(it * (2 * HT) + h * HT, HT), :]).then_inc(tab_in[h], 16)

            def reload_slots(it):
                for h in range(2):
                    sp.wait_ge(gathered[h], it * (16 * HT))
                    sp.wait_ge(hot_done[h], it)
                    load_slots(it, h)

            def stage_expert(e, k, to):
                for n, (a, chunks) in enumerate(((eW1, KC), (eW2, HC))):
                    sp.dma_start(to[:, 2 * k + n, :].rearrange("p (c n) -> p c n", c=chunks),
                                 a[ds(e, 1), :, :].rearrange("e (c p) n -> p (e c) n", p=P)).then_inc(stage_in[k], 16)

            for h in range(2):
                load_slots(0, h)
            sp.wait_ge(mix_done, FULL + 1)
            sp.wait_ge(xnb_stored, 16 * (FULL + 1))
            sp.wait_ge(dest_done, 1)
            for k in range(2):
                reload_slots(k + 1)
                stage_expert(k, k, work)
            with sp.Fori(1, EARLY_E // 2) as pair:
                for k in range(2):
                    reload_slots(pair * 2 + (k + 1))
                    sp.wait_ge(wlo_done, pair * 4 + (2 * k - 2))
                    stage_expert(pair * 2 + k, k, work)
            with sp.Fori(EARLY_E + 1, GATHER_STEPS) as it:
                reload_slots(it)

            sp.wait_ge(wlo_done, 2 * EARLY_E)
            for to, a in ((xb, xnb), (y[0], resid)):
                sp.dma_start(to, a[0:GB * P, :].rearrange("(t p) d -> p t d", p=P)).then_inc(group_in[0], 16)

            sp.wait_ge(carried, NG)
            for h in range(2):
                sp.wait_ge(gathered[h], GATHER_STEPS * 16 * HT)
            sp.wait_ge(sum_kept, NG + KEPT_CREDIT)
            FIRST = 2 * GB

            def store_sums(k, lo, hi_):
                sp.dma_start(agg[lo * P:hi_ * P, :].rearrange("(t p) d -> p t d", p=P), R[:, lo:hi_, :]).then_inc(agg_stored[k], 16)

            sp.dma_start(ag, R[:, 0:GB, :]).then_inc(group_in[0], 16)
            store_sums(0, 0, FIRST)
            for n, a in enumerate((gamma, beta)):
                sp.dma_start(lrow_b[:, n, :], a.partition_broadcast(P)).then_inc(late_in, 16)
            sp.dma_start(br_b[:, :], br.partition_broadcast(P)).then_inc(late_in, 16)
            sp.dma_start(eb2_sb[:, :], eb2).then_inc(late_in, 16)
            sp.dma_start(router_f[:, :, :], Wr.rearrange("(c p) n -> p c n", p=P)).then_inc(late_in, 16)
            with nc.allow_non_contiguous_dma(reason="bias columns, a few kilobytes"):
                sp.dma_start(eb1_col[:, :], eb1.rearrange("e (c p) -> p (e c)", p=P)).then_inc(late_in, 16)
            def store_group(g, k, nb):
                sp.wait_ge(down_read, g * (E * GB) + (E * nb + READ_CREDIT))
                if nb == GB:
                    sp.dma_start(out[ds(g * (GB * P), GB * P), :].rearrange("(t p) d -> p t d", p=P),
                                 y[k]).then_inc(out_stored[k], 16)
                else:
                    sp.dma_start(out[g * (GB * P):N, :], y[k][0:LASTN, 0, :]).then_inc(out_stored[k], 16)

            def load_group(n, k, nb, pairs):
                row = n * (GB * P)
                sp.wait_ge(zt_done, n * KC)
                for to, a in ((ag, agg), (xb, xnb)):
                    sp.dma_start(to[:, 0:nb, :], a[ds(row, nb * P), :].rearrange("(t p) d -> p t d", p=P)).then_inc(group_in[k], 16)
                if pairs is not None:
                    sp.wait_ge(out_stored[k], pairs * 16)
                sp.dma_start(y[k][:, 0:nb, :], resid[ds(row, nb * P), :].rearrange("(t p) d -> p t d", p=P)).then_inc(group_in[k], 16)

            store_sums(1, FIRST, NB)
            for e in range(EARLY_E, E):
                stage_expert(e, e % 2, stage_rest)
            for k in range(2):
                sp.wait_ge(agg_stored[k], 16)
            load_group(1, 1, GB, None)
            store_group(0, 0, GB)
            with sp.Fori(1, FULL // 2) as i:
                load_group(i * 2, 0, GB, i)
                store_group(i * 2 - 1, 1, GB)
                load_group(i * 2 + 1, 1, GB, i)
                store_group(i * 2, 0, GB)
            load_group(FULL, 0, 1, FULL // 2)
            store_group(FULL - 1, 1, GB)
            store_group(FULL, 0, 1)
            sp.wait_ge(out_stored[0], 16 * (FULL // 2 + 1))
            sp.wait_ge(out_stored[1], 16 * (FULL // 2))

        @block.gpsimd
        def _(pool):
            seq = Chain(pool, pool_seq)
            seq(pool.memset(ones[:, :], 1.0))
            seq(pool.iota(iota_row[:, :], [[1, P]], base=0, channel_multiplier=0, allow_small_or_imprecise_dtypes=True))
            seq(pool.iota(iota_g[:, :], [[1, NG]], base=0, channel_multiplier=0, allow_small_or_imprecise_dtypes=True))
            seq(pool.affine_select(out=ident[:, :], in_=ones[:, :], compare_op=ALU.is_equal, fill=0.0, base=0,
                                   pattern=[[-1, P]], channel_multiplier=1))
            seq(pool.affine_select(out=tri[:, :], in_=ones[:, :], compare_op=ALU.is_gt, fill=0.0, base=0,
                                   pattern=[[1, P]], channel_multiplier=-1))
            bv3 = blockones[:, :].rearrange("p (h d) -> p h d", d=DH)
            seq(pool.affine_select(out=bv3, in_=ones[:, :].rearrange("p (h d) -> p h d", d=DH), compare_op=ALU.is_ge,
                                   fill=0.0, base=0, pattern=[[-DH, P // DH], [0, DH]], channel_multiplier=1))
            pool.affine_select(out=bv3, in_=bv3, compare_op=ALU.is_ge, fill=0.0, base=DH - 1,
                               pattern=[[DH, P // DH], [0, DH]], channel_multiplier=-1).then_inc(consts, 1)
            pool.iota(pads[:, :], [[P, ECP - EC]], base=P * NT, channel_multiplier=1).then_inc(consts, 1)

            pool.wait_ge(slots_zero, 16 * ZERO_DMAS)
            with pool.Fori(0, SCAT_STEPS) as it:
                for h in range(2):
                    wait_apart(pool, staged[h], it * 32 + 32, pool_passed)
                    for j in range(SH):
                        pool.indirect_dma_start(
                            out=slots, out_offset=bass.IndirectOffsetOnAxis(ap=st_pos[h][:, j:j + 1], axis=0),
                            in_=st_rec[h][:, j, :], in_offset=None).then_inc(scattered[h], 16)

            pool.wait_ge(sup_stored, 16 * (FULL + 1))

            def gather(it, h):
                wait_apart(pool, tab_in[h], it * 16 + 16, pool_passed)
                for j in range(HT):
                    pool.indirect_dma_start(
                        out=rows[h][:, j, :], out_offset=None, in_=support,
                        in_offset=bass.IndirectOffsetOnAxis(ap=st_tab[h][:, j, 0:1].bitcast(I32), axis=0)
                    ).then_inc(gathered[h], 16)

            pool.wait_ge(mix_done, FULL + 1)
            for h in range(2):
                gather(0, h)
            with pool.Fori(1, GATHER_STEPS) as it:
                for h in range(2):
                    pool.wait_ge(summed[h], it * HALF_G)
                    gather(it, h)

        @block.tensor
        def _(pe):
            pe.wait_ge(consts, 1)
            pe.wait_ge(counts_done, 1)
            pe.matmul(ps[6][:, 0:NB], lhsT=tri[:, :], rhs=cnt[:, :], start=True, stop=True)
            pe.matmul(ps[6][:, 64:64 + NB], lhsT=ones[:, :], rhs=cnt[:, :], start=True, stop=True)
            pe.matmul(ps[6][0:NB, 128:129], lhsT=cnt[:, :], rhs=ones[:, 0:1], start=True, stop=True).then_inc(sums_ready, 1)
            pe.wait_ge(gb_done, 1)
            pe.matmul(ps[5][0:NB, 0:1], lhsT=tri[0:NB, 0:NB], rhs=gcol[0:NB, 0:1], start=True, stop=True).then_inc(sg_ready, 1)
            pe.wait_ge(flags_done, 1)
            for k in range(3):
                for half in range(2):
                    last = pe.matmul(ps[2 * k + half][:, 0:NG // 2], lhsT=ones[0:NB, :],
                                     rhs=gflags[0:NB, k, half * (NG // 2):(half + 1) * (NG // 2)], start=True, stop=True)
            last.then_inc(flags_summed, 1)
            pe.wait_ge(dest_done, 1)

            def transposes(nb, source, banks, done):
                for c in range(KC):
                    for j in range(nb):
                        last = pe.transpose(ps[banks[c]][:, j * P:(j + 1) * P], source[:, j, c * P:(c + 1) * P], ident[:, :])
                last.then_inc(done, 1)

            pe.wait_ge(mixw_in, 16 * MIXW_DMAS)
            pe.matmul(ps[5][:, 0:2 * (P + 4)], lhsT=zeros[:, 0:P], rhs=zeros[:, 0:2 * (P + 4)], start=True, stop=False)

            def pass1(g, nb):
                rowsn = P if nb == GB else LASTN
                pe.wait_ge(xn_done, g + 1)
                transposes(nb, xn, (0, 1), tr_done)
                pe.wait_ge(trc_done, g + 1)

                def products(j):
                    if j >= 2:
                        pe.wait_ge(kv_read, g * GB + (j - 1))
                        pe.wait_ge(sup_read, g * GB + (j - 1))
                    for c in range(KC):
                        last = pe.matmul(ps[2 + j % 2][:, :], lhsT=xnT[:, c, j * P:(j + 1) * P], rhs=wkv_sb[:, c, :],
                                         start=(c == 0), stop=(c == KC - 1))
                    last.then_inc(kv_done, 1)
                    for c in range(KC):
                        last = pe.matmul(ps[4 + j % 2 * 2][:, 0:D], lhsT=xnT[:, c, j * P:(j + 1) * P],
                                         rhs=wg_sb[:, c, :], start=(c == 0), stop=(c == KC - 1))
                    last.then_inc(sup_done, 1)

                def accumulate(j):
                    pe.wait_ge(kphi_done, g * GB + (j + 1))
                    for c in range(KC):
                        last = pe.matmul(ps[5][:, c * (P + 4):c * (P + 4) + P + 1], lhsT=kphi[0:rowsn, j % 2, c * P:(c + 1) * P],
                                         rhs=vaug[0:rowsn, j % 2, c, 0:P + 1], start=False, stop=False, skip_group_check=True)
                    last.then_inc(acc_done, 1)

                for j in range(nb):
                    products(j)
                    if j:
                        accumulate(j - 1)
                accumulate(nb - 1)

            over_groups(pe, None, 0, pass1)
            pe.matmul(ps[5][:, 0:2 * (P + 4)], lhsT=zeros[:, 0:P], rhs=zeros[:, 0:2 * (P + 4)], start=False, stop=True).then_inc(kvacc_done, 1)

            pe.wait_ge(kvbd_done, 1)

            def pass2(a, na, b, nb):
                Ta, Tb = na * P, nb * P

                def hidden(chunks):
                    if nb == 0:
                        return
                    for f in chunks:
                        if f >= 2:
                            pe.wait_ge(relu_done, b * FC + (f - 1))
                        for c in range(KC):
                            last = pe.matmul(ps[4 + f % 2][:, 0:Tb], lhsT=w1_sb[:, c, f * P:(f + 1) * P], rhs=hT[:, c, 0:Tb],
                                             start=(c == 0), stop=(c == KC - 1))
                        last.then_inc(ff1_done, 1)

                if nb:
                    pe.wait_ge(trhc_done, b + 1)
                if na:
                    pe.wait_ge(xn2_done, a + 1)
                    transposes(na, xn, (0, 1), tr2_done)
                hidden((0, 1))
                if na:
                    pe.wait_ge(trc2_done, a + 1)
                    for hh in range(KC):
                        for c in range(KC):
                            last = pe.matmul(ps[2 + hh][:, 0:Ta], lhsT=wq_sb[:, c, hh * P:(hh + 1) * P], rhs=xnT[:, c, 0:Ta],
                                             start=(c == 0), stop=(c == KC - 1))
                    last.then_inc(q_done, 1)
                hidden((2, 3, 4))
                if na:
                    pe.wait_ge(qphi_done, a + 1)
                    for hh in range(KC):
                        pe.matmul(ps[hh][:, 0:Ta], lhsT=kvbd[:, hh, :], rhs=qphi[:, hh, 0:Ta], start=True, stop=True)
                        last = pe.matmul(ps[2 + hh][:, 0:Ta], lhsT=ksel[:, hh, :], rhs=qphi[:, hh, 0:Ta], start=True, stop=True)
                    last.then_inc(att_done, 1)
                hidden((5, 6, 7))
                if na:
                    pe.wait_ge(attn_done, a + 1)
                    for j in range(na):
                        for c in range(KC):
                            last = pe.matmul(ps[j // 2][:, (j % 2) * D:(j % 2 + 1) * D], lhsT=attnT[:, c, j * P:(j + 1) * P],
                                             rhs=wo_sb[:, c, :], start=(c == 0), stop=(c == KC - 1))
                    last.then_inc(wo_done, 1)
                if nb:
                    pe.wait_ge(relu_done, b * FC + FC)
                    for j in range(nb):
                        for f in range(FC):
                            last = pe.matmul(ps[6 + j // 2][:, (j % 2) * D:(j % 2 + 1) * D], lhsT=uT[:, f, j * P:(j + 1) * P],
                                             rhs=w2_sb[:, f, :], start=(f == 0), stop=(f == FC - 1))
                    last.then_inc(ff2_done, 1)
                if na:
                    pe.wait_ge(h1_done, a + 1)
                    transposes(na, h1, (0, 1), trh_done)

            assert FC == 8
            over_stages(pe, None, 0, pass2)

            def sum_half(it, h, wait_free):
                pe.wait_ge(hot_done[h], it + 1)
                pe.wait_ge(gathered[h], it * (16 * HT) + 16 * HT)
                for q in range(HALF_G):
                    c = h * HALF_G + q
                    if wait_free:
                        pe.wait_ge(carried, it * CARRY + (c + 1 - CARRY))
                    for t in range(GT):
                        k = q * GT + t
                        last = pe.matmul(ps[c][:, 0:D], lhsT=hot[h][:, k, :], rhs=rows[h][:, k, :],
                                         start=(t == 0), stop=(t == GT - 1))
                    last.then_inc(summed[h], 1)

            for h in range(2):
                sum_half(0, h, False)
            with pe.Fori(1, GATHER_STEPS) as it:
                for h in range(2):
                    sum_half(it, h, True)

            pe.wait_ge(late_in, 16 * LATE_DMAS)

            def split_product(to, a, b, first=True, last=True):
                for n, (s, m) in enumerate(((0, 0), (0, 1), (1, 0))):
                    ins = pe.matmul(to, lhsT=a(s), rhs=b(m), start=(first and n == 0), stop=(last and n == 2))
                return ins

            def prepare(slot, n, k, nb):
                if slot in (2, 3):
                    c = slot - 2
                    pe.wait_ge(z_done, n + 1)
                    if c:
                        pe.wait_ge(zlo_done, n * KC + 1)
                    for j in range(nb):
                        last = pe.transpose(ps[3][:, j * P:(j + 1) * P], ag[:, j, c * P:(c + 1) * P], ident[:, :])
                    last.then_inc(zt_done, 1)
                if slot == 4:
                    pe.wait_ge(zlo_done, n * KC + KC)
                    for j in range(nb):
                        for c in range(KC):
                            last = split_product(ps[3][:, j * E:(j + 1) * E], lambda s: z_s[s][:, k, c, j * P:(j + 1) * P],
                                                 lambda m: router_w[m][:, c, :], c == 0, c == KC - 1)
                    last.then_inc(logit_done, 1)
                if slot == 6:
                    pe.wait_ge(wfull_done, n + 1)
                    for j in range(nb):
                        last = pe.transpose(ps[3][0:E, j * P:(j + 1) * P], wfull[k][:, j, :], ident[:, :])
                    last.then_inc(wft_done, 1)
                if slot in (7, 8):
                    h = slot - 7
                    if h == 0:
                        pe.wait_ge(wftc_done, n + 1)
                    else:
                        pe.wait_ge(bias_read, n * 2 + 1)
                    for j in range(2 * h, min(nb, 2 * h + 2)):
                        last = pe.matmul(ps[3][:, (j % 2) * D:(j % 2 + 1) * D], lhsT=wfT[:, j * P:(j + 1) * P],
                                         rhs=eb2_sb[:, :], start=True, stop=True)
                    if nb > 2 * h:
                        last.then_inc(bias_done, 1)

            def up(g, e, k, nb):
                T = nb * P
                for f in range(HC):
                    c = e * HC + f
                    if f == 0:
                        pe.wait_ge(gelu_done, g * (E * HC) + (c + GELU_CREDIT))
                    if f == 3:
                        pe.wait_ge(gelu_done, g * (E * HC) + (c - 2 + GELU_CREDIT))
                    for kc in range(KC):
                        last = split_product(ps[f % 3][:, 0:T], lambda s: up_w(e, s, kc, f),
                                             lambda m: z_s[m][:, k, kc, 0:T], kc == 0, kc == KC - 1)
                    last.then_inc(up_done, 1)

            def down(g, e, nb):
                pe.wait_ge(lo_done, g * (E * HC) + (e * HC + HC + LO_CREDIT))
                for j in range(nb):
                    read = (e - 1) * nb + j + 1 if e else j + 1 - GB
                    pe.wait_ge(down_read, g * (E * GB) + (read + READ_CREDIT))
                    for f in range(HC):
                        last = split_product(ps[4 + j][:, 0:D], lambda s: hid_s[s][:, e % 2, f, j * P:(j + 1) * P],
                                             lambda m: down_w(e, m, f), f == 0, f == HC - 1)
                    last.then_inc(down_done, 1)

            def group(g, k, nb, nb_next, pair):
                for e in range(E):
                    if e + 1 < E:
                        up(g, e + 1, k, nb)
                    elif nb_next:
                        up(g + 1, 0, 1 - k, nb_next)
                    down(g, e, nb)
                    if e == 0:
                        prepare(8, g, k, nb)
                    if nb_next:
                        prepare(e, g + 1, 1 - k, nb_next)

            pe.wait_ge(wlo_done, 2 * EARLY_E + 1)
            for slot in range(8):
                prepare(slot, 0, 0, GB)
            pe.wait_ge(wlo_done, 2 * E + 1)
            up(0, 0, 0, GB)
            over_pairs(pe, None, 0, group)

        @block.scalar
        def _(act):
            act.wait_ge(z_ready, 1)
            for k in range(ZERO_DMAS):
                act.dma_start(slots[0:P * NT, :].rearrange("(p a t) c -> a p (t c)", p=P, a=ZERO_DMAS)[k, :, :],
                              zeros[:, :]).then_inc(slots_zero, 16)
            act.wait_ge(var_done, 1)
            act.activation(rstd[:, :], mv[:, :, 1], ACT.Sqrt, bias=eps_col[:, 0:1]).then_inc(std_done, 1)

            def copy_transposed(g, nb, wait, to, done):
                T = nb * P
                act.wait_ge(wait, g + 1)
                act.activation(to[:, 0, 0:T], ps[0][:, 0:T], ACT.Copy)
                act.activation(to[:, 1, 0:T], ps[1][:, 0:T], ACT.Copy).then_inc(done, 1)

            def pass1(g, nb):
                copy_transposed(g, nb, tr_done, xnT, trc_done)
                for j in range(nb):
                    n = g * GB + (j + 1)
                    act.wait_ge(kneg_done, n)
                    act.activation(kneg[:, j % 2, :], kneg[:, j % 2, :], ACT.Exp).then_inc(kexp_done, 1)
                    act.wait_ge(sup_done, n)
                    act.activation(sup_sb[:, j, :], ps[4 + j % 2 * 2][:, 0:D], ACT.Copy).then_inc(sup_read, 1)
                act.wait_ge(sup_read, g * GB + nb)
                act.dma_start(support[ds(g * (GB * P), nb * P), :].rearrange("(t p) d -> p t d", p=P),
                              sup_sb[:, 0:nb, :]).then_inc(sup_stored, 16)
                act.wait_ge(sup_stored, g * 16 + 16)

            over_groups(act, None, 0, pass1)

            def pass2(a, na, b, nb):
                Ta, Tb = na * P, nb * P

                def hidden(chunks):
                    if nb == 0:
                        return
                    for f in chunks:
                        act.wait_ge(ff1_done, b * FC + (f + 1))
                        act.activation(uT[:, f, 0:Tb], ps[4 + f % 2][:, 0:Tb], ACT.Relu, bias=b1_col[:, f:f + 1]).then_inc(relu_done, 1)

                if na:
                    copy_transposed(a, na, tr2_done, xnT, trc2_done)
                    act.wait_ge(xnb_ready, a + 1)
                    act.dma_start(xnb[ds(a * (GB * P), Ta), :].rearrange("(t p) d -> p t d", p=P), sup_sb[:, 0:na, :]).then_inc(xnb_stored, 16)
                hidden((0, 1))
                if na:
                    for hh in range(KC):
                        act.wait_ge(qneg_done, a * KC + (hh + 1))
                        act.activation(qneg[:, hh, 0:Ta], qneg[:, hh, 0:Ta], ACT.Exp).then_inc(qexp_done, 1)
                hidden(range(2, FC))
                if na:
                    act.wait_ge(var1_done, a + 1)
                    act.wait_ge(xnb_stored, a * 16 + 16)
                    act.activation(grs[:, 0:na], gmv[:, 0:na, 1], ACT.Sqrt, bias=eps_col[:, 0:1]).then_inc(std1_done, 1)
                    copy_transposed(a, na, trh_done, hT, trhc_done)
                if nb:
                    act.wait_ge(var2_done, b + 1)
                    act.activation(grs[:, 0:nb], gmv[:, 0:nb, 1], ACT.Sqrt, bias=eps_col[:, 0:1]).then_inc(std2_done, 1)
                    act.wait_ge(mix_done, b + 1)
                    act.dma_start(resid[ds(b * (GB * P), Tb), :].rearrange("(t p) d -> p t d", p=P), mixed[:, 0:nb, :]).then_inc(resid_stored, 16)
                    act.wait_ge(resid_stored, b * 16 + 16)

            over_stages(act, None, 0, pass2)

            act.wait_ge(dest_done, 1)
            act.wait_ge(mix_done, FULL + 1)
            act.sem_inc(sum_kept, KEPT_CREDIT)
            def high_parts(to, k, source):
                for n in range(2):
                    act.activation(to[:, :, 0, n, :].rearrange("p e n -> p (e n)"), source[:, 2 * k + n, :],
                                   ACT.Copy).then_inc(whi_done, 1)

            def keep_sums(it):
                for c in range(CARRY):
                    where = act.value_load(dest_i[0:1, ds(it * CARRY + c, 1)], min_val=0, max_val=NB)
                    act.wait_ge(sum_kept, it * CARRY + (c + KEPT_CREDIT))
                    act.wait_ge(carried, it * CARRY + (c + 1))
                    act.activation(R[:, ds(where, 1), :].rearrange("p a d -> p (a d)"), carry[:, c, :],
                                   ACT.Copy).then_inc(sum_kept, 1)

            with act.Fori(0, EARLY_E // 2) as pair:
                for k in range(2):
                    keep_sums(pair * 2 + k)
                    act.wait_ge(stage_in[k], pair * 32 + 32)
                    high_parts(w_first[:, ds(pair * 2 + k, 1)], k, work)
            with act.Fori(EARLY_E, GATHER_STEPS) as it:
                keep_sums(it)

            act.wait_ge(late_in, 16 * LATE_DMAS)
            act.activation(router_w[0][:, :, :], router_f[:, :, :], ACT.Copy).then_inc(whi_done, 1)
            def prepare(slot, n, k, nb):
                T = nb * P
                if slot == 1:
                    act.wait_ge(var_t, n + 1)
                    act.activation(lrs[:, 0:nb], lrs[:, 0:nb], ACT.Sqrt).then_inc(std_t, 1)
                if slot in (2, 3):
                    c = slot - 2
                    act.wait_ge(zt_done, n * KC + (c + 1))
                    act.activation(z_s[0][:, k, c, 0:T], ps[3][:, 0:T], ACT.Copy).then_inc(zhi_done, 1)
                if slot == 5:
                    act.wait_ge(gap_done, n + 1)
                    act.activation(gw[:, 0:nb, 1], gw[:, 0:nb, 0], ACT.Exp).then_inc(exp_done, 1)
                if slot == 6:
                    act.wait_ge(wft_done, n + 1)
                    act.activation(wfT[:, 0:T], ps[3][0:E, 0:T], ACT.Copy).then_inc(wftc_done, 1)

            def hidden(g, e, nb):
                T = nb * P
                for f in range(HC):
                    n = e * HC + f + 1
                    act.wait_ge(up_done, g * (E * HC) + n)
                    act.wait_ge(lo_done, g * (E * HC) + (n - HC + LO_CREDIT))
                    act.activation(hid[:, f, 0:T], ps[f % 3][:, 0:T], ACT.Gelu,
                                   bias=eb1_col[:, e * HC + f:e * HC + f + 1]).then_inc(gelu_done, 1)
                    if f == 0:
                        used = (e - 1) * nb if e >= 2 else (e - 1) * GB
                        act.wait_ge(down_done, g * (E * GB) + (used + DOWN_CREDIT))
                    act.wait_ge(gelu_done, g * (E * HC) + (n + GELU_CREDIT))
                    act.activation(hid_s[0][:, e % 2, f, 0:T], hid[:, f, 0:T], ACT.Copy).then_inc(hi_done, 1)

            def group(g, k, nb, nb_next, pair):
                for e in range(E):
                    if e + 1 < E:
                        hidden(g, e + 1, nb)
                    elif nb_next:
                        hidden(g + 1, 0, nb_next)
                    if nb_next:
                        prepare(e, g + 1, 1 - k, nb_next)

            for slot in range(8):
                prepare(slot, 0, 0, GB)
            for k in range(2):
                act.wait_ge(agg_stored[k], 16)
            for e in range(EARLY_E, E):
                act.wait_ge(stage_in[e % 2], 32 * (e // 2 + 1))
                high_parts(w_rest[:, e - EARLY_E:e - EARLY_E + 1], e % 2, stage_rest)
            hidden(0, 0, GB)
            over_pairs(act, None, 0, group)

        @block.vector
        def _(dve):
            seq = Chain(dve, dve_seq, dve_passed)
            ebi, eai, eci = [e[:, 0:EC].bitcast(I32) for e in (eb, ea, ec)]
            seq(dve.memset(ebi[:, TAILE:EC], N))
            seq(dve.memset(eai[:, TAILE:EC], 0))
            dve.memset(ec[:, TAILE:EC], 0.0).then_inc(e_ready, 1)
            dve.memset(R[:, NB - 1, :], 0.0).then_inc(r_ready, 1)
            dve.memset(zeros[:, :], 0.0).then_inc(z_ready, 1)
            dve.memset(eps_col[:, :], EPS)
            dve.memset(vaug[:, :, :, P:P + 1], 1.0)
            dve.memset(hi[:, EC:ECP], 0.0)
            seq(dve.memset(rec[:, :, :], 0.0))

            dve.wait_ge(edges_in, 16 * 6)
            dve.tensor_copy(out=rec[:, 0:EC, 0].bitcast(I32), in_=eai)
            seq(dve.tensor_copy(out=rec[:, 0:EC, 2], in_=ec[:, 0:EC]))
            dve.tensor_scalar(out=eai, in0=ebi, scalar1=7, scalar2=None, op0=ALU.logical_shift_right)
            seq(dve.tensor_scalar(out=eci, in0=ebi, scalar1=127, scalar2=None, op0=ALU.bitwise_and))
            dve.tensor_copy(out=hi[:, 0:EC], in_=eai)
            seq(dve.tensor_copy(out=rec[:, 0:EC, 1], in_=eci))

            dve.wait_ge(consts, 1)
            flags = [e[:, :].bitcast(BF16)[:, l * ECP:l * ECP + EC] for e in (ea, eb, ec, pos_i) for l in range(2)][:LANES]
            seq.turn(0, 0)
            with dve.Fori(0, NB // LANES) as i:
                seq.off, seq.k = i * 1, 0
                for l in range(LANES):
                    b = ds(i * LANES + l, 1)
                    last = dve.tensor_scalar(out=flags[l], in0=hi[:, 0:EC], scalar1=iota_row[:, b], scalar2=None,
                                             op0=ALU.is_equal, op1=ALU.add, accum_out=cnt[:, b])
                seq(last)
            seq.after(NB // LANES, 1)
            dve.sem_inc(counts_done, 1)

            dve.wait_ge(sums_ready, 1)
            def groups_of(count, out_f, out_i):
                seq(dve.tensor_scalar(out=out_i, in0=count, scalar1=float(GS - 1), scalar2=None, op0=ALU.add))
                seq(dve.tensor_scalar(out=out_i, in0=out_i, scalar1=GS.bit_length() - 1, scalar2=None, op0=ALU.logical_shift_right))
                seq(dve.tensor_scalar(out=out_f, in0=out_i, scalar1=1.0, scalar2=None, op0=ALU.max))
            groups_of(ps[6][0:NB, 128:129], gcol[0:NB, 0:1], gcol_i[0:NB, :])
            dve.sem_inc(gb_done, 1)
            groups_of(ps[6][:, 64:64 + NB], gcount[:, :], gint[:, :])
            seq(dve.tensor_tensor_scan(out=prefix[:, :], data0=ones[:, 0:NB], data1=gcount[:, :], initial=0.0,
                                       op0=ALU.mult, op1=ALU.add))
            seq(dve.tensor_tensor(out=prefix[:, :], in0=prefix[:, :], in1=gcount[:, :], op=ALU.subtract))
            seq(dve.tensor_scalar(out=base[:, :], in0=prefix[:, :], scalar1=float(GS), scalar2=-1.0, op0=ALU.mult, op1=ALU.add))
            seq(dve.tensor_tensor(out=base[:, :], in0=base[:, :], in1=ps[6][:, 0:NB], op=ALU.add))

            SHIFT = GT.bit_length() - 1
            RANK_SEQ = 4
            PART_SEQ = 1 + NB // LANES * RANK_SEQ + 7

            def rank(col, n, off):
                mask, lanes, count = [e[:, 0:LANES * n].rearrange("p (l c) -> p l c", l=LANES) for e in (ea, eb, ec)]
                slot, slot_i, low_i = mask[:, 0, :], count[:, 0, :].bitcast(I32), count[:, 1, :].bitcast(I32)
                seq.off, seq.k = off, 0
                seq(dve.memset(lanes, 0.0), apart=True)
                with dve.Fori(0, NB // LANES) as i:
                    seq.off, seq.k = off + i * RANK_SEQ, 1
                    for l in range(LANES):
                        last = dve.tensor_scalar(out=mask[:, l, :], in0=hi[:, ds(col, n)],
                                                 scalar1=iota_row[:, ds(i * LANES + l, 1)], scalar2=None, op0=ALU.is_equal)
                    seq(last, apart=True)
                    for l in range(LANES):
                        last = dve.tensor_tensor_scan(out=count[:, l, :], data0=ones[:, 0:1].to_broadcast([P, n]),
                                                      data1=mask[:, l, :], initial=base[:, ds(i * LANES + l, 1)],
                                                      op0=ALU.mult, op1=ALU.add)
                    seq(last, apart=True)
                    seq(dve.copy_predicated(lanes, mask.bitcast(I32), count))
                    seq(dve.tensor_scalar(out=base[:, ds(i * LANES, LANES)], in0=count[:, :, n - 1], scalar1=0.0,
                                          scalar2=None, op0=ALU.add))
                seq.off, seq.k = off + NB // LANES * RANK_SEQ, 1
                seq(dve.tensor_reduce(out=slot, in_=lanes.rearrange("p l c -> p c l"), axis=mybir.AxisListType.X, op=ALU.add))
                seq(dve.tensor_copy(out=slot_i, in_=slot))
                seq(dve.tensor_scalar(out=low_i, in0=slot_i, scalar1=SHIFT, scalar2=P - 1, op0=ALU.logical_shift_right,
                                      op1=ALU.bitwise_and))
                seq(dve.tensor_scalar(out=slot, in0=low_i, scalar1=float(NT), scalar2=None, op0=ALU.mult))
                seq(dve.tensor_scalar(out=low_i, in0=slot_i, scalar1=GS.bit_length() - 1, scalar2=None,
                                      op0=ALU.logical_shift_right))
                seq(dve.scalar_tensor_tensor(out=slot, in0=low_i, scalar=float(GT), in1=slot, op0=ALU.mult, op1=ALU.add))
                seq(dve.tensor_scalar(out=low_i, in0=slot_i, scalar1=GT - 1, scalar2=None, op0=ALU.bitwise_and))
                dve.tensor_tensor(out=pos_i[:, ds(col, n)], in0=low_i, in1=slot, op=ALU.add).then_inc(pos_done, 1)

            dve.wait_ge(consts, 2)
            col = 0
            for steps in FIRST_STEPS:
                seq.turn(0, 0)
                rank(col, steps * 2 * SH, 0)
                seq.after(1, PART_SEQ)
                col += steps * 2 * SH
            seq.turn(0, 0)
            with dve.Fori(1, PARTS) as part:
                rank(part * PC, PC, (part - 1) * PART_SEQ)
            seq.after(PARTS - 1, PART_SEQ)
            dve.wait_ge(pos_done, PARTS - 1 + len(FIRST_STEPS))
            dve.tensor_copy(out=pos_i[:, EC:ECP], in_=pads[:, :]).then_inc(pos_done, 1)

            dve.wait_ge(sg_ready, 1)
            seq(dve.tensor_copy(out=gcol[0:NB, 1:2], in_=ps[5][0:NB, 0:1]))
            seq(dve.tensor_tensor(out=gcol[0:NB, 2:3], in0=gcol[0:NB, 1:2], in1=gcol[0:NB, 0:1], op=ALU.add))
            seq(dve.tensor_scalar(out=gcol[0:NB, 3:4], in0=gcol[0:NB, 2:3], scalar1=-1.0, scalar2=None, op0=ALU.add))
            for k, (col, op) in enumerate(((2, ALU.is_ge), (1, ALU.is_equal), (3, ALU.is_equal))):
                seq(dve.tensor_scalar(out=gflags[0:NB, k, :], in0=iota_g[0:NB, :], scalar1=gcol[0:NB, col:col + 1],
                                      scalar2=None, op0=op))
            dve.sem_inc(flags_done, 1)

            dve.wait_ge(flags_summed, 1)
            for half in range(2):
                cols = slice(half * (NG // 2), (half + 1) * (NG // 2))
                bucket, is_first, is_last = [ps[2 * k + half][:, 0:NG // 2] for k in (0, 1, 2)]
                dve.tensor_scalar(out=keep[:, cols], in0=is_first, scalar1=-1.0, scalar2=1.0, op0=ALU.mult, op1=ALU.add)
                seq(dve.tensor_scalar(out=dest_f[:, cols], in0=bucket, scalar1=-float(NB), scalar2=None, op0=ALU.add))
                seq(dve.tensor_tensor(out=dest_f[:, cols], in0=dest_f[:, cols], in1=is_last, op=ALU.mult))
            dve.tensor_scalar(out=dest_i[:, :], in0=dest_f[:, :], scalar1=float(NB), scalar2=None, op0=ALU.add).then_inc(dest_done, 1)

            dve.wait_ge(x_in, 32)
            seq.turn(0, 0)
            with dve.Fori(0, NB // STATB) as t:
                seq.off, seq.k = t * 3, 0
                for j in range(STATB):
                    last = dve.bn_stats(out=stats[:, j, :], in_=R[:, ds(t * STATB + j, 1), :].rearrange("p a d -> p (a d)"))
                seq(last, apart=True)
                for j in range(STATB):
                    last = dve.bn_aggr(out=smv[:, j, :], in_=stats[:, j, :])
                seq(last)
                seq(dve.tensor_copy(out=mv[:, ds(t * STATB, STATB), :], in_=smv[:, :, :]))
            seq.after(NB // STATB, 3)
            dve.sem_inc(var_done, 1)
            dve.wait_ge(std_done, 1)
            seq(dve.reciprocal(out=rstd[:, :], in_=rstd[:, :]))

            def normalise(g, nb, to, source, dynamic):
                for j in range(nb):
                    n = g * GB + j
                    s = source[:, ds(n, 1), :].rearrange("p a d -> p (a d)") if dynamic else source[:, j, :]
                    last = dve.tensor_scalar(out=to[:, j, :], in0=s, scalar1=mv[:, ds(n, 1), 0:1].rearrange("p a d -> p (a d)"),
                                             scalar2=rstd[:, ds(n, 1)], op0=ALU.subtract, op1=ALU.mult)
                return last

            dve.wait_ge(mixw_in, 16 * MIXW_DMAS)

            def pass1(g, nb):
                normalise(g, nb, xn, R, True).then_inc(xn_done, 1)
                for j in range(nb):
                    n = g * GB + (j + 1)
                    dve.wait_ge(kv_done, n)
                    if j >= 2:
                        dve.wait_ge(acc_done, g * GB + (j - 1))
                    bank = ps[2 + j % 2]
                    seq(dve.tensor_tensor(out=kraw[:, j % 2, :], in0=bank[:, 0:D], in1=bkv_b[:, 0:D], op=ALU.add))
                    dve.tensor_scalar(out=kneg[:, j % 2, :], in0=kraw[:, j % 2, :], scalar1=0.0, scalar2=None,
                                      op0=ALU.min).then_inc(kneg_done, 1)
                    dve.tensor_tensor(out=vaug[:, j % 2, :, 0:P], in0=bank[:, D:2 * D].rearrange("p (c e) -> p c e", c=KC),
                                      in1=bkv_b[:, D:2 * D].rearrange("p (c e) -> p c e", c=KC), op=ALU.add).then_inc(kv_read, 1)
                    dve.wait_ge(kexp_done, n)
                    dve.scalar_tensor_tensor(out=kphi[:, j % 2, :], in0=kraw[:, j % 2, :], scalar=0.0, in1=kneg[:, j % 2, :],
                                             op0=ALU.max, op1=ALU.add).then_inc(kphi_done, 1)

            over_groups(dve, seq, GB, pass1)

            dve.wait_ge(kvacc_done, 1)
            for c in range(KC):
                o = c * (P + 4)
                dve.tensor_tensor(out=kvbd[:, c, :], in0=ps[5][:, o:o + P], in1=blockones[:, :], op=ALU.mult)
                seq(dve.tensor_copy(out=ksum[:, c:c + 1], in_=ps[5][:, o + P:o + P + 1]))
            for c in range(KC):
                last = dve.tensor_scalar(out=ksel[:, c, :], in0=blockones[:, :], scalar1=ksum[:, c:c + 1], scalar2=None, op0=ALU.mult)
            last.then_inc(kvbd_done, 1)

            def wide(row, nb):
                return row_b[:, row:row + 1, :].to_broadcast([P, nb, D])

            def layer_norm(nb, t, affine, to, var_ready, std_ready, g, s=stats, m=gmv, r=grs):
                for j in range(nb):
                    last = dve.bn_stats(out=s[:, j, :], in_=t[:, j, :])
                seq(last, apart=True)
                for j in range(nb):
                    last = dve.bn_aggr(out=m[:, j, :], in_=s[:, j, :])
                last.then_inc(var_ready, 1)
                dve.wait_ge(std_ready, g + 1)
                seq(dve.reciprocal(out=r[:, 0:nb], in_=r[:, 0:nb]))
                for j in range(nb):
                    if affine is None:
                        last = dve.tensor_scalar(out=to(j), in0=t[:, j, :], scalar1=m[:, j, 0:1], scalar2=r[:, j:j + 1],
                                                 op0=ALU.subtract, op1=ALU.mult)
                    else:
                        last = dve.scalar_tensor_tensor(out=t[:, j, :], in0=t[:, j, :], scalar=m[:, j, 0:1], in1=affine[0],
                                                        op0=ALU.subtract, op1=ALU.mult)
                if affine is not None:
                    seq(last)
                    for j in range(nb):
                        last = dve.scalar_tensor_tensor(out=to(j), in0=t[:, j, :], scalar=r[:, j:j + 1], in1=affine[1],
                                                        op0=ALU.mult, op1=ALU.add)
                return last

            def attend(g, nb):
                T = nb * P
                normalise(g, nb, xn, R, True).then_inc(xn2_done, 1)
                dve.wait_ge(xn2_done, g + 1)
                dve.tensor_tensor(out=sup_sb[:, 0:nb, :], in0=xn[:, 0:nb, :], in1=wide(6, nb), op=ALU.add).then_inc(xnb_ready, 1)
                dve.wait_ge(q_done, g + 1)
                for hh in range(KC):
                    dve.tensor_scalar(out=qneg[:, hh, 0:T], in0=ps[2 + hh][:, 0:T], scalar1=bq_col[:, hh:hh + 1], scalar2=0.0,
                                      op0=ALU.add, op1=ALU.min).then_inc(qneg_done, 1)
                    last = dve.tensor_scalar(out=qphi[:, hh, 0:T], in0=ps[2 + hh][:, 0:T], scalar1=bq_col[:, hh:hh + 1], scalar2=0.0,
                                             op0=ALU.add, op1=ALU.max)
                seq(last)
                for hh in range(KC):
                    dve.wait_ge(qexp_done, g * KC + (hh + 1))
                    last = dve.tensor_tensor(out=qphi[:, hh, 0:T], in0=qphi[:, hh, 0:T], in1=qneg[:, hh, 0:T], op=ALU.add)
                last.then_inc(qphi_done, 1)
                dve.wait_ge(att_done, g + 1)
                for hh in range(KC):
                    last = dve.tensor_scalar(out=attnT[:, hh, 0:T], in0=ps[2 + hh][:, 0:T], scalar1=1e-6, scalar2=None, op0=ALU.add)
                seq(last)
                for hh in range(KC):
                    last = dve.reciprocal(out=attnT[:, hh, 0:T], in_=attnT[:, hh, 0:T])
                seq(last)
                for hh in range(KC):
                    last = dve.tensor_tensor(out=attnT[:, hh, 0:T], in0=ps[hh][:, 0:T], in1=attnT[:, hh, 0:T], op=ALU.mult)
                last.then_inc(attn_done, 1)
                seq(dve.tensor_tensor(out=xn[:, 0:nb, :], in0=xn[:, 0:nb, :], in1=wide(0, nb), op=ALU.add))
                dve.wait_ge(wo_done, g + 1)
                for q in range(-(-nb // 2)):
                    w = min(2, nb - 2 * q)
                    last = dve.tensor_tensor(out=tmp[:, 2 * q:2 * q + w, :], in0=xn[:, 2 * q:2 * q + w, :],
                                             in1=ps[q][:, 0:w * D].rearrange("p (t d) -> p t d", d=D), op=ALU.add)
                seq(last)
                layer_norm(nb, tmp, (row_b[:, 2, :], row_b[:, 3, :]), lambda j: h1[:, j, :], var1_done, std1_done, g).then_inc(h1_done, 1)
                dve.wait_ge(h1_done, g + 1)

            def finish(g, nb):
                dve.wait_ge(ff2_done, g + 1)
                for q in range(-(-nb // 2)):
                    w = min(2, nb - 2 * q)
                    last = dve.tensor_tensor(out=tmp[:, 2 * q:2 * q + w, :], in0=h1b[:, 2 * q:2 * q + w, :],
                                             in1=ps[6 + q][:, 0:w * D].rearrange("p (t d) -> p t d", d=D), op=ALU.add)
                seq(last)
                seq(layer_norm(nb, tmp, (row_b[:, 4, :], row_b[:, 5, :]), lambda j: tmp[:, j, :], var2_done, std2_done, g))
                dve.tensor_tensor(out=mixed[:, 0:nb, :], in0=tmp[:, 0:nb, :], in1=R[:, ds(g * GB, nb), :], op=ALU.add).then_inc(mix_done, 1)

            def pass2(a, na, b, nb):
                if na:
                    attend(a, na)
                if nb:
                    finish(b, nb)
                if na:
                    seq(dve.tensor_tensor(out=h1b[:, 0:na, :], in0=h1[:, 0:na, :], in1=wide(1, na), op=ALU.add))

            PASS2_SEQ = 14
            dve.wait_ge(sup_stored, 16 * (FULL + 1))
            over_stages(dve, seq, PASS2_SEQ, pass2)

            dve.wait_ge(mix_done, FULL + 1)
            dve.wait_ge(resid_stored, 16 * (FULL + 1))
            seq(dve.memset(carry[:, CARRY - 1, :], 0.0))

            def select(it, h, wait_free):
                dve.wait_ge(tab_in[h], it * 16 + 16)
                if wait_free:
                    dve.wait_ge(summed[h], it * HALF_G)
                for k in range(HT):
                    last = dve.tensor_scalar(out=hot[h][:, k, :], in0=iota_row[:, :], scalar1=st_tab[h][:, k, 1:2],
                                             scalar2=st_tab[h][:, k, 2:3], op0=ALU.is_equal, op1=ALU.mult)
                last.then_inc(hot_done[h], 1)

            def carry_on(it, h, wait_kept):
                for q in range(HALF_G):
                    c = h * HALF_G + q
                    dve.wait_ge(summed[h], it * HALF_G + (q + 1))
                    if wait_kept:
                        dve.wait_ge(sum_kept, it * CARRY + (c + 1 - CARRY + KEPT_CREDIT))
                    dve.scalar_tensor_tensor(out=carry[:, c, :], in0=carry[:, (c - 1) % CARRY, :],
                                             scalar=keep[:, ds(it * CARRY + c, 1)], in1=ps[c][:, 0:D],
                                             op0=ALU.mult, op1=ALU.add).then_inc(carried, 1)
                    dve.wait_ge(carried, it * CARRY + (c + 1))

            def step(it, kept_before, kept):
                select(it, 0, True)
                carry_on(it - 1, 1, kept_before)
                select(it, 1, True)
                carry_on(it, 0, kept)

            select(0, 0, False)
            select(0, 1, False)
            carry_on(0, 0, False)
            step(1, False, True)

            def low_weights(to, k, before, source):
                for n in range(2):
                    dve.wait_ge(whi_done, before + (n + 1))
                    dve.tensor_tensor(out=to[:, :, 1, n, :].rearrange("p e n -> p (e n)"), in0=source[:, 2 * k + n, :],
                                      in1=to[:, :, 0, n, :].rearrange("p e n -> p (e n)").bitcast(F32),
                                      op=ALU.subtract).then_inc(wlo_done, 1)

            with dve.Fori(0, EARLY_E // 2) as pair:
                for k in range(2):
                    step(pair * 2 + (k + 2), True, True)
                    low_weights(w_first[:, ds(pair * 2 + k, 1)], k, pair * 4 + 2 * k, work)
            with dve.Fori(EARLY_E + 2, GATHER_STEPS) as it:
                step(it, True, True)
            carry_on(GATHER_STEPS - 1, 1, True)

            dve.sem_inc(lo_done, LO_CREDIT)
            dve.sem_inc(gelu_done, GELU_CREDIT)
            dve.sem_inc(down_done, DOWN_CREDIT)
            dve.sem_inc(down_read, READ_CREDIT)
            dve.wait_ge(whi_done, 2 * EARLY_E + 1)
            dve.tensor_tensor(out=router_w[1][:, :, :], in0=router_f[:, :, :], in1=router_w[0][:, :, :].bitcast(F32),
                              op=ALU.subtract).then_inc(wlo_done, 1)
            def prepare(slot, n, k, nb, pair):
                T = nb * P
                if slot == 0:
                    dve.wait_ge(group_in[k], pair * 48 + 48)
                    seq(dve.tensor_tensor(out=xb[:, 0:nb, :], in0=ag[:, 0:nb, :], in1=xb[:, 0:nb, :], op=ALU.add))
                    seq(dve.scalar_tensor_tensor(out=y[k][:, 0:nb, :], in0=xb[:, 0:nb, :], scalar=0.0, in1=y[k][:, 0:nb, :],
                                                 op0=ALU.max, op1=ALU.add))
                    for j in range(nb):
                        last = dve.bn_stats(out=lstats[:, j, :], in_=y[k][:, j, :])
                    seq(last, apart=True)
                    for j in range(nb):
                        last = dve.bn_aggr(out=lmv[:, j, :], in_=lstats[:, j, :])
                    seq(last)
                    dve.tensor_scalar(out=lrs[:, 0:nb], in0=lmv[:, 0:nb, 1], scalar1=1.0 + EPS, scalar2=EPS * EPS,
                                      op0=ALU.mult, op1=ALU.add).then_inc(var_t, 1)
                if slot == 1:
                    dve.wait_ge(std_t, n + 1)
                    seq(dve.reciprocal(out=lrs[:, 0:nb], in_=lrs[:, 0:nb]))
                    for j in range(nb):
                        last = dve.scalar_tensor_tensor(out=ag[:, j, :], in0=y[k][:, j, :], scalar=lmv[:, j, 0:1],
                                                        in1=lrow_b[:, 0, :], op0=ALU.subtract, op1=ALU.mult)
                    seq(last)
                    for j in range(nb):
                        last = dve.scalar_tensor_tensor(out=ag[:, j, :], in0=ag[:, j, :], scalar=lrs[:, j:j + 1],
                                                        in1=lrow_b[:, 1, :], op0=ALU.mult, op1=ALU.add)
                    last.then_inc(z_done, 1)
                if slot in (2, 3):
                    c = slot - 2
                    dve.wait_ge(zhi_done, n * KC + (c + 1))
                    dve.tensor_tensor(out=z_s[1][:, k, c, 0:T], in0=ps[3][:, 0:T], in1=z_s[0][:, k, c, 0:T].bitcast(F32),
                                      op=ALU.subtract).then_inc(zlo_done, 1)
                if slot == 4:
                    dve.wait_ge(logit_done, n + 1)
                    seq(dve.tensor_tensor(out=logit[:, 0:nb, :], in0=ps[3][:, 0:nb * E].rearrange("p (t e) -> p t e", e=E),
                                          in1=br_b[:, None, :].to_broadcast([P, nb, E]), op=ALU.add), apart=True)
                    for j in range(nb):
                        last = dve.max(out=top[:, j, :], in_=logit[:, j, :])
                    seq(last, apart=True)
                    for j in range(nb):
                        last = dve.max_index(out=topi[:, j, :], in_max=top[:, j, :], in_values=logit[:, j, :])
                    seq(last)
                    dve.tensor_tensor(out=gw[:, 0:nb, 0], in0=top[:, 0:nb, 1], in1=top[:, 0:nb, 0], op=ALU.subtract).then_inc(gap_done, 1)
                if slot == 5:
                    seq(dve.tensor_copy(out=topf[:, 0:nb, :], in_=topi[:, 0:nb, 0:2]))
                    dve.wait_ge(exp_done, n + 1)
                    seq(dve.tensor_scalar(out=gw[:, 0:nb, 2], in0=gw[:, 0:nb, 1], scalar1=1.0, scalar2=None, op0=ALU.add))
                    seq(dve.reciprocal(out=gw[:, 0:nb, 2], in_=gw[:, 0:nb, 2]))
                    seq(dve.tensor_tensor(out=gw[:, 0:nb, 3], in0=gw[:, 0:nb, 1], in1=gw[:, 0:nb, 2], op=ALU.mult))
                    for m, to in enumerate((wfull[k], wtmp)):
                        seq(dve.tensor_tensor(out=to[:, 0:nb, :], in0=iota_row[:, None, 0:E].to_broadcast([P, nb, E]),
                                              in1=topf[:, 0:nb, m:m + 1].to_broadcast([P, nb, E]), op=ALU.is_equal))
                        seq(dve.tensor_tensor(out=to[:, 0:nb, :], in0=to[:, 0:nb, :],
                                              in1=gw[:, 0:nb, 2 + m:3 + m].to_broadcast([P, nb, E]), op=ALU.mult))
                    dve.tensor_tensor(out=wfull[k][:, 0:nb, :], in0=wfull[k][:, 0:nb, :], in1=wtmp[:, 0:nb, :],
                                      op=ALU.add).then_inc(wfull_done, 1)
                    dve.wait_ge(wfull_done, n + 1)
                if slot in (7, 8):
                    h = slot - 7
                    if nb > 2 * h:
                        w = min(2, nb - 2 * h)
                        dve.wait_ge(bias_done, n * 2 + (h + 1))
                        dve.tensor_tensor(out=y[k][:, 2 * h:2 * h + w, :], in0=y[k][:, 2 * h:2 * h + w, :],
                                          in1=ps[3][:, 0:w * D].rearrange("p (t d) -> p t d", d=D), op=ALU.add).then_inc(bias_read, 1)
                        dve.wait_ge(bias_read, n * 2 + (h + 1))

            def low_parts(g, e, nb):
                for f in range(HC):
                    dve.wait_ge(hi_done, g * (E * HC) + (e * HC + f + 1))
                    dve.tensor_tensor(out=hid_s[1][:, e % 2, f, 0:nb * P], in0=hid[:, f, 0:nb * P],
                                      in1=hid_s[0][:, e % 2, f, 0:nb * P].bitcast(F32), op=ALU.subtract).then_inc(lo_done, 1)

            def add_expert(g, e, k, nb):
                for j in range(nb):
                    n = e * nb + j + 1
                    dve.wait_ge(down_done, g * (E * GB) + (n + DOWN_CREDIT))
                    if e:
                        dve.wait_ge(down_read, g * (E * GB) + (n - nb + READ_CREDIT))
                    dve.scalar_tensor_tensor(out=y[k][:, j, :], in0=ps[4 + j][:, 0:D], scalar=wfull[k][:, j, e:e + 1],
                                             in1=y[k][:, j, :], op0=ALU.mult, op1=ALU.add).then_inc(down_read, 1)

            def group(g, k, nb, nb_next, pair):
                for e in range(E):
                    if e + 1 < E:
                        low_parts(g, e + 1, nb)
                    elif nb_next:
                        low_parts(g + 1, 0, nb_next)
                    add_expert(g, e, k, nb)
                    if e == 0:
                        dve.wait_ge(down_read, g * (E * GB) + (nb + READ_CREDIT))
                        prepare(8, g, k, nb, pair)
                    if nb_next:
                        prepare(e, g + 1, 1 - k, nb_next, pair + k)

            for slot in range(8):
                prepare(slot, 0, 0, GB, 0)
            for e in range(EARLY_E, E):
                low_weights(w_rest[:, e - EARLY_E:e - EARLY_E + 1], e % 2, 2 * e + 1, stage_rest)
            low_parts(0, 0, GB)
            over_pairs(dve, seq, 2 * PREPARE_SEQ, group)


_OUT = ("out", (N, D))
_NAMES = ["x", "src", "dst", "edge_weight", "L0_gnn_weight", "L0_gnn_bias", "L0_mix_Wq", "L0_mix_bq", "L0_mix_Wk",
          "L0_mix_bk", "L0_mix_Wv", "L0_mix_bv", "L0_mix_Wo", "L0_mix_bo", "L0_mix_W1", "L0_mix_b1", "L0_mix_W2",
          "L0_mix_b2", "L0_mix_ln1_g", "L0_mix_ln1_b", "L0_mix_ln2_g", "L0_mix_ln2_b", "L0_ffn_gamma", "L0_ffn_beta",
          "L0_ffn_Wr", "L0_ffn_br", "L0_ffn_W1", "L0_ffn_b1", "L0_ffn_W2", "L0_ffn_b2"]


def kernel(**inputs):
    import numpy as np
    import concourse.bacc as bacc
    from concourse.bass_utils import run_bass_kernel_spmd

    nc = bacc.Bacc("TRN2", target_bir_lowering=False, num_devices=1)
    arrays, args = {}, []
    for name in _NAMES:
        a = np.ascontiguousarray(inputs[name])
        arrays["in_" + name] = a
        args.append(nc.dram_tensor("in_" + name, a.shape, mybir.dt.from_np(a.dtype), kind="ExternalInput").ap())
    out = nc.dram_tensor(_OUT[0], _OUT[1], F32, kind="ExternalOutput").ap()
    program(nc, *args, out)
    result = run_bass_kernel_spmd(nc, [arrays], core_ids=[0])
    return result.results[0][_OUT[0]]
```
